# Optimizing a Trainium2 kernel written in Bass

```python
import numpy as np
import jax
import jax.numpy as jnp

def _softmax(x, axis=-1):
    return jax.nn.softmax(x, axis=axis)

def _gelu(x):
    return jax.nn.gelu(x, approximate=True)

def _silu(x):
    return jax.nn.silu(x)

def _sigmoid(x):
    return jax.nn.sigmoid(x)

def _layernorm(x, axis=-1, eps=1e-05):
    m = jnp.mean(x, axis=axis, keepdims=True)
    v = jnp.var(x, axis=axis, keepdims=True)
    return (x - m) / jnp.sqrt(v + eps)

def _scatter_add(tgt, idx, src, axis=0):
    return tgt.at[idx].add(src)

def _segment_sum(src, seg, n):
    return jax.ops.segment_sum(src, seg, n)
kernel_name = 'mk_perceiver_d2_seqx_r4_8350c2'

def setup_inputs(seed: int=0):
    np.random.seed(seed)
    _w = jnp.asarray

    def _rec_inputs():
        import jax
        import jax.numpy as jnp
        _rk = jax.random.key(seed)
        x = -0.0002928 + 1 * jax.random.normal(jax.random.fold_in(_rk, 1), (32, 32, 256), jnp.float32)
        _lenS = 32 - jax.random.randint(jax.random.fold_in(_rk, 7), (32,), 0, max(1, 32 // 4) + 1, jnp.int32)
        _lenS2 = 257 - jax.random.randint(jax.random.fold_in(_rk, 8), (32,), 0, max(1, 257 // 4) + 1, jnp.int32)
        _ctx_1024P = jax.random.normal(jax.random.fold_in(_rk, 11), (32, 16, 256), jnp.float32)
        _ctx_1024c = jax.random.dirichlet(jax.random.fold_in(_rk, 511), 0.3 * jnp.ones((16,), jnp.float32), (32, 257))
        _ctx_1024t = jnp.einsum('bsk,bkd->bsd', _ctx_1024c, _ctx_1024P)
        _ctx_1024t = _ctx_1024t * jax.lax.rsqrt(jnp.mean(jnp.square(_ctx_1024t)) + 1e-12) * 0.953939
        ctx_1024 = 4.13588e-05 + 0.999923 * (_ctx_1024t + 0.3 * jax.random.normal(jax.random.fold_in(_rk, 611), (32, 257, 256), jnp.float32))
        itok_BxS_8_8191 = jax.random.randint(jax.random.fold_in(_rk, 12), (32, 32), 8, 2048, jnp.int32)
        itok_BxS2_1_8191 = jax.random.randint(jax.random.fold_in(_rk, 13), (32, 257), 1, 2048, jnp.int32)
        _validS = jnp.arange(32)[None, :] < _lenS[:, None]
        _validS2 = jnp.arange(257)[None, :] < _lenS2[:, None]
        _causal = jnp.tril(jnp.ones((32, 32), dtype=bool))
        mask_BxSxS2_if1 = jnp.where(jnp.ones((32, 32, 257), dtype=bool), 1, 0).astype(jnp.int32)
        return (x, ctx_1024, itok_BxS_8_8191, itok_BxS2_1_8191, mask_BxSxS2_if1)
    x, ctx_1024, itok_BxS_8_8191, itok_BxS2_1_8191, mask_BxSxS2_if1 = _rec_inputs()

    def _L0_xattn_setup():
        import jax, jax.numpy as jnp
        import numpy as np
        DIM = 256
        NUM_HEADS = 16
        HEAD_DIM = DIM // NUM_HEADS

        def _slopes(num_heads):
            ratio = 2.0 ** (-8.0 / num_heads)
            return jnp.asarray([ratio ** i for i in range(1, num_heads + 1)], dtype=jnp.float32)
        key = jax.random.key(seed)
        ks = jax.random.split(key, 10)
        b, q_len, k_len = (2, 512, 1024)
        query = jax.random.normal(ks[0], (b, q_len, DIM), dtype=jnp.float32)
        keys = jax.random.normal(ks[1], (b, k_len, DIM), dtype=jnp.float32)
        values = jax.random.normal(ks[2], (b, k_len, DIM), dtype=jnp.float32)
        query_pos = jnp.sort(jax.random.randint(ks[3], (b, q_len), 0, 2048), axis=-1)
        key_pos = jnp.sort(jax.random.randint(ks[4], (b, k_len), 0, 2048), axis=-1)
        mask = jnp.ones((b, q_len, k_len), dtype=jnp.int32)
        lim = float(np.sqrt(6.0 / (DIM + DIM)))
        W_q = jax.random.uniform(ks[5], (DIM, DIM), minval=-lim, maxval=lim, dtype=jnp.float32)
        W_k = jax.random.uniform(ks[6], (DIM, DIM), minval=-lim, maxval=lim, dtype=jnp.float32)
        W_v = jax.random.uniform(ks[7], (DIM, DIM), minval=-lim, maxval=lim, dtype=jnp.float32)
        W_o = jax.random.uniform(ks[8], (DIM, DIM), minval=-lim, maxval=lim, dtype=jnp.float32)
        return {'query': query, 'keys': keys, 'values': values, 'W_q': W_q, 'W_k': W_k, 'W_v': W_v, 'W_o': W_o, 'query_pos': query_pos, 'key_pos': key_pos, 'mask': mask}
    _L0_xattn_all = _L0_xattn_setup()
    _L0_xattn_in = {k: v for k, v in _L0_xattn_all.items() if k in ('W_q', 'W_k', 'W_v', 'W_o')}
    del _L0_xattn_all

    def _L0_attn_setup():
        import jax, jax.numpy as jnp
        import numpy as np
        EMBED_DIM = 256
        NUM_HEADS = 16
        HEAD_DIM = EMBED_DIM // NUM_HEADS
        EPSILON = 1e-06
        SCORE_SCALE = 1.0
        B, L = (2, 512)
        key = jax.random.key(seed)
        k0, k1, k2, k3, k4 = jax.random.split(key, 5)
        s_in = 1.0 / np.sqrt(EMBED_DIM)
        return {'x': jax.random.normal(k0, (B, L, EMBED_DIM), dtype=jnp.float32), 'w_qkv': jax.random.normal(k1, (EMBED_DIM, 3 * EMBED_DIM), dtype=jnp.float32) * s_in, 'b_qkv': jnp.zeros((3 * EMBED_DIM,), dtype=jnp.float32), 'w_out': jax.random.normal(k2, (EMBED_DIM, EMBED_DIM), dtype=jnp.float32) * s_in, 'b_out': jnp.zeros((EMBED_DIM,), dtype=jnp.float32)}
    _L0_attn_all = _L0_attn_setup()
    _L0_attn_in = {k: v for k, v in _L0_attn_all.items() if k in ('w_qkv', 'b_qkv', 'w_out', 'b_out')}
    del _L0_attn_all

    def _L0_ffn_setup():
        import jax, jax.numpy as jnp
        import numpy as np
        BLOCK = 32
        W_BITS = 4
        ACT_BITS = 16

        def act_qdq(x):
            qmax = 2.0 ** (ACT_BITS - 1) - 1.0
            scale = jnp.maximum(jnp.max(jnp.abs(x)) / qmax, 1e-12)
            return jnp.clip(jnp.round(x / scale), -qmax - 1.0, qmax) * scale

        def fixed_qdq_u16(x):
            scale = 1.0 / 65536.0
            return jnp.clip(jnp.round(x / scale), 0.0, 65535.0) * scale

        def lpbq_dequant(w):
            O, I = w.shape
            qmax = 2.0 ** (W_BITS - 1) - 1.0
            wb = w.reshape(O, I // BLOCK, BLOCK)
            s = jnp.maximum(jnp.max(jnp.abs(wb), axis=-1, keepdims=True) / qmax, 1e-12)
            wq = jnp.clip(jnp.round(wb / s), -qmax - 1.0, qmax) * s
            return wq.reshape(O, I)
        key = jax.random.key(seed)
        k1, k2, k3, k4 = jax.random.split(key, 4)
        B, S, H, I = (2, 1024, 256, 768)
        x = jax.random.normal(k1, (B, S, H), jnp.float32)
        w_gate = jax.random.normal(k2, (I, H), jnp.float32) * 0.02
        w_up = jax.random.normal(k3, (I, H), jnp.float32) * 0.02
        w_down = jax.random.normal(k4, (H, I), jnp.float32) * 0.02
        return {'x': x, 'w_gate': w_gate, 'w_up': w_up, 'w_down': w_down}
    _L0_ffn_all = _L0_ffn_setup()
    _L0_ffn_in = {k: v for k, v in _L0_ffn_all.items() if k in ('w_gate', 'w_up', 'w_down')}
    del _L0_ffn_all

    def _L1_xattn_setup():
        import jax, jax.numpy as jnp
        import numpy as np
        DIM = 256
        key = jax.random.key(seed)
        ks = jax.random.split(key, 9)
        B, S, D = (8, 512, DIM)
        inv = 1.0 / np.sqrt(D)
        return {'image_emb': jax.random.normal(ks[0], (B, S, D), dtype=jnp.float32), 'text_emb': jax.random.normal(ks[1], (B, S, D), dtype=jnp.float32), 'edge_index': jax.random.randint(ks[2], (2, 16), 0, 512, dtype=jnp.int64), 'Wq': jax.random.normal(ks[3], (D, D), dtype=jnp.float32) * inv, 'bq': jnp.zeros((D,), dtype=jnp.float32), 'Wk': jax.random.normal(ks[4], (D, D), dtype=jnp.float32) * inv, 'bk': jnp.zeros((D,), dtype=jnp.float32), 'Wv': jax.random.normal(ks[5], (D, D), dtype=jnp.float32) * inv, 'bv': jnp.zeros((D,), dtype=jnp.float32)}
    _L1_xattn_all = _L1_xattn_setup()
    _L1_xattn_in = {k: v for k, v in _L1_xattn_all.items() if k in ('edge_index', 'Wq', 'bq', 'Wk', 'bk', 'Wv', 'bv')}
    del _L1_xattn_all

    def _L1_attn_setup():
        import jax, jax.numpy as jnp
        import numpy as np
        B, S, D, H, NSEG = (2, 512, 256, 16, 8)

        def _mha(x, w_in, b_in, w_out, b_out, n_heads, mask=None):
            b, s, d = x.shape
            dh = d // n_heads
            qkv = x @ w_in.T + b_in
            q, k, v = jnp.split(qkv, 3, axis=-1)

            def to_heads(t):
                return t.reshape(b, s, n_heads, dh).transpose(0, 2, 1, 3)
            q, k, v = (to_heads(q), to_heads(k), to_heads(v))
            scores = jnp.einsum('bhqd,bhkd->bhqk', q, k) / jnp.sqrt(jnp.asarray(dh, x.dtype))
            if mask is not None:
                scores = jnp.where(mask[:, None, :, :], scores, jnp.asarray(-1000000000.0, x.dtype))
            attn = jax.nn.softmax(scores, axis=-1)
            out = jnp.einsum('bhqk,bhkd->bhqd', attn, v)
            out = out.transpose(0, 2, 1, 3).reshape(b, s, d)
            return out @ w_out.T + b_out
        key = jax.random.key(seed)
        ks = jax.random.split(key, 13)
        sc = 0.02
        return {'x': jax.random.normal(ks[0], (B, S, D), jnp.float32), 'lt_w_in': jax.random.normal(ks[1], (3 * D, D), jnp.float32) * sc, 'lt_b_in': jnp.zeros((3 * D,), jnp.float32), 'lt_w_out': jax.random.normal(ks[2], (D, D), jnp.float32) * sc, 'lt_b_out': jnp.zeros((D,), jnp.float32), 'st_w_in': jax.random.normal(ks[3], (3 * D, D), jnp.float32) * sc, 'st_b_in': jnp.zeros((3 * D,), jnp.float32), 'st_w_out': jax.random.normal(ks[4], (D, D), jnp.float32) * sc, 'st_b_out': jnp.zeros((D,), jnp.float32), 'protos': jax.random.normal(ks[5], (NSEG, D), jnp.float32), 'fus_w': jax.random.normal(ks[6], (D, 2 * D), jnp.float32) * sc, 'fus_b': jnp.zeros((D,), jnp.float32)}
    _L1_attn_all = _L1_attn_setup()
    _L1_attn_in = {k: v for k, v in _L1_attn_all.items() if k in ('lt_w_in', 'lt_b_in', 'lt_w_out', 'lt_b_out', 'st_w_in', 'st_b_in', 'st_w_out', 'st_b_out', 'protos', 'fus_w', 'fus_b')}
    del _L1_attn_all

    def _L1_ffn_setup():
        import jax, jax.numpy as jnp
        import numpy as np
        S, B, H = (512, 1, 256)
        E, K, F = (8, 2, 352)
        key = jax.random.key(seed)
        k1, k2, k3, k4 = jax.random.split(key, 4)
        return {'hidden_states': jax.random.normal(k1, (S, B, H), jnp.float32), 'router_weight': jax.random.normal(k2, (H, E), jnp.float32) * 0.02, 'w1': jax.random.normal(k3, (E, H, 2 * F), jnp.float32) * 0.02, 'w2': jax.random.normal(k4, (E, F, H), jnp.float32) * 0.02}
    _L1_ffn_all = _L1_ffn_setup()
    _L1_ffn_in = {k: v for k, v in _L1_ffn_all.items() if k in ('router_weight', 'w1', 'w2')}
    del _L1_ffn_all
    return {'x': x, 'ctx_1024': ctx_1024, 'itok_BxS_8_8191': itok_BxS_8_8191, 'itok_BxS2_1_8191': itok_BxS2_1_8191, 'mask_BxSxS2_if1': mask_BxSxS2_if1, 'L0_xattn_W_q': _L0_xattn_in['W_q'], 'L0_xattn_W_k': _L0_xattn_in['W_k'], 'L0_xattn_W_v': _L0_xattn_in['W_v'], 'L0_xattn_W_o': _L0_xattn_in['W_o'], 'L0_attn_w_qkv': _L0_attn_in['w_qkv'], 'L0_attn_b_qkv': _L0_attn_in['b_qkv'], 'L0_attn_w_out': _L0_attn_in['w_out'], 'L0_attn_b_out': _L0_attn_in['b_out'], 'L0_ffn_w_gate': _L0_ffn_in['w_gate'], 'L0_ffn_w_up': _L0_ffn_in['w_up'], 'L0_ffn_w_down': _L0_ffn_in['w_down'], 'L1_xattn_edge_index': _L1_xattn_in['edge_index'], 'L1_xattn_Wq': _L1_xattn_in['Wq'], 'L1_xattn_bq': _L1_xattn_in['bq'], 'L1_xattn_Wk': _L1_xattn_in['Wk'], 'L1_xattn_bk': _L1_xattn_in['bk'], 'L1_xattn_Wv': _L1_xattn_in['Wv'], 'L1_xattn_bv': _L1_xattn_in['bv'], 'L1_attn_lt_w_in': _L1_attn_in['lt_w_in'], 'L1_attn_lt_b_in': _L1_attn_in['lt_b_in'], 'L1_attn_lt_w_out': _L1_attn_in['lt_w_out'], 'L1_attn_lt_b_out': _L1_attn_in['lt_b_out'], 'L1_attn_st_w_in': _L1_attn_in['st_w_in'], 'L1_attn_st_b_in': _L1_attn_in['st_b_in'], 'L1_attn_st_w_out': _L1_attn_in['st_w_out'], 'L1_attn_st_b_out': _L1_attn_in['st_b_out'], 'L1_attn_protos': _L1_attn_in['protos'], 'L1_attn_fus_w': _L1_attn_in['fus_w'], 'L1_attn_fus_b': _L1_attn_in['fus_b'], 'L1_ffn_router_weight': _L1_ffn_in['router_weight'], 'L1_ffn_w1': _L1_ffn_in['w1'], 'L1_ffn_w2': _L1_ffn_in['w2']}

def reference(x, ctx_1024, itok_BxS_8_8191, itok_BxS2_1_8191, mask_BxSxS2_if1, L0_xattn_W_q, L0_xattn_W_k, L0_xattn_W_v, L0_xattn_W_o, L0_attn_w_qkv, L0_attn_b_qkv, L0_attn_w_out, L0_attn_b_out, L0_ffn_w_gate, L0_ffn_w_up, L0_ffn_w_down, L1_xattn_edge_index, L1_xattn_Wq, L1_xattn_bq, L1_xattn_Wk, L1_xattn_bk, L1_xattn_Wv, L1_xattn_bv, L1_attn_lt_w_in, L1_attn_lt_b_in, L1_attn_lt_w_out, L1_attn_lt_b_out, L1_attn_st_w_in, L1_attn_st_b_in, L1_attn_st_w_out, L1_attn_st_b_out, L1_attn_protos, L1_attn_fus_w, L1_attn_fus_b, L1_ffn_router_weight, L1_ffn_w1, L1_ffn_w2):
    import jax
    import jax.numpy as jnp

    def _L0_xattn_ref(query, keys, values, W_q, W_k, W_v, W_o, query_pos, key_pos, mask):
        import jax, jax.numpy as jnp
        import numpy as np
        DIM = 256
        NUM_HEADS = 16
        HEAD_DIM = DIM // NUM_HEADS

        def _slopes(num_heads):
            ratio = 2.0 ** (-8.0 / num_heads)
            return jnp.asarray([ratio ** i for i in range(1, num_heads + 1)], dtype=jnp.float32)
        b, q_len, _ = query.shape
        k_len = keys.shape[1]
        scale = 1.0 / np.sqrt(HEAD_DIM)
        Q = (query @ W_q.T).reshape(b, q_len, NUM_HEADS, HEAD_DIM).transpose(0, 2, 1, 3)
        K = (keys @ W_k.T).reshape(b, k_len, NUM_HEADS, HEAD_DIM).transpose(0, 2, 1, 3)
        V = (values @ W_v.T).reshape(b, k_len, NUM_HEADS, HEAD_DIM).transpose(0, 2, 1, 3)
        scores = jnp.einsum('bhqd,bhkd->bhqk', Q, K) * scale
        dist = (query_pos[:, :, None] - key_pos[:, None, :]).astype(scores.dtype)
        bias = -_slopes(NUM_HEADS)[None, :, None, None] * dist[:, None, :, :]
        scores = scores + bias
        scores = jnp.where(mask[:, None, :, :] == 0, -jnp.inf, scores)
        m = jnp.max(scores, axis=-1, keepdims=True)
        e = jnp.exp(scores - m)
        attn = e / (1.0 + jnp.sum(e, axis=-1, keepdims=True))
        out = jnp.einsum('bhqk,bhkd->bhqd', attn, V)
        out = out.transpose(0, 2, 1, 3).reshape(b, q_len, DIM)
        return out @ W_o.T

    def _L0_attn_ref(x, w_qkv, b_qkv, w_out, b_out):
        import jax, jax.numpy as jnp
        import numpy as np
        EMBED_DIM = 256
        NUM_HEADS = 16
        HEAD_DIM = EMBED_DIM // NUM_HEADS
        EPSILON = 1e-06
        SCORE_SCALE = 1.0
        B, L = (2, 512)
        Bq, Lq, E = x.shape
        qkv = x @ w_qkv + b_qkv
        q, k, v = jnp.split(qkv, 3, axis=-1)
        q = q.reshape(Bq, Lq, NUM_HEADS, HEAD_DIM).transpose(0, 2, 1, 3)
        k = k.reshape(Bq, Lq, NUM_HEADS, HEAD_DIM).transpose(0, 2, 1, 3)
        v = v.reshape(Bq, Lq, NUM_HEADS, HEAD_DIM).transpose(0, 2, 1, 3)
        dot = jnp.einsum('bhid,bhjd->bhij', q, k)
        q_norm_sq = jnp.sum(q * q, axis=-1, keepdims=True)
        k_norm_sq = jnp.sum(k * k, axis=-1, keepdims=True)
        vals = q_norm_sq + k_norm_sq.transpose(0, 1, 3, 2)
        scores = dot * dot / (vals - 2.0 * dot + EPSILON) * SCORE_SCALE
        mask = jnp.triu(jnp.ones((Lq, Lq), dtype=scores.dtype), k=1) * -1000000000.0
        scores = scores + mask[None, None, :, :]
        attn = jax.nn.softmax(scores, axis=-1)
        out = jnp.einsum('bhij,bhjd->bhid', attn, v)
        out = out.transpose(0, 2, 1, 3).reshape(Bq, Lq, E)
        return out @ w_out + b_out

    def _L0_ffn_ref(x, w_gate, w_up, w_down):
        import jax, jax.numpy as jnp
        import numpy as np
        BLOCK = 32
        W_BITS = 4
        ACT_BITS = 16

        def act_qdq(x):
            qmax = 2.0 ** (ACT_BITS - 1) - 1.0
            scale = jnp.maximum(jnp.max(jnp.abs(x)) / qmax, 1e-12)
            return jnp.clip(jnp.round(x / scale), -qmax - 1.0, qmax) * scale

        def fixed_qdq_u16(x):
            scale = 1.0 / 65536.0
            return jnp.clip(jnp.round(x / scale), 0.0, 65535.0) * scale

        def lpbq_dequant(w):
            O, I = w.shape
            qmax = 2.0 ** (W_BITS - 1) - 1.0
            wb = w.reshape(O, I // BLOCK, BLOCK)
            s = jnp.maximum(jnp.max(jnp.abs(wb), axis=-1, keepdims=True) / qmax, 1e-12)
            wq = jnp.clip(jnp.round(wb / s), -qmax - 1.0, qmax) * s
            return wq.reshape(O, I)
        x = act_qdq(x)
        up = act_qdq(x @ lpbq_dequant(w_up).T)
        gate = act_qdq(x @ lpbq_dequant(w_gate).T)
        sig = fixed_qdq_u16(jax.nn.sigmoid(gate))
        gate = act_qdq(gate * sig)
        o = act_qdq(gate * up)
        return o @ lpbq_dequant(w_down).T

    def _L1_xattn_ref(image_emb, text_emb, edge_index, Wq, bq, Wk, bk, Wv, bv):
        import jax, jax.numpy as jnp
        import numpy as np
        DIM = 256
        D = image_emb.shape[-1]
        scale = D ** (-0.5)
        q = jnp.einsum('bsd,ed->bse', image_emb, Wq) + bq
        k = jnp.einsum('bsd,ed->bse', text_emb, Wk) + bk
        v = jnp.einsum('bsd,ed->bse', text_emb, Wv) + bv
        scores = jnp.einsum('bqd,bkd->bqk', q, k) * scale
        probs = jax.nn.softmax(scores, axis=-1)
        attended = jnp.einsum('bqk,bkd->bqd', probs, v)
        return attended

    def _L1_attn_ref(x, lt_w_in, lt_b_in, lt_w_out, lt_b_out, st_w_in, st_b_in, st_w_out, st_b_out, protos, fus_w, fus_b):
        import jax, jax.numpy as jnp
        import numpy as np
        B, S, D, H, NSEG = (2, 512, 256, 16, 8)

        def _mha(x, w_in, b_in, w_out, b_out, n_heads, mask=None):
            b, s, d = x.shape
            dh = d // n_heads
            qkv = x @ w_in.T + b_in
            q, k, v = jnp.split(qkv, 3, axis=-1)

            def to_heads(t):
                return t.reshape(b, s, n_heads, dh).transpose(0, 2, 1, 3)
            q, k, v = (to_heads(q), to_heads(k), to_heads(v))
            scores = jnp.einsum('bhqd,bhkd->bhqk', q, k) / jnp.sqrt(jnp.asarray(dh, x.dtype))
            if mask is not None:
                scores = jnp.where(mask[:, None, :, :], scores, jnp.asarray(-1000000000.0, x.dtype))
            attn = jax.nn.softmax(scores, axis=-1)
            out = jnp.einsum('bhqk,bhkd->bhqd', attn, v)
            out = out.transpose(0, 2, 1, 3).reshape(b, s, d)
            return out @ w_out.T + b_out
        long_out = _mha(x, lt_w_in, lt_b_in, lt_w_out, lt_b_out, H)
        seg = jnp.argmax(x @ protos.T, axis=-1)
        same = seg[:, :, None] == seg[:, None, :]
        short_out = _mha(x, st_w_in, st_b_in, st_w_out, st_b_out, H, mask=same)
        cnt = jnp.sum(jax.nn.one_hot(seg, NSEG, dtype=jnp.int32), axis=1)
        tok_cnt = jnp.take_along_axis(cnt, seg, axis=1)
        short_out = jnp.where((tok_cnt == 1)[..., None], x, short_out)
        combined = jnp.concatenate([long_out, short_out], axis=-1)
        return combined @ fus_w.T + fus_b

    def _L1_ffn_ref(hidden_states, router_weight, w1, w2):
        import jax, jax.numpy as jnp
        import numpy as np
        S, B, H = (512, 1, 256)
        E, K, F = (8, 2, 352)
        s, b, h = hidden_states.shape
        x = hidden_states.reshape(-1, h)
        logits = x @ router_weight
        probs = jax.nn.softmax(logits, axis=-1)
        _, topk_idx = jax.lax.top_k(probs, K)
        routing_map = jax.nn.one_hot(topk_idx, E, dtype=probs.dtype).sum(axis=1)
        local_probs = probs * routing_map
        y = jnp.einsum('th,ehf->tef', x, w1)
        y1, y2 = jnp.split(y, 2, axis=-1)
        g = jax.nn.silu(y1) * y2
        o = jnp.einsum('tef,efh->teh', g, w2)
        out = jnp.einsum('teh,te->th', o, local_probs)
        return out.reshape(s, b, h)
    x = x + _L0_xattn_ref(_layernorm(x, axis=-1), ctx_1024, ctx_1024, L0_xattn_W_q, L0_xattn_W_k, L0_xattn_W_v, L0_xattn_W_o, itok_BxS_8_8191, itok_BxS2_1_8191, mask_BxSxS2_if1)
    x = x + _L0_attn_ref(_layernorm(x, axis=-1), L0_attn_w_qkv, L0_attn_b_qkv, L0_attn_w_out, L0_attn_b_out)
    x = x + _L0_ffn_ref(_layernorm(x, axis=-1), L0_ffn_w_gate, L0_ffn_w_up, L0_ffn_w_down)
    x = x + _L1_xattn_ref(_layernorm(x, axis=-1), ctx_1024, L1_xattn_edge_index, L1_xattn_Wq, L1_xattn_bq, L1_xattn_Wk, L1_xattn_bk, L1_xattn_Wv, L1_xattn_bv)
    x = x + _L1_attn_ref(_layernorm(x, axis=-1), L1_attn_lt_w_in, L1_attn_lt_b_in, L1_attn_lt_w_out, L1_attn_lt_b_out, L1_attn_st_w_in, L1_attn_st_b_in, L1_attn_st_w_out, L1_attn_st_b_out, L1_attn_protos, L1_attn_fus_w, L1_attn_fus_b)
    x = x + _L1_ffn_ref(_layernorm(x, axis=-1), L1_ffn_router_weight, L1_ffn_w1, L1_ffn_w2)
    return x

_drawn_inputs = setup_inputs


def setup_inputs(seed=0):
    import zlib

    import numpy as np

    out = dict(_drawn_inputs(seed))
    spreads = {'L0_attn_b_qkv': (0.0, 0.1),
     'L0_attn_b_out': (0.0, 0.1),
     'L1_xattn_bq': (0.0, 0.304),
     'L1_xattn_bk': (0.0, 0.8),
     'L1_xattn_bv': (0.0, 0.1),
     'L1_attn_lt_b_in': (0.0, 0.8),
     'L1_attn_lt_b_out': (0.0, 0.363),
     'L1_attn_st_b_in': (0.0, 0.8),
     'L1_attn_st_b_out': (0.0, 0.387),
     'L1_attn_fus_b': (0.0, 0.1)}
    factors = {'L1_attn_lt_w_in': 3.932,
     'L1_attn_lt_w_out': 3.419,
     'L1_attn_st_w_in': 3.56,
     'L1_attn_st_w_out': 3.333,
     'L1_ffn_router_weight': 8.0,
     'L1_ffn_w1': 8.0,
     'L1_ffn_w2': 8.0}
    for name, (base, spread) in spreads.items():
        noise = np.random.default_rng([zlib.crc32(name.encode()), seed]).standard_normal(out[name].shape)
        drawn = base * np.exp(spread * noise) if base else spread * noise
        out[name] = jnp.asarray(drawn.astype(out[name].dtype))
    for name, factor in factors.items():
        out[name] = (out[name] * factor).astype(out[name].dtype)
    return out
```

```python
from contextlib import ExitStack

import numpy as np
import concourse.bass as bass
from concourse import mybir

F32 = mybir.dt.float32
I32 = mybir.dt.int32
ALU = mybir.AluOpType
ACT = mybir.ActivationFunctionType
AX = mybir.AxisListType
RMAX = bass.bass_isa.ReduceOp.max

NB, SQ, D, SK = 32, 32, 256, 257
NH, DH = 16, 16
P = 128
NT = NB * SQ // P
BT = P // SQ
KT = D // P
NG = NH // 4
FF = 768
FT = FF // P
QB = 32
NE, FE = 8, 352
FCH = [(0, 128), (128, 128), (256, 96)]
ROUND = 1.5 * 2.0 ** 23
BIG = 3e38
LN_EPS = 1e-5

C_ID, C_HEADQ, C_HEAD, C_ROW, C_EQ, C_CAUSAL, C_SLOPE, C_EXP8, C_LAST, C_HALF, C_ONES, C_QUARTER = (
    0, 128, 256, 260, 264, 296, 328, 332, 340, 356, 372, 404)
C_END = 408


def at_least(eng, sem, value):
    if isinstance(value, int) and value <= 0:
        return
    eng.wait_ge(sem, value)


def alone(eng, sem):
    eng.sem_inc(sem, 1)


class Steps:

    def __init__(self, sem):
        self.sem, self.base, self.n = sem, 0, 0

    def enter(self, i, first, per):
        self.start, self.per, self.first = self.base + self.n, per, first
        self.base, self.n = self.start + (i - first) * per, 0

    def leave(self, count):
        assert self.n == self.per, (self.n, self.per)
        self.base, self.n = self.start + count * self.per, 0

    def done(self, ins):
        ins.then_inc(self.sem, 1)
        self.n += 1
        return self.base + self.n

    def now(self):
        return self.base + self.n

    def link(self, eng, ins):
        eng.wait_ge(self.sem, self.done(ins))



class Uses:

    def __init__(self, order):
        self.index, self.first = {}, {}
        for n, (kind, t, b) in enumerate(order):
            self.index[kind, t, b] = n + 1

    def filled(self, kind, t, b):
        if isinstance(t, int):
            return self.index[kind, t, b]
        return self.index[kind, 2, b] + (t - 2) * (self.index[kind, 3, b] - self.index[kind, 2, b])


def build(nc, a, out):
    with ExitStack() as ctx:
        def sb(name, shape, dt=F32, where=ctx):
            return where.enter_context(nc.sbuf_tensor(name, shape, dt))

        def sem(name):
            return ctx.enter_context(nc.semaphore(name))

        bank = [ctx.enter_context(nc.psum_tensor(f"bank{i}", [P, 512], F32)) for i in range(8)]
        cst = sb("cst", [P, C_END])
        x = sb("x", [P, NT, D])
        w = {}
        for name in WEIGHTS:
            w[name] = sb("w_" + name, [P] + list(a[name].shape[1:]))
        w_gate_T, w_up_T = sb("w_gate_T", [P, KT, FF]), sb("w_up_T", [P, KT, FF])
        w_down_T = sb("w_down_T", [P, FT, D])
        c = Consts(cst)
        loaded = {name: sem("loaded_" + name) for name in GROUPS}
        x_loaded, stored = sem("x_loaded"), sem("stored")

        phases = [
            lambda s: prepare_and_cross_attention(nc, a, sb, s, bank, c, cst, x, w, loaded, x_loaded,
                                                  w_gate_T, w_up_T, w_down_T),
            lambda s: ratio_attention(nc, a, sb, s, bank, c, x, w, loaded),
            lambda s: quantised_ffn(nc, a, sb, s, bank, c, x, w_gate_T, w_up_T, w_down_T),
            lambda s: context_attention(nc, a, sb, s, bank, c, x, w, loaded),
            lambda s: segment_attention(nc, a, sb, s, bank, c, x, w, loaded),
            lambda s: experts(nc, a, sb, s, bank, c, x, w, loaded),
        ]
        for phase in phases:
            own = []

            def phase_sem(name):
                own.append(nc.alloc_semaphore(name=name))
                return own[-1]

            phase(phase_sem)
            nc.clear_and_free_semaphores(own)
            nc.all_engine_barrier()
        with nc.Block() as block:
            @block.sync
            def _(sp):
                sp.dma_start(out, x[:]).then_inc(stored, 16)
                sp.wait_ge(stored, 16)


class Consts:

    def __init__(self, cst):
        self.ident = cst[:, C_ID:C_ID + P]
        self.headq = cst[:, C_HEADQ:C_HEADQ + P]
        self.head = cst[:, C_HEAD:C_HEAD + 4]
        self.row = cst[:, C_ROW:C_ROW + 4]
        self.eq = cst[:, C_EQ:C_EQ + SQ]
        self.causal = cst[:, C_CAUSAL:C_CAUSAL + SQ]
        self.slope = cst[:, C_SLOPE:C_SLOPE + NG]
        self.exp8 = cst[:, C_EXP8:C_EXP8 + 8]
        self.last = cst[0:16, C_LAST:C_LAST + 16]
        self.half = cst[:, C_HALF:C_HALF + 16]
        self.quarter = cst[:, C_QUARTER:C_QUARTER + 4]
        self.ones = cst[:, C_ONES:C_ONES + SQ]


GROUPS = {
    "xattn": ("xa_q", "xa_k", "xa_v", "xa_o"),
    "ratio": ("ra_qkv", "ra_o", "ra_bqk", "ra_bv", "ra_bo"),
    "cross": ("cx_q", "cx_k", "cx_v", "cx_bq", "cx_bk", "cx_bv"),
    "segs": ("lt_qkv", "lt_o", "lt_bqk", "lt_bv", "lt_bo", "st_qkv", "st_o", "st_bqk", "st_bv", "st_bo",
             "protos", "fus", "fus_b"),
    "router": ("router",),
}
WEIGHTS = sum(GROUPS.values(), ())


def prepare_and_cross_attention(nc, a, sb_, sem, bank, c, cst, x, w, loaded, x_loaded,
                                w_gate_T, w_up_T, w_down_T):
    with ExitStack() as own:
        def sb(name, shape, dt=F32):
            return sb_(name, shape, dt, own)

        NBLK = 3 * KT * FF // QB
        wn = sb("wn", [P, NBLK, QB])
        wmax, wscale, wrecip = sb("wmax", [P, NBLK]), sb("wscale", [P, NBLK]), sb("wrecip", [P, NBLK])
        last_T = sb("last_T", [P, KT, NB])
        last_rep = sb("last_rep", [P, KT, NB, NG])
        v_last = sb("v_last", [16, NT, D])

        qpos = sb("qpos", [P, NB], I32)
        qposf = sb("qposf", [P, NB])
        ctxT = [sb(f"ctxT{b}", [P, KT, SK]) for b in range(BT)]
        msk = [sb(f"msk{b}", [P, SK], I32) for b in range(BT)]
        kpos = [sb(f"kpos{b}", [P, SK], I32) for b in range(BT)]
        dist = [sb(f"dist{i}", [P, SK]) for i in range(2)]
        shut = sb("shut", [P, SK])
        bias = [sb(f"bias{i}", [P, NG, SK]) for i in range(2)]
        kT = [sb(f"kT{i}", [P, KT, SK]) for i in range(2)]
        v = [sb(f"v{b}", [P, 2, D]) for b in range(BT)]
        s_sb = [sb(f"s_sb{i}", [P, NG, SK]) for i in range(2)]
        prob = [sb(f"prob{i}", [P, NG, SK]) for i in range(2)]
        mx, negm = sb("mx", [P, BT, NG]), sb("negm", [P, BT, NG])
        esum, rden = sb("esum", [P, BT, NG]), sb("rden", [P, BT, NG])
        rmask = sb("rmask", [P, BT, NG, 4])
        pT = [sb(f"pT{i}", [P, NG, 2, P]) for i in range(2)]
        plast, plast_T = sb("plast", [P, BT, NG]), sb("plast_T", [16, P])
        vx = sb("vx", [16, BT, NG, 64])
        om = sb("om", [P, BT, NG, 64])
        oT, xn, xT = sb("oT", [P, KT, P]), sb("xn", [P, D]), sb("xT", [P, KT, P])
        stat, mv, rstd = sb("stat", [P, 6]), sb("mv", [P, 2]), sb("rstd", [P, 1])
        veps = sb("veps", [P, 1])
        qbd = sb("qbd", [P, KT, BT, 4, SQ])
        sc, pt, kv, oo = bank[0:2], bank[2:4], bank[4:6], bank[6:8]

        ctx_loaded = [sem(f"ctx_loaded{b}") for b in range(BT)]
        passed_sp, passed_dve, passed_pool = sem("xa_passed_sp"), sem("xa_passed_dve"), sem("xa_passed_pool")
        cst_loaded, wn_loaded, pos_loaded = sem("cst_loaded"), sem("wn_loaded"), sem("pos_loaded")
        wq_steps = Steps(sem("xa_dve_steps"))
        w_ready, wt_full, wt_done = sem("w_ready"), sem("wt_full"), [sem("wt_done0"), sem("wt_done1")]
        last_ready, vl_full, vl_done = sem("last_ready"), sem("vl_full"), sem("vl_done")
        kv_full = [sem("kv0_full"), sem("kv1_full")]
        kv_done = [sem("kv0_done"), sem("kv1_done")]
        s_full, s_done = sem("s_full"), sem("s_done")
        negm_ready, p_ready = sem("negm_ready"), sem("p_ready")
        pt_full, pt_done = sem("pt_full"), sem("pt_done")
        pv_done, o_full, o_done = sem("pv_done"), sem("o_full"), sem("o_done")
        var_ready, rstd_ready, xn_ready = sem("var_ready"), sem("rstd_ready"), sem("xn_ready")
        rmask_ready, dist_ready, bias_ready = sem("rmask_ready"), sem("dist_ready"), sem("bias_ready")
        plast_ready, vx_ready = sem("plast_ready"), sem("vx_ready")

        use0, use1 = [], [("xT", -1, 2), ("q", -1, 3)]
        for t in range(NT + 1):
            for b in range(BT):
                if t < NT:
                    use0 += [("k", t, b), ("v", t, b)]
                if b == 1 and t > 0:
                    use1 += [("plast", t, b)]
                if t < NT:
                    use1 += [("k", t, b)]
                if b == 2 and t > 0:
                    use1 += [("oT", t, b)]
                if b == 2 and t < NT - 1:
                    use1 += [("xT", t, b)]
                if b == 3 and t < NT - 1:
                    use1 += [("q", t, b)]
                if b == 3 and t > 0:
                    use1 += [("out", t, b)]
        uses = [Uses(use0), Uses(use1)]

        def tiles(eng, step, steps=None, per=None):
            for b in range(BT):
                step(0, b)
            with eng.Fori(1, NT - 1) as t:
                if steps:
                    steps.enter(t, 1, per)
                for b in range(BT):
                    step(t, b)
                if steps:
                    steps.leave(NT - 2)
            for t in (NT - 1, NT):
                for b in range(BT):
                    step(t, b)

        def exists(t):
            return not isinstance(t, int) or 0 <= t < NT

        def before(t, b, lag):
            return t + (b - lag) // BT, (b - lag) % BT

        def turned(copy, n):
            src = bank[n % 2][:].rearrange("p (j o) -> p j o", j=4)
            if n < 6:
                dst = (w_gate_T, w_up_T)[n // 3]
                return copy(dst[:].rearrange("p k (o q) -> p (k o) q", q=P)[:, 4 * (n % 3):4 * (n % 3) + 4, :], src)
            i = n - 6
            return copy(w_down_T[:].rearrange("p f (o q) -> p (f o) q", q=P)[:, 4 * i:4 * i + 4, :], src)

        with nc.Block() as block:
            @block.sync
            def _(sp):
                sp.dma_start(cst[:], a["cst"]).then_inc(cst_loaded, 16)
                sp.dma_start(x[:], a["x"]).then_inc(x_loaded, 16)
                for name in GROUPS["xattn"]:
                    sp.dma_start(w[name][:], a[name]).then_inc(loaded["xattn"], 16)
                sp.dma_start(last_T[:], a["ctx_last_T"]).then_inc(pos_loaded, 16)
                for h in range(4):
                    sp.dma_start(qpos[SQ * h:SQ * h + SQ, :], a["qpos_T"]).then_inc(pos_loaded, 16)

                def context(t, b):
                    tt, bb = t - 1, b
                    if exists(tt) and not (isinstance(t, int) and t == 0):
                        sp.wait_ge(kv_full[0], uses[0].filled("v", tt, bb))
                        alone(sp, passed_sp)
                        sp.wait_ge(dist_ready, 4 * tt + bb + 1)
                        alone(sp, passed_sp)
                    sp.dma_start(ctxT[b][:], a["ctx_T"][BT * t + b]).then_inc(ctx_loaded[b], 16)
                    sp.dma_start(kpos[b][:], a["kpos"][BT * t + b].unsqueeze(0).broadcast_to([P, SK])) \
                        .then_inc(ctx_loaded[b], 16)
                    sp.dma_start(msk[b][:], a["mask"][BT * t + b].unsqueeze(0).broadcast_to([4, SQ, SK])) \
                        .then_inc(ctx_loaded[b], 16)

                for b in range(BT):
                    context(0, b)
                for n, name in enumerate(("w_gate", "w_up", "w_down")):
                    sp.dma_start(wn[:, n * NBLK // 3:(n + 1) * NBLK // 3, :], a[name]).then_inc(wn_loaded, 16)
                for g in ("ratio", "cross", "segs", "router"):
                    for name in GROUPS[g]:
                        sp.dma_start(w[name][:], a[name]).then_inc(loaded[g], 16)
                with sp.Fori(1, NT) as t:
                    for b in range(BT):
                        context(t, b)

            @block.gpsimd
            def _(pool):
                pool.wait_ge(pos_loaded, 80)
                nc.gpsimd.tensor_copy(last_rep[:], last_T[:].unsqueeze(3).broadcast_to([P, KT, NB, NG])) \
                    .then_inc(last_ready, 1)
                nc.gpsimd.tensor_copy(qposf[:], qpos[:]).then_inc(last_ready, 1)

                def root(t):
                    pool.wait_ge(var_ready, t + 1)
                    nc.gpsimd.tensor_tensor(rstd[:], veps[:], c.half[:, 0:1], ALU.pow).then_inc(rstd_ready, 1)

                def biases(t, b):
                    if not exists(t):
                        return
                    pool.wait_ge(dist_ready, 4 * t + b + 1)
                    at_least(pool, s_done, 16 * t + 4 * b + 4 - 8)
                    alone(pool, passed_pool)
                    for g in range(NG):
                        nc.gpsimd.tensor_scalar(bias[b % 2][:, g, :], dist[b % 2][:], c.slope[:, g:g + 1], 1.0,
                                                ALU.mult, ALU.mult).then_inc(bias_ready, 1)

                pool.wait_ge(cst_loaded, 16)
                root(0)
                biases(0, 0)

                def step(t, b):
                    if b == 1 and exists(t + 1) and exists(t):
                        root(t + 1)
                    biases(*before(t, b, -1))

                tiles(pool, step)

            @block.scalar
            def _(act):
                for n in range(1, 9, 2):
                    act.wait_ge(wt_full, n + 1)
                    turned(nc.scalar.copy, n).then_inc(wt_done[1], 1)

                def xT_copy(t, b):
                    act.wait_ge(kv_full[1], uses[1].filled("xT", t, b))
                    nc.scalar.copy(xT[:], kv[1][:, 0:D].rearrange("p (k n) -> p k n", k=KT)) \
                        .then_inc(kv_done[1], 1)

                xT_copy(-1, 2)

                def keys(t, b, m):
                    act.wait_ge(kv_full[m], uses[m].filled("k", t, b))
                    at_least(act, s_full, 16 * t + 4 * b - 4)
                    nc.scalar.copy(kT[b % 2][:, m, :], kv[m][:, 0:SK]).then_inc(kv_done[m], 1)

                def exps(t, b, gs):
                    if not exists(t):
                        return
                    if gs[0] == 0:
                        act.wait_ge(negm_ready, 4 * t + b + 1)
                        at_least(act, pt_full, 8 * t + 2 * b + 2 - 4)
                        at_least(act, plast_ready, 4 * t + b + 1 - 2)
                        if b == 0:
                            at_least(act, rmask_ready, t)
                    for g in gs:
                        nc.scalar.activation(prob[b % 2][:, g, :], s_sb[b % 2][:, g, :], ACT.Exp,
                                             bias=negm[:, b, g:g + 1], accum_out=esum[:, b, g:g + 1]) \
                            .then_inc(p_ready, 1)

                def step(t, b):
                    if b == 1 and exists(t - 1):
                        act.wait_ge(kv_full[1], uses[1].filled("plast", t, b))
                        nc.scalar.copy(plast_T[:], kv[1][0:16, 0:P]).then_inc(kv_done[1], 1)
                    if exists(t):
                        keys(t, b, 0)
                    te, be = before(t, b, 1)
                    exps(te, be, (0, 1))
                    if exists(t):
                        keys(t, b, 1)
                        act.wait_ge(kv_full[0], uses[0].filled("v", t, b))
                        at_least(act, pv_done, 4 * t + b + 1 - BT)
                        nc.scalar.copy(v[b][:], kv[0][:].rearrange("p (k n) -> p k n", k=2)) \
                            .then_inc(kv_done[0], 1)
                    exps(te, be, (2, 3))
                    if b == 2 and exists(t - 1):
                        act.wait_ge(kv_full[1], uses[1].filled("oT", t, b))
                        nc.scalar.copy(oT[:], kv[1][:, 0:D].rearrange("p (k n) -> p k n", k=KT)) \
                            .then_inc(kv_done[1], 1)
                    if b == 2 and exists(t) and exists(t + 1):
                        xT_copy(t, b)

                tiles(act, step)

            @block.tensor
            def _(pe):
                pe.wait_ge(cst_loaded, 16)
                wgu = wn[:].rearrange("p (j b) q -> p j (b q)", j=3)
                pe.wait_ge(w_ready, 1)
                for n in range(9):
                    at_least(pe, wt_done[n % 2], n // 2)
                    for j in range(4):
                        if n < 6:
                            i = 4 * (n % 3) + j
                            src = wgu[:, n // 3, :].rearrange("p (o k q) -> p k o q", o=FT, k=KT)[:, i // FT, i % FT, :]
                        else:
                            i = 4 * (n - 6) + j
                            src = wgu[:, 2, :].rearrange("p (o f q) -> p f o q", o=KT, f=FT)[:, i // KT, i % KT, :]
                        ins = nc.tensor.transpose(bank[n % 2][:, P * j:P * j + P], src, c.ident)
                    ins.then_inc(wt_full, 1)
                pe.wait_ge(last_ready, 1)
                pe.wait_ge(loaded["xattn"], 64)
                for t in range(NT):
                    at_least(pe, vl_done, t - 1)
                    for k in range(KT):
                        ins = nc.tensor.matmul(bank[2 + t % 2][0:16, 0:D],
                                               last_rep[:, k, BT * t:BT * t + BT, :].rearrange("p b g -> p (b g)"),
                                               w["xa_v"][:, k, :], start=(k == 0), stop=(k == KT - 1))
                    ins.then_inc(vl_full, 1)

                def turn_x(t, b):
                    pe.wait_ge(xn_ready, t + 2)
                    if not (isinstance(t, int) and t < 0):
                        pe.wait_ge(kv_done[1], uses[1].filled("xT", t, b) - 1)
                    for k in range(KT):
                        ins = nc.tensor.transpose(kv[1][:, P * k:P * k + P], xn[:, P * k:P * k + P], c.ident)
                    ins.then_inc(kv_full[1], 1)

                def queries(t, b):
                    pe.wait_ge(kv_done[1], uses[1].filled("q", t, b) - 1)
                    for m in range(KT):
                        for k in range(KT):
                            ins = nc.tensor.matmul(kv[1][:, P * m:P * m + P], w["xa_q"][:, k, P * m:P * m + P],
                                                   xT[:, k, :], start=(m == 0 and k == 0),
                                                   stop=(m == KT - 1 and k == KT - 1), skip_group_check=True)
                    ins.then_inc(kv_full[1], 1)

                turn_x(-1, 2)
                queries(-1, 3)
                pe.wait_ge(wt_done[0], 5)
                pe.wait_ge(wt_done[1], 4)
                pe.wait_ge(vl_done, NT)

                def keys(t, b, m):
                    at_least(pe, kv_done[m], uses[m].filled("k", t, b) - 1)
                    for k in range(KT):
                        ins = nc.tensor.matmul(kv[m][:, 0:SK], w["xa_k"][:, k, P * m:P * m + P], ctxT[b][:, k, :],
                                               start=(k == 0), stop=(k == KT - 1))
                    ins.then_inc(kv_full[m], 1)

                def values(t, b):
                    pe.wait_ge(kv_done[0], uses[0].filled("v", t, b) - 1)
                    for i in range(2):
                        for k in range(KT):
                            ins = nc.tensor.matmul(kv[0][:, D * i:D * i + D], ctxT[b][:, k, P * i:P * i + P],
                                                   w["xa_v"][:, k, :], start=(i == 0 and k == 0),
                                                   stop=(i == 1 and k == KT - 1), skip_group_check=True)
                    ins.then_inc(kv_full[0], 1)

                def scores(t, b):
                    pe.wait_ge(kv_done[0], uses[0].filled("k", t, b))
                    pe.wait_ge(kv_done[1], uses[1].filled("k", t, b))
                    for g in range(NG):
                        lo = 64 * (g % 2)
                        at_least(pe, s_done, 16 * t + 4 * b + g - 1)
                        nc.tensor.matmul(sc[g % 2][:, 0:SK],
                                         qbd[lo:lo + 64, g // 2, b, :, :].rearrange("p h q -> p (h q)"),
                                         kT[b % 2][lo:lo + 64, g // 2, :], start=True, stop=True).then_inc(s_full, 1)

                def turn_p(t, b):
                    for j in range(2):
                        pe.wait_ge(p_ready, 16 * t + 4 * b + 2 * j + 2)
                        at_least(pe, pt_done, 8 * t + 2 * b + j + 1 - 2)
                        for g in (2 * j, 2 * j + 1):
                            for i in range(2):
                                at = 2 * P * (g % 2) + P * i
                                ins = nc.tensor.transpose(pt[j][:, at:at + P], prob[b % 2][:, g, P * i:P * i + P],
                                                          c.ident)
                        ins.then_inc(pt_full, 1)

                def weighted(t, b):
                    pe.wait_ge(pt_done, 8 * t + 2 * b + 2)
                    pe.wait_ge(kv_done[0], uses[0].filled("v", t, b))
                    if b == 0:
                        at_least(pe, o_done, t)
                    for g in range(NG):
                        for i in range(2):
                            at = D * (b % 2) + 64 * g
                            ins = nc.tensor.matmul(oo[b // 2][:, at:at + 64], pT[b % 2][:, g, i, :],
                                                   v[b][:, i, 64 * g:64 * g + 64],
                                                   start=(b % 2 == 0 and g == 0 and i == 0), stop=False,
                                                   skip_group_check=True)
                    ins.then_inc(pv_done, 1)

                def turn_last(t, b):
                    pe.wait_ge(plast_ready, 4 * t)
                    pe.wait_ge(kv_done[1], uses[1].filled("plast", t, b) - 1)
                    nc.tensor.transpose(kv[1][0:16, 0:P], plast[:].rearrange("p b g -> p (b g)"), c.ident) \
                        .then_inc(kv_full[1], 1)

                def weighted_last(t, b):
                    pe.wait_ge(kv_done[1], uses[1].filled("plast", t, b))
                    pe.wait_ge(vx_ready, t)
                    for i in range(2):
                        ins = nc.tensor.matmul(oo[i][:], plast_T[:],
                                               vx[:, 2 * i:2 * i + 2, :, :].rearrange("p b g d -> p (b g d)"),
                                               start=False, stop=True, skip_group_check=True)
                    ins.then_inc(o_full, 1)

                def heads_to_features(t, b):
                    pe.wait_ge(o_done, t)
                    pe.wait_ge(kv_done[1], uses[1].filled("oT", t, b) - 1)
                    for bb in range(BT):
                        for m in range(KT):
                            at = P * m + SQ * bb
                            ins = nc.tensor.matmul(kv[1][:, at:at + SQ],
                                                   om[:, bb, 2 * m:2 * m + 2, :].rearrange("p g d -> p (g d)"), c.eq,
                                                   start=(bb == 0 and m == 0), stop=True, skip_group_check=True)
                    ins.then_inc(kv_full[1], 1)

                def output(t, b):
                    pe.wait_ge(kv_done[1], uses[1].filled("out", t, b) - 1)
                    for k in range(KT):
                        ins = nc.tensor.matmul(kv[1][:, 0:D], oT[:, k, :], w["xa_o"][:, k, :],
                                               start=(k == 0), stop=(k == KT - 1))
                    ins.then_inc(kv_full[1], 1)

                def step(t, b):
                    if b == 1 and exists(t - 1):
                        turn_last(t, b)
                    if exists(t):
                        pe.wait_ge(ctx_loaded[b], 48 * (t + 1))
                        keys(t, b, 0)
                        keys(t, b, 1)
                        values(t, b)
                        scores(t, b)
                    t1, b1 = before(t, b, 1)
                    if exists(t1):
                        turn_p(t1, b1)
                    if b == 2 and exists(t - 1):
                        heads_to_features(t, b)
                    t2, b2 = before(t, b, 2)
                    if exists(t2):
                        weighted(t2, b2)
                    if b == 1 and exists(t - 1):
                        weighted_last(t, b)
                    if b == 2 and exists(t) and exists(t + 1):
                        turn_x(t, b)
                    if b == 3 and exists(t) and exists(t + 1):
                        queries(t, b)
                    if b == 3 and exists(t - 1):
                        output(t, b)

                tiles(pe, step)

            @block.vector
            def _(dve):
                st = wq_steps

                def norm_stats(t):
                    st.link(dve, nc.vector.bn_stats(stat[:], x[:, t, :]))
                    alone(dve, passed_dve)
                    st.link(dve, nc.vector.bn_aggr(mv[:], stat[:]))
                    nc.vector.tensor_scalar(veps[:], mv[:, 1:2], LN_EPS, None, ALU.add).then_inc(var_ready, 1)

                def norm(t):
                    dve.wait_ge(rstd_ready, t + 1)
                    if not isinstance(t, int) or t > 0:
                        dve.wait_ge(s_full, 16 * (t - 1) + 4)
                    nc.vector.tensor_scalar(xn[:], x[:, t, :], mv[:, 0:1], rstd[:], ALU.subtract, ALU.mult) \
                        .then_inc(xn_ready, 1)

                def distances(t, b):
                    if not exists(t):
                        return
                    dve.wait_ge(ctx_loaded[b], 48 * (t + 1))
                    at_least(dve, bias_ready, 16 * t + 4 * b + 4 - 8)
                    n = st.done(nc.vector.tensor_scalar(dist[b % 2][:], kpos[b][:], qcol(t, b), None, ALU.subtract))
                    n = st.done(nc.vector.tensor_scalar(shut[:], msk[b][:], 0.0, -BIG, ALU.is_equal, ALU.mult))
                    dve.wait_ge(st.sem, n)
                    nc.vector.scalar_tensor_tensor(dist[b % 2][:], shut[:], BIG, dist[b % 2][:], ALU.mult, ALU.add) \
                        .then_inc(dist_ready, 1)

                def qcol(t, b):
                    if isinstance(t, int):
                        return qposf[:, BT * t + b:BT * t + b + 1]
                    return qposf[:, bass.ds(t * BT + b, 1)]

                def rows_max(t, b):
                    dve.wait_ge(bias_ready, 16 * t + 4 * b + 4)
                    at_least(dve, p_ready, 16 * t + 4 * b + 4 - 8)
                    for g in range(NG):
                        dve.wait_ge(s_full, 16 * t + 4 * b + g + 1)
                        alone(dve, passed_dve)
                        nc.vector.tensor_tensor_reduce(s_sb[b % 2][:, g, :], sc[g % 2][:, 0:SK], bias[b % 2][:, g, :],
                                                       1.0, float("-inf"), ALU.add, ALU.max, mx[:, b, g:g + 1]) \
                            .then_inc(s_done, 1)
                    dve.wait_ge(s_done, 16 * t + 4 * b + 4)
                    nc.vector.tensor_scalar(negm[:, b, :], mx[:, b, :], -1.0, None, ALU.mult).then_inc(negm_ready, 1)

                def spread_queries(t):
                    dve.wait_ge(kv_full[1], uses[1].filled("q", t - 1, 3))
                    at_least(dve, s_full, 16 * t)
                    for m in range(KT):
                        src = kv[1][:, P * m:P * m + P].rearrange("p (b q) -> p b q", b=BT)
                        ins = nc.vector.tensor_tensor(
                            qbd[:, m, :, :, :], src.unsqueeze(2).broadcast_to([P, BT, 4, SQ]),
                            c.quarter.unsqueeze(1).unsqueeze(3).broadcast_to([P, BT, 4, SQ]), ALU.mult)
                    ins.then_inc(kv_done[1], 1)

                def copy_turned(t, b):
                    dve.wait_ge(p_ready, 16 * t + 4 * b + 4)
                    if b == 0:
                        at_least(dve, kv_full[1], 0 if isinstance(t, int) and t == 0
                                 else uses[1].filled("plast", t, 1))
                    nc.vector.tensor_copy(plast[:, b, :], prob[b % 2][:, :, SK - 1]).then_inc(plast_ready, 1)
                    at_least(dve, pv_done, 4 * t + b + 1 - 2)
                    for j in range(2):
                        dve.wait_ge(pt_full, 8 * t + 2 * b + j + 1)
                        nc.vector.tensor_copy(pT[b % 2][:, 2 * j:2 * j + 2, :, :],
                                              pt[j][:].rearrange("p (g i n) -> p g i n", g=2, i=2)) \
                            .then_inc(pt_done, 1)

                def spread_last(t):
                    if not (isinstance(t, int) and t == 0):
                        dve.wait_ge(o_full, t)
                    src = v_last[:, t, :].rearrange("p (g d) -> p g d", g=NG)
                    for b in range(BT):
                        ins = nc.vector.tensor_tensor(
                            vx[:, b, :, :], src, c.last[:, NG * b:NG * b + NG].unsqueeze(2).broadcast_to([16, NG, 64]),
                            ALU.mult)
                    ins.then_inc(vx_ready, 1)

                def weigh(t):
                    dve.wait_ge(p_ready, 16 * t + 16)
                    st.link(dve, nc.vector.tensor_scalar(rden[:], esum[:], 1.0, None, ALU.add))
                    st.link(dve, nc.vector.reciprocal(rden[:], rden[:]))
                    nc.vector.tensor_tensor(
                        rmask[:].rearrange("p b g h -> p (b g) h"),
                        rden[:].rearrange("p b g -> p (b g)").unsqueeze(2).broadcast_to([P, 16, 4]),
                        c.row.unsqueeze(1).broadcast_to([P, 16, 4]), ALU.mult).then_inc(rmask_ready, 1)

                def normalise(t):
                    dve.wait_ge(rmask_ready, t + 1)
                    dve.wait_ge(o_full, t + 1)
                    for i in range(2):
                        ins = nc.vector.tensor_tensor(
                            om[:, 2 * i:2 * i + 2, :, :].rearrange("p b g (h d) -> p (b g h) d", h=4),
                            oo[i][:].rearrange("p (n d) -> p n d", d=DH),
                            rmask[:, 2 * i:2 * i + 2, :, :].rearrange("p b g h -> p (b g h)").unsqueeze(2)
                            .broadcast_to([P, 32, DH]), ALU.mult)
                    ins.then_inc(o_done, 1)

                def add_output(t, tt):
                    dve.wait_ge(kv_full[1], uses[1].filled("out", t, 3))
                    nc.vector.tensor_tensor(x[:, tt, :], kv[1][:, 0:D], x[:, tt, :], ALU.add).then_inc(kv_done[1], 1)

                def step(t, b):
                    t1, b1 = before(t, b, 1)
                    if b == 1 and exists(t - 1):
                        weigh(t - 1)
                    if b == 2 and exists(t - 1):
                        normalise(t - 1)
                    if exists(t):
                        rows_max(t, b)
                    if exists(t1):
                        copy_turned(t1, b1)
                    if b == 1 and exists(t) and exists(t + 1):
                        norm_stats(t + 1)
                        norm(t + 1)
                    if b == 3 and exists(t) and exists(t + 1):
                        spread_queries(t + 1)
                    if b == 3 and exists(t - 1):
                        add_output(t, t - 1)
                    if exists(t):
                        distances(*before(t, b, -1))
                    if b == 3 and exists(t):
                        spread_last(t)

                dve.wait_ge(cst_loaded, 16)
                dve.wait_ge(wn_loaded, 48)
                st.link(dve, nc.vector.tensor_reduce(wmax[:], wn[:], AX.X, ALU.max, apply_absolute_value=True))
                st.link(dve, nc.vector.tensor_scalar(wscale[:], wmax[:], 1.0 / 7.0, 1e-12, ALU.mult, ALU.max))
                st.link(dve, nc.vector.reciprocal(wrecip[:], wscale[:]))
                each = [P, NBLK, QB]
                st.link(dve, nc.vector.tensor_tensor(wn[:], wn[:], wrecip[:].unsqueeze(2).broadcast_to(each), ALU.mult))
                st.link(dve, nc.vector.tensor_scalar(wn[:], wn[:], ROUND, ROUND, ALU.add, ALU.subtract))
                nc.vector.tensor_tensor(wn[:], wn[:], wscale[:].unsqueeze(2).broadcast_to(each), ALU.mult) \
                    .then_inc(w_ready, 1)
                for n in range(0, 9, 2):
                    dve.wait_ge(wt_full, n + 1)
                    turned(nc.vector.tensor_copy, n).then_inc(wt_done[0], 1)
                for t in range(NT):
                    dve.wait_ge(vl_full, t + 1)
                    nc.vector.tensor_copy(v_last[:, t, :], bank[2 + t % 2][0:16, 0:D]).then_inc(vl_done, 1)
                dve.wait_ge(vl_done, NT)
                dve.wait_ge(last_ready, 2)
                dve.wait_ge(x_loaded, 16)
                norm_stats(0)
                norm(0)
                distances(0, 0)
                spread_queries(0)
                tiles(dve, step, st, 4 * 2 + 2 + 2)



def turn_tokens(nc, dst, src, c):
    for k in range(KT):
        ins = nc.tensor.transpose(dst[:, P * k:P * k + P], src[:, P * k:P * k + P], c.ident)
    return ins


def project_qk(nc, dst, weight, xT):
    for m in range(2 * KT):
        for k in range(KT):
            ins = nc.tensor.matmul(dst[:, P * m:P * m + P], weight[:, k, P * m:P * m + P], xT[:, k, :],
                                   start=(m == 0 and k == 0), stop=True, skip_group_check=True)
    return ins


def project_tokens(nc, dst, lhs_T, weight):
    n = weight.shape[1]
    for k in range(n):
        ins = nc.tensor.matmul(dst[:, 0:D], lhs_T[:, k, :], weight[:, k, :], start=(k == 0), stop=(k == n - 1))
    return ins


def spread_heads(eng, qbd, qT, head):
    for m in range(KT):
        src = qT[:, m, :].rearrange("p (b q) -> p b q", b=BT)
        ins = eng.tensor_tensor(qbd[:, m, :, :, :], src.unsqueeze(2).broadcast_to([P, BT, 4, SQ]),
                                head.unsqueeze(1).unsqueeze(3).broadcast_to([P, BT, 4, SQ]), ALU.mult)
    return ins


def spread_batches(eng, vbd, v, c):
    for g in range(NG):
        ins = eng.tensor_tensor(vbd[:, g, :, :], v[:, 64 * g:64 * g + 64].unsqueeze(1).broadcast_to([P, BT, 64]),
                                c.row.unsqueeze(2).broadcast_to([P, BT, 64]), ALU.mult)
    return ins


def score_heads(nc, dst, qbd, kT, f, first):
    lo = 64 * f
    for m in range(KT):
        for b in range(BT):
            at = P * m + SQ * b
            ins = nc.tensor.matmul(dst[:, at:at + SQ], qbd[lo:lo + 64, m, b, :, :].rearrange("p h q -> p (h q)"),
                                   kT[lo:lo + 64, m, SQ * b:SQ * b + SQ], start=first, stop=True,
                                   skip_group_check=True)
            first = False
    return ins


def turn_probabilities(nc, dst, prob, c):
    for g in range(NG):
        ins = nc.tensor.transpose(dst[:, P * g:P * g + P], prob[:, g, :, :].rearrange("p b k -> p (b k)"), c.ident)
    return ins


def weigh_values(nc, dst, pT, vbd):
    for g in range(NG):
        at = D * (g % 2)
        ins = nc.tensor.matmul(dst[g // 2][:, at:at + D], pT[:, g, :], vbd[:, g, :, :].rearrange("p b d -> p (b d)"),
                               start=(g % 2 == 0), stop=True, skip_group_check=True)
    return ins


def own_heads(nc, om, src, rmask):
    for g in range(NG):
        at = D * (g % 2)
        ins = nc.vector.tensor_tensor(
            om[:, :, g, :].rearrange("p b (h d) -> p b h d", h=4),
            src[g // 2][:, at:at + D].rearrange("p (b h d) -> p b h d", b=BT, h=4),
            rmask[:, g, :, :].unsqueeze(3).broadcast_to([P, BT, 4, DH]), ALU.mult)
    return ins


def heads_to_features(nc, dst, om, c):
    for m in range(KT):
        for b in range(BT):
            at = P * m + SQ * b
            ins = nc.tensor.matmul(dst[:, at:at + SQ], om[:, b, 2 * m:2 * m + 2, :].rearrange("p g d -> p (g d)"), c.eq,
                                   start=(m == 0 and b == 0), stop=True, skip_group_check=True)
    return ins


def halves(scores, f):
    return scores[:].rearrange("p (m f) b k -> p f m (b k)", f=2)[:, f, :, :]


def slots(eng, step, count=NT, steps=None, per=None):
    step(-1)
    step(0)
    with eng.Fori(1, count - 2) as u:
        if steps:
            steps.enter(u, 1, per)
        step(u)
        if steps:
            steps.leave(count - 3)
    step(count - 2)
    step(count - 1)


def there(u, count=NT):
    return not isinstance(u, int) or 0 <= u < count


def ratio_attention(nc, a, sb_, sem, bank, c, x, w, loaded):
    with ExitStack() as own:
        def sb(name, shape, dt=F32):
            return sb_("ra_" + name, shape, dt, own)

        def rsem(name):
            return sem("ra_" + name)

        xn, xT = sb("xn", [P, D]), sb("xT", [P, KT, P])
        stat, mv, veps, rstd = sb("stat", [P, 6]), sb("mv", [P, 2]), sb("veps", [P, 1]), sb("rstd", [P, 1])
        qT, kT, k2T = sb("qT", [P, KT, P]), sb("kT", [P, KT, P]), sb("k2T", [P, KT, P])
        v, vbd = sb("v", [P, D]), sb("vbd", [P, NG, BT, 64])
        qbd, q2bd = sb("qbd", [P, KT, BT, 4, SQ]), sb("q2bd", [P, KT, BT, 4, SQ])
        dot, num = sb("dot", [P, NG, BT, SQ]), sb("num", [P, NG, BT, SQ])
        den, score, prob = sb("den", [P, NG, BT, SQ]), sb("score", [P, NG, BT, SQ]), sb("prob", [P, NG, BT, SQ])
        mx, esum, rden = sb("mx", [P, 16]), sb("esum", [P, 16]), sb("rden", [P, 16])
        rmask, om = sb("rmask", [P, NG, BT, 4]), sb("om", [P, BT, NG, 64])
        pT, oT, y = sb("pT", [P, NG, P]), sb("oT", [P, KT, P]), sb("y", [P, D])
        b_qk, s_bank, v_bank, p_bank, o_bank, m_bank = bank[0], bank[1:3], bank[3], bank[4], bank[5:7], bank[7]

        st = Steps(rsem("dve_steps"))
        passed_dve, passed_pool, passed_act = rsem("passed_dve"), rsem("passed_pool"), rsem("passed_act")
        var_ready, rstd_ready, xn_ready = rsem("var_ready"), rsem("rstd_ready"), rsem("xn_ready")
        xT_full, xT_done = rsem("xT_full"), rsem("xT_done")
        qk_full, qk_done, v_full, v_done = rsem("qk_full"), rsem("qk_done"), rsem("v_full"), rsem("v_done")
        qbd_ready, q2_ready, vbd_ready = rsem("qbd_ready"), rsem("q2_ready"), rsem("vbd_ready")
        s_full, s_read, den_read = rsem("s_full"), rsem("s_read"), rsem("den_read")
        sub_ready, p_ready, pT_full, pT_done = rsem("sub_ready"), rsem("p_ready"), rsem("pT_full"), rsem("pT_done")
        o_full, o_done, oT_full, oT_done = rsem("o_full"), rsem("o_done"), rsem("oT_full"), rsem("oT_done")
        y_full, y_done = rsem("y_full"), rsem("y_done")

        with nc.Block() as block:
            @block.gpsimd
            def _(pool):
                def root(u):
                    pool.wait_ge(var_ready, u + 1)
                    nc.gpsimd.tensor_tensor(rstd[:], veps[:], c.half[:, 0:1], ALU.pow).then_inc(rstd_ready, 1)

                def step(u):
                    n = u + 1
                    if there(n):
                        pool.wait_ge(qk_done, n + 1)
                        at_least(pool, s_full, n)
                        alone(pool, passed_pool)
                        spread_heads(nc.gpsimd, qbd, qT, c.head).then_inc(qbd_ready, 1)
                        pool.wait_ge(v_done, n + 1)
                        at_least(pool, o_full, n)
                        alone(pool, passed_pool)
                        spread_batches(nc.gpsimd, vbd, v, c).then_inc(vbd_ready, 1)
                    if there(u + 2):
                        root(u + 2)

                root(0)
                slots(pool, step)

            @block.scalar
            def _(act):
                act.wait_ge(loaded["ratio"], 16 * len(GROUPS["ratio"]))

                def step(u):
                    n = u + 1
                    if there(n):
                        act.wait_ge(xT_full, n + 1)
                        nc.scalar.copy(xT[:], m_bank[:, 0:D].rearrange("p (k t) -> p k t", k=KT)).then_inc(xT_done, 1)
                        act.wait_ge(qk_full, n + 1)
                        at_least(act, qbd_ready, n)
                        at_least(act, s_full, n)
                        for m in range(KT):
                            nc.scalar.activation(qT[:, m, :], b_qk[:, P * m:P * m + P], ACT.Identity,
                                                 bias=w["ra_bqk"][:, m:m + 1])
                            at = P * (KT + m)
                            nc.scalar.activation(kT[:, m, :], b_qk[:, at:at + P], ACT.Identity,
                                                 bias=w["ra_bqk"][:, KT + m:KT + m + 1])
                            ins = nc.scalar.activation(k2T[:, m, :], b_qk[:, at:at + P], ACT.Square,
                                                       bias=w["ra_bqk"][:, KT + m:KT + m + 1])
                        ins.then_inc(qk_done, 1)
                    if there(u):
                        act.wait_ge(pT_full, u + 1)
                        nc.scalar.copy(pT[:], p_bank[:].rearrange("p (g t) -> p g t", g=NG)).then_inc(pT_done, 1)
                    if there(n):
                        act.wait_ge(qbd_ready, n + 1)
                        nc.scalar.activation(q2bd[:], qbd[:], ACT.Square).then_inc(q2_ready, 1)
                        act.wait_ge(s_full, n + 1)
                        at_least(act, sub_ready, n)
                        for f in range(2):
                            src = s_bank[f][:, 0:D].rearrange("p (m t) -> p m t", m=KT)
                            nc.scalar.copy(halves(dot, f), src)
                            ins = nc.scalar.activation(halves(num, f), src, ACT.Square)
                        ins.then_inc(s_read, 1)
                    if there(u):
                        act.wait_ge(oT_full, u + 1)
                        nc.scalar.copy(oT[:], m_bank[:, 0:D].rearrange("p (k t) -> p k t", k=KT)).then_inc(oT_done, 1)
                    if there(n):
                        act.wait_ge(sub_ready, n + 1)
                        at_least(act, pT_full, n)
                        nc.scalar.activation(prob[:], score[:], ACT.Exp).then_inc(p_ready, 1)

                slots(act, step)

            @block.tensor
            def _(pe):
                pe.wait_ge(loaded["ratio"], 16 * len(GROUPS["ratio"]))

                def step(u):
                    n = u + 1
                    if there(n):
                        pe.wait_ge(xn_ready, n + 1)
                        at_least(pe, y_done, n - 1)
                        turn_tokens(nc, m_bank, xn, c).then_inc(xT_full, 1)
                        pe.wait_ge(xT_done, n + 1)
                        at_least(pe, qk_done, n)
                        project_qk(nc, b_qk, w["ra_qkv"], xT).then_inc(qk_full, 1)
                        at_least(pe, v_done, n)
                        project_tokens(nc, v_bank, xT, w["ra_qkv"][:, :, 2 * D:3 * D]).then_inc(v_full, 1)
                    if there(u):
                        pe.wait_ge(p_ready, u + 1)
                        at_least(pe, pT_done, u)
                        turn_probabilities(nc, p_bank, prob, c).then_inc(pT_full, 1)
                        pe.wait_ge(pT_done, u + 1)
                        pe.wait_ge(vbd_ready, u + 1)
                        at_least(pe, o_done, u)
                        weigh_values(nc, o_bank, pT, vbd).then_inc(o_full, 1)
                    if there(n):
                        pe.wait_ge(q2_ready, n + 1)
                        at_least(pe, s_read, n)
                        at_least(pe, den_read, n)
                        for f in range(2):
                            lo = 64 * f
                            score_heads(nc, s_bank[f], qbd, kT, f, True)
                            for m in range(KT):
                                at = D + P * m
                                nc.tensor.matmul(s_bank[f][:, at:at + P], c.headq[lo:lo + 64, :], k2T[lo:lo + 64, m, :],
                                                 start=False, stop=False, skip_group_check=True)
                                for b in range(BT):
                                    ins = nc.tensor.matmul(s_bank[f][:, at + SQ * b:at + SQ * b + SQ],
                                                           q2bd[lo:lo + 64, m, b, :, :].rearrange("p h q -> p (h q)"),
                                                           c.ones[lo:lo + 64, :], start=False, stop=True,
                                                           skip_group_check=True)
                        ins.then_inc(s_full, 1)
                    if there(u):
                        pe.wait_ge(o_done, u + 1)
                        if there(n):
                            pe.wait_ge(xT_done, n + 1)
                        heads_to_features(nc, m_bank, om, c).then_inc(oT_full, 1)
                        pe.wait_ge(oT_done, u + 1)
                        project_tokens(nc, m_bank, oT, w["ra_o"]).then_inc(y_full, 1)

                slots(pe, step)

            @block.vector
            def _(dve):
                def norm(u):
                    st.link(dve, nc.vector.bn_stats(stat[:], x[:, u, :]))
                    alone(dve, passed_dve)
                    st.link(dve, nc.vector.bn_aggr(mv[:], stat[:]))
                    nc.vector.tensor_scalar(veps[:], mv[:, 1:2], LN_EPS, None, ALU.add).then_inc(var_ready, 1)
                    dve.wait_ge(rstd_ready, u + 1)
                    at_least(dve, xT_full, u)
                    nc.vector.tensor_scalar(xn[:], x[:, u, :], mv[:, 0:1], rstd[:], ALU.subtract, ALU.mult) \
                        .then_inc(xn_ready, 1)

                def step(u):
                    n = u + 1
                    if there(n):
                        dve.wait_ge(v_full, n + 1)
                        at_least(dve, vbd_ready, n)
                        nc.vector.tensor_tensor(v[:], v_bank[:, 0:D], w["ra_bv"][:], ALU.add).then_inc(v_done, 1)
                    if there(u):
                        dve.wait_ge(p_ready, u + 1)
                        st.link(dve, nc.vector.tensor_reduce(esum[:], prob[:].rearrange("p g b k -> p (g b) k"),
                                                             AX.X, ALU.add))
                        st.link(dve, nc.vector.reciprocal(rden[:], esum[:]))
                        st.link(dve, nc.vector.tensor_tensor(
                            rmask[:].rearrange("p g b h -> p (g b) h"), rden[:].unsqueeze(2).broadcast_to([P, 16, 4]),
                            c.row.unsqueeze(1).broadcast_to([P, 16, 4]), ALU.mult))
                        dve.wait_ge(o_full, u + 1)
                        own_heads(nc, om, o_bank, rmask).then_inc(o_done, 1)
                    if there(n):
                        dve.wait_ge(s_read, n + 1)
                        for f in range(2):
                            ins = nc.vector.scalar_tensor_tensor(
                                halves(den, f), halves(dot, f), -2.0,
                                s_bank[f][:, D:2 * D].rearrange("p (m t) -> p m t", m=KT), ALU.mult, ALU.add)
                        ins.then_inc(den_read, 1)
                        dve.wait_ge(den_read, n + 1)
                        st.link(dve, nc.vector.tensor_scalar(den[:], den[:], 1e-6, None, ALU.add))
                        st.link(dve, nc.vector.reciprocal(den[:], den[:]))
                        st.link(dve, nc.vector.tensor_tensor(num[:], num[:], den[:], ALU.mult))
                        flat = [P, 16, SQ]
                        flatten = "p g b k -> p (g b) k"
                        at_least(dve, p_ready, n)
                        st.link(dve, nc.vector.tensor_tensor(
                            score[:].rearrange(flatten), num[:].rearrange(flatten),
                            c.causal.unsqueeze(1).broadcast_to(flat), ALU.add))
                        st.link(dve, nc.vector.tensor_reduce(mx[:], score[:].rearrange(flatten), AX.X, ALU.max))
                        nc.vector.tensor_tensor(score[:].rearrange(flatten), score[:].rearrange(flatten),
                                                mx[:].unsqueeze(2).broadcast_to(flat), ALU.subtract) \
                            .then_inc(sub_ready, 1)
                    if there(u):
                        dve.wait_ge(y_full, u + 1)
                        st.link(dve, nc.vector.tensor_tensor(y[:], m_bank[:, 0:D], w["ra_bo"][:], ALU.add))
                        nc.vector.tensor_tensor(x[:, u, :], x[:, u, :], y[:], ALU.add).then_inc(y_done, 1)
                    if there(u + 2):
                        norm(u + 2)

                dve.wait_ge(loaded["ratio"], 16 * len(GROUPS["ratio"]))
                norm(0)
                slots(dve, step, steps=st, per=3 + 5 + 1 + 2)


def quantised_ffn(nc, a, sb_, sem, bank, c, x, w_gate_T, w_up_T, w_down_T):
    with ExitStack() as own:
        def sb(name, shape, dt=F32):
            return sb_("ff_" + name, shape, dt, own)

        def fsem(name):
            return sem("ff_" + name)

        T = NT * P
        stats, mv = sb("stats", [P, NT, 6]), sb("mv", [P, NT, 2])
        veps, rstd = sb("veps", [P, NT]), sb("rstd", [P, NT])
        xn, xT = sb("xn", [P, NT, D]), sb("xT", [P, KT, T])
        gate, up, sig = sb("gate", [P, FT, T]), sb("up", [P, FT, T]), sb("sig", [P, FT, T])
        X, G, U, H, O = range(5)
        peak, top = sb("peak", [P, 5, 2 * FT]), sb("top", [P, 5])
        topall, scale, inv = sb("topall", [P, 5]), sb("scale", [P, 5]), sb("inv", [P, 5])
        st = Steps(fsem("dve_steps"))
        pool_steps = Steps(fsem("pool_steps"))
        veps_ready, rstd_ready = fsem("veps_ready"), fsem("rstd_ready")
        top_ready, topall_ready = [fsem(f"top_ready{i}") for i in range(5)], [fsem(f"topall_ready{i}") for i in range(5)]
        xn_ready, xT_full, xT_done = fsem("xn_ready"), fsem("xT_full"), fsem("xT_done")
        gu_full, gu_done, peak_done = fsem("gu_full"), fsem("gu_done"), fsem("peak_done")
        gate_ready, sig_ready, up_ready = fsem("gate_ready"), fsem("sig_ready"), fsem("up_ready")
        up_scale, o_ready, y_full = fsem("up_scale"), fsem("o_ready"), fsem("y_full")

        with nc.Block() as block:
            @block.gpsimd
            def _(pool):
                pool.wait_ge(veps_ready, 1)
                nc.gpsimd.tensor_tensor(rstd[:], veps[:], c.half[:, 0:NT], ALU.pow).then_inc(rstd_ready, 1)

                def largest(i):
                    pool.wait_ge(top_ready[i], 1)
                    nc.gpsimd.partition_all_reduce(topall[:, i:i + 1], top[:, i:i + 1], P, RMAX) \
                        .then_inc(topall_ready[i], 1)

                for i in (X, G, U):
                    largest(i)
                pool.wait_ge(up_scale, 1)
                for m in range(FT):
                    pool_steps.link(pool, nc.gpsimd.tensor_scalar(up[:, m, :], up[:, m, :], inv[:, U:U + 1], ROUND,
                                                                  ALU.mult, ALU.add))
                    nc.gpsimd.tensor_scalar(up[:, m, :], up[:, m, :], -ROUND, scale[:, U:U + 1],
                                            ALU.add, ALU.mult).then_inc(up_ready, 1)
                for i in (H, O):
                    largest(i)

            @block.scalar
            def _(act):
                for i in range(NT // 2):
                    act.wait_ge(xT_full, i + 1)
                    src = bank[i % 2][:].rearrange("p (j k t) -> p j k t", j=2, k=KT)
                    for j in range(2):
                        at = P * (2 * i + j)
                        ins = nc.scalar.copy(xT[:, :, at:at + P], src[:, j, :, :])
                    ins.then_inc(xT_done, 1)
                for n in range(4 * FT):
                    act.wait_ge(gu_full, n + 1)
                    dst = (gate, up)[n // (2 * FT)]
                    m, h = n // 2 % FT, n % 2
                    nc.scalar.copy(dst[:, m, 512 * h:512 * h + 512], bank[2 + n % 6][:]).then_inc(gu_done, 1)
                for m in range(FT):
                    act.wait_ge(gate_ready, m + 1)
                    nc.scalar.activation(sig[:, m, :], gate[:, m, :], ACT.Sigmoid).then_inc(sig_ready, 1)

            @block.tensor
            def _(pe):
                for i in range(NT // 2):
                    pe.wait_ge(xn_ready, i + 1)
                    at_least(pe, xT_done, i - 1)
                    for j in range(2):
                        ins = turn_tokens(nc, bank[i % 2][:, D * j:D * j + D], xn[:, 2 * i + j, :], c)
                    ins.then_inc(xT_full, 1)
                pe.wait_ge(xT_done, NT // 2)
                for n in range(4 * FT):
                    wt = (w_gate_T, w_up_T)[n // (2 * FT)]
                    m, h = n // 2 % FT, n % 2
                    at_least(pe, gu_done, n - 5)
                    for k in range(KT):
                        ins = nc.tensor.matmul(bank[2 + n % 6][:], wt[:, k, P * m:P * m + P],
                                               xT[:, k, 512 * h:512 * h + 512], start=(k == 0), stop=(k == KT - 1))
                    ins.then_inc(gu_full, 1)
                pe.wait_ge(gu_done, 4 * FT)
                pe.wait_ge(o_ready, 2 * FT)
                for t in range(NT):
                    for f in range(FT):
                        ins = nc.tensor.matmul(bank[t][:, 0:D], gate[:, f, P * t:P * t + P], w_down_T[:, f, :],
                                               start=(f == 0), stop=(f == FT - 1))
                    ins.then_inc(y_full, 1)

            @block.vector
            def _(dve):
                for t in range(NT):
                    ins = nc.vector.bn_stats(stats[:, t, :], x[:, t, :])
                st.link(dve, ins)
                for t in range(NT):
                    ins = nc.vector.bn_aggr(mv[:, t, :], stats[:, t, :])
                st.link(dve, ins)
                nc.vector.tensor_scalar(veps[:], mv[:, :, 1], LN_EPS, None, ALU.add).then_inc(veps_ready, 1)
                dve.wait_ge(rstd_ready, 1)
                for t in range(NT):
                    ins = nc.vector.tensor_scalar(xn[:, t, :], x[:, t, :], mv[:, t, 0:1], rstd[:, t:t + 1],
                                                  ALU.subtract, ALU.mult)
                st.link(dve, ins)

                def scales(i, n):
                    nc.vector.tensor_reduce(top[:, i:i + 1], peak[:, i, 0:n], AX.X, ALU.max).then_inc(top_ready[i], 1)
                    dve.wait_ge(topall_ready[i], 1)
                    st.link(dve, nc.vector.tensor_scalar(scale[:, i:i + 1], topall[:, i:i + 1], 1.0 / 32767.0, 1e-12,
                                                         ALU.mult, ALU.max))
                    st.link(dve, nc.vector.reciprocal(inv[:, i:i + 1], scale[:, i:i + 1]))

                def rounded(piece, i):
                    st.link(dve, nc.vector.tensor_scalar(piece, piece, inv[:, i:i + 1], ROUND, ALU.mult, ALU.add))
                    return nc.vector.tensor_scalar(piece, piece, ROUND, scale[:, i:i + 1], ALU.subtract, ALU.mult)

                def magnitude(i, n, piece):
                    return nc.vector.tensor_reduce(peak[:, i, n:n + 1], piece, AX.XY if len(piece.shape) == 3 else AX.X,
                                                   ALU.max, apply_absolute_value=True)

                st.link(dve, magnitude(X, 0, xn[:]))
                scales(X, 1)
                for i in range(NT // 2):
                    rounded(xn[:, 2 * i:2 * i + 2, :], X).then_inc(xn_ready, 1)
                for n in range(4 * FT):
                    dve.wait_ge(gu_done, n + 1)
                    src = (gate, up)[n // (2 * FT)]
                    m, h = n // 2 % FT, n % 2
                    ins = magnitude((G, U)[n // (2 * FT)], n % (2 * FT), src[:, m, 512 * h:512 * h + 512])
                    if n % (2 * FT) == 2 * FT - 1:
                        st.link(dve, ins)
                        scales((G, U)[n // (2 * FT)], 2 * FT)
                        if n // (2 * FT) == 0:
                            for k in range(FT):
                                rounded(gate[:, k, :], G).then_inc(gate_ready, 1)
                dve.sem_inc(up_scale, 1)
                for m in range(FT):
                    dve.wait_ge(sig_ready, m + 1)
                    st.link(dve, nc.vector.tensor_scalar(sig[:, m, :], sig[:, m, :], 65536.0, ROUND, ALU.mult, ALU.add))
                    st.link(dve, nc.vector.tensor_scalar(sig[:, m, :], sig[:, m, :], ROUND, 65535.0,
                                                         ALU.subtract, ALU.min))
                    st.link(dve, nc.vector.scalar_tensor_tensor(gate[:, m, :], sig[:, m, :], 1.0 / 65536.0, gate[:, m, :],
                                                                ALU.mult, ALU.mult))
                    st.link(dve, magnitude(H, m, gate[:, m, :]))
                scales(H, FT)
                for m in range(FT):
                    st.link(dve, rounded(gate[:, m, :], H))
                    dve.wait_ge(up_ready, m + 1)
                    st.link(dve, nc.vector.tensor_tensor(gate[:, m, :], gate[:, m, :], up[:, m, :], ALU.mult))
                    st.link(dve, magnitude(O, m, gate[:, m, :]))
                scales(O, FT)
                for m in range(FT):
                    for h in range(2):
                        rounded(gate[:, m, 512 * h:512 * h + 512], O).then_inc(o_ready, 1)
                for t in range(NT):
                    dve.wait_ge(y_full, t + 1)
                    nc.vector.tensor_tensor(x[:, t, :], bank[t][:, 0:D], x[:, t, :], ALU.add)


def context_attention(nc, a, sb_, sem, bank, c, x, w, loaded):
    with ExitStack() as own:
        def sb(name, shape, dt=F32):
            return sb_("cx_" + name, shape, dt, own)

        def csem(name):
            return sem("cx_" + name)

        SCALE = D ** -0.5
        xn, xT = sb("xn", [P, D]), sb("xT", [P, KT, P])
        stat, mv, veps, rstd = sb("stat", [P, 6]), sb("mv", [P, 2]), sb("veps", [P, 1]), sb("rstd", [P, 1])
        ctxT = [sb(f"ctxT{b}", [P, KT, SK]) for b in range(BT)]
        cn = [sb(f"ctx{b}", [P, 2, D]) for b in range(BT)]
        last = sb("last", [BT, D])
        qT, qk, qb = sb("qT", [P, KT, P]), sb("qk", [P, KT, P]), sb("qb", [P, 1])
        mx, nb = sb("mx", [P, 1]), sb("nb", [P, 1])
        raw, esum, rden = sb("raw", [P, SK]), sb("esum", [P, 1]), sb("rden", [P, 1])
        prob, plast = sb("prob", [P, SK]), sb("plast", [P, BT])
        pT, plT = sb("pT", [P, 2, P]), sb("plT", [BT, P])
        aT, y = sb("aT", [P, KT, P]), sb("y", [P, D])
        x_bank, q_bank, k_bank, s_bank, p_bank, a_bank, y_bank = bank[0:7]

        st = Steps(csem("dve_steps"))
        passed_dve, passed_sp = csem("passed_dve"), csem("passed_sp")
        ctxT_loaded = [csem(f"ctxT_loaded{b}") for b in range(BT)]
        ctx_loaded = [csem(f"ctx_loaded{b}") for b in range(BT)]
        last_loaded = csem("last_loaded")
        var_ready, rstd_ready, xn_ready = csem("var_ready"), csem("rstd_ready"), csem("xn_ready")
        xT_full, xT_done, q_full, q_done = csem("xT_full"), csem("xT_done"), csem("q_full"), csem("q_done")
        k_full, k_done, qb_ready = csem("k_full"), csem("k_done"), csem("qb_ready")
        s_full, nb_ready, e_ready = csem("s_full"), csem("nb_ready"), csem("e_ready")
        p_ready, p_full, p_done = csem("p_ready"), csem("p_full"), csem("p_done")
        a_full, a_done, y_full, y_done = csem("a_full"), csem("a_done"), csem("y_full"), csem("y_done")

        with nc.Block() as block:
            @block.sync
            def _(sp):
                def turned(t):
                    for b in range(BT):
                        sp.dma_start(ctxT[b][:], a["ctx_T"][BT * t + b]).then_inc(ctxT_loaded[b], 16)

                def plain(t):
                    for b in range(BT):
                        sp.dma_start(cn[b][:], a["ctx"][BT * t + b, 0:SK - 1, :].rearrange("(i p) d -> p i d", p=P)) \
                            .then_inc(ctx_loaded[b], 16)
                    sp.dma_start(last[:], a["ctx_rows"][t]).then_inc(last_loaded, 16)

                turned(0)
                plain(0)
                with sp.Fori(1, NT) as t:
                    sp.wait_ge(s_full, t)
                    alone(sp, passed_sp)
                    turned(t)
                    sp.wait_ge(a_full, t)
                    alone(sp, passed_sp)
                    plain(t)

            @block.gpsimd
            def _(pool):
                def step(u):
                    if there(u + 2):
                        pool.wait_ge(var_ready, u + 3)
                        nc.gpsimd.tensor_tensor(rstd[:], veps[:], c.half[:, 0:1], ALU.pow).then_inc(rstd_ready, 1)

                pool.wait_ge(var_ready, 1)
                nc.gpsimd.tensor_tensor(rstd[:], veps[:], c.half[:, 0:1], ALU.pow).then_inc(rstd_ready, 1)
                slots(pool, step)

            @block.scalar
            def _(act):
                act.wait_ge(loaded["cross"], 16 * len(GROUPS["cross"]))

                def step(u):
                    n = u + 1
                    if there(n):
                        act.wait_ge(xT_full, n + 1)
                        nc.scalar.copy(xT[:], x_bank[:, 0:D].rearrange("p (k t) -> p k t", k=KT)).then_inc(xT_done, 1)
                        act.wait_ge(q_full, n + 1)
                        for m in range(KT):
                            ins = nc.scalar.activation(qT[:, m, :], q_bank[:, P * m:P * m + P], ACT.Identity,
                                                       bias=w["cx_bq"][:, m:m + 1])
                        ins.then_inc(q_done, 1)
                        act.wait_ge(k_full, n + 1)
                        at_least(act, qb_ready, n)
                        at_least(act, s_full, n)
                        nc.scalar.copy(qk[:], k_bank[:, 0:D].rearrange("p (k t) -> p k t", k=KT))
                        nc.scalar.mul(qb[:], k_bank[:, D:D + 1], SCALE).then_inc(k_done, 1)
                    if there(u):
                        act.wait_ge(p_full, u + 1)
                        at_least(act, a_full, u)
                        nc.scalar.copy(pT[:], p_bank[:, 0:2 * P].rearrange("p (i t) -> p i t", i=2))
                        nc.scalar.copy(plT[:], p_bank[0:BT, 2 * P:3 * P]).then_inc(p_done, 1)
                        act.wait_ge(a_full, u + 1)
                        nc.scalar.copy(aT[:], a_bank[:, 0:D].rearrange("p (k t) -> p k t", k=KT)).then_inc(a_done, 1)
                    if there(n):
                        act.wait_ge(nb_ready, n + 1)
                        at_least(act, p_ready, n)
                        nc.scalar.activation(raw[:], s_bank[:, 0:SK], ACT.Exp, bias=nb[:], scale=SCALE,
                                             accum_out=esum[:]).then_inc(e_ready, 1)

                slots(act, step)

            @block.tensor
            def _(pe):
                pe.wait_ge(loaded["cross"], 16 * len(GROUPS["cross"]))

                def step(u):
                    n = u + 1
                    if there(n):
                        pe.wait_ge(xn_ready, n + 1)
                        at_least(pe, xT_done, n)
                        turn_tokens(nc, x_bank, xn, c).then_inc(xT_full, 1)
                        pe.wait_ge(xT_done, n + 1)
                        at_least(pe, q_done, n)
                        for m in range(KT):
                            for k in range(KT):
                                ins = nc.tensor.matmul(q_bank[:, P * m:P * m + P], w["cx_q"][:, k, P * m:P * m + P],
                                                       xT[:, k, :], start=(m == 0 and k == 0), stop=True,
                                                       skip_group_check=True)
                        ins.then_inc(q_full, 1)
                    if there(u):
                        pe.wait_ge(p_ready, u + 1)
                        at_least(pe, p_done, u)
                        for i in range(2):
                            nc.tensor.transpose(p_bank[:, P * i:P * i + P], prob[:, P * i:P * i + P], c.ident)
                        nc.tensor.transpose(p_bank[0:BT, 2 * P:3 * P], plast[:], c.ident).then_inc(p_full, 1)
                    if there(n):
                        pe.wait_ge(q_done, n + 1)
                        at_least(pe, k_done, n)
                        for m in range(KT):
                            for k in range(KT):
                                nc.tensor.matmul(k_bank[:, P * m:P * m + P], w["cx_k"][:, k, P * m:P * m + P],
                                                 qT[:, k, :], start=(m == 0 and k == 0), stop=True,
                                                 skip_group_check=True)
                        for k in range(KT):
                            ins = nc.tensor.matmul(k_bank[:, D:D + 1], qT[:, k, :], w["cx_bk"][:, k:k + 1],
                                                   start=False, stop=True, skip_group_check=True)
                        ins.then_inc(k_full, 1)
                    if there(u):
                        pe.wait_ge(p_done, u + 1)
                        at_least(pe, a_done, u)
                        for b in range(BT):
                            pe.wait_ge(ctx_loaded[b], 16 * (u + 1))
                            for m in range(KT):
                                for i in range(2):
                                    at = P * m + SQ * b
                                    nc.tensor.matmul(a_bank[:, at:at + SQ], cn[b][:, i, P * m:P * m + P],
                                                     pT[:, i, SQ * b:SQ * b + SQ],
                                                     start=(b == 0 and m == 0 and i == 0), stop=False,
                                                     skip_group_check=True)
                        pe.wait_ge(last_loaded, 16 * (u + 1))
                        for m in range(KT):
                            ins = nc.tensor.matmul(a_bank[:, P * m:P * m + P], last[:, P * m:P * m + P], plT[:],
                                                   start=False, stop=True, skip_group_check=True)
                        ins.then_inc(a_full, 1)
                    if there(n):
                        pe.wait_ge(k_done, n + 1)
                        at_least(pe, e_ready, n)
                        for b in range(BT):
                            pe.wait_ge(ctxT_loaded[b], 16 * (n + 1))
                            for k in range(KT):
                                ins = nc.tensor.matmul(s_bank[SQ * b:SQ * b + SQ, 0:SK], qk[:, k, SQ * b:SQ * b + SQ],
                                                       ctxT[b][:, k, :], start=(k == 0), stop=(k == KT - 1))
                        ins.then_inc(s_full, 1)
                    if there(u):
                        pe.wait_ge(a_done, u + 1)
                        at_least(pe, y_done, u)
                        project_tokens(nc, y_bank, aT, w["cx_v"]).then_inc(y_full, 1)

                slots(pe, step)

            @block.vector
            def _(dve):
                def norm(u):
                    st.link(dve, nc.vector.bn_stats(stat[:], x[:, u, :]))
                    alone(dve, passed_dve)
                    st.link(dve, nc.vector.bn_aggr(mv[:], stat[:]))
                    nc.vector.tensor_scalar(veps[:], mv[:, 1:2], LN_EPS, None, ALU.add).then_inc(var_ready, 1)
                    dve.wait_ge(rstd_ready, u + 1)
                    at_least(dve, xT_full, u)
                    nc.vector.tensor_scalar(xn[:], x[:, u, :], mv[:, 0:1], rstd[:], ALU.subtract, ALU.mult) \
                        .then_inc(xn_ready, 1)

                def step(u):
                    n = u + 1
                    if there(u + 2) and not (isinstance(u, int) and u < 0):
                        norm(u + 2)
                    if there(n):
                        dve.wait_ge(s_full, n + 1)
                        dve.wait_ge(k_done, n + 1)
                        at_least(dve, e_ready, n)
                        st.link(dve, nc.vector.tensor_reduce(mx[:], s_bank[:, 0:SK], AX.X, ALU.max))
                        st.link(dve, nc.vector.tensor_scalar(mx[:], mx[:], SCALE, qb[:], ALU.mult, ALU.add))
                        nc.vector.tensor_tensor(nb[:], qb[:], mx[:], ALU.subtract).then_inc(nb_ready, 1)
                        dve.wait_ge(e_ready, n + 1)
                        at_least(dve, p_full, n)
                        st.link(dve, nc.vector.reciprocal(rden[:], esum[:]))
                        st.link(dve, nc.vector.tensor_scalar(prob[:], raw[:], rden[:], None, ALU.mult))
                        nc.vector.tensor_scalar(plast[:], c.row, prob[:, SK - 1:SK], None, ALU.mult) \
                            .then_inc(p_ready, 1)
                        dve.sem_inc(qb_ready, 1)
                    if there(u):
                        dve.wait_ge(y_full, u + 1)
                        st.link(dve, nc.vector.tensor_tensor(y[:], y_bank[:, 0:D], w["cx_bv"][:], ALU.add))
                        nc.vector.tensor_tensor(x[:, u, :], x[:, u, :], y[:], ALU.add).then_inc(y_done, 1)

                dve.wait_ge(loaded["cross"], 16 * len(GROUPS["cross"]))
                norm(0)
                norm(1)
                slots(dve, step, steps=st, per=2 + 4 + 1)


def segment_attention(nc, a, sb_, sem, bank, c, x, w, loaded):
    with ExitStack() as own:
        def sb(name, shape, dt=F32):
            return sb_("sg_" + name, shape, dt, own)

        def gsem(name):
            return sem("sg_" + name)

        kinds = ("lt", "st")
        xn, xT = sb("xn", [P, D]), sb("xT", [P, KT, P])
        stat, mv, veps, rstd = sb("stat", [P, 6]), sb("mv", [P, 2]), sb("veps", [P, 1]), sb("rstd", [P, 1])
        qT, kT = sb("qT", [P, KT, P]), sb("kT", [P, KT, P])
        v, vbd, qbd = sb("v", [P, D]), sb("vbd", [P, NG, BT, 64]), sb("qbd", [P, KT, BT, 4, SQ])
        score, prob = sb("score", [P, NG, BT, SQ]), sb("prob", [P, NG, BT, SQ])
        mx, esum, rden = sb("mx", [P, 16]), sb("esum", [P, 16]), sb("rden", [P, 16])
        rmask, om = sb("rmask", [P, NG, BT, 4]), sb("om", [P, BT, NG, 64])
        pT, oT = sb("pT", [P, NG, P]), sb("oT", [P, KT, P])
        longT, shortT, short, y = sb("longT", [P, KT, P]), sb("shortT", [P, KT, P]), sb("short", [P, D]), sb("y", [P, D])
        lmax, first, chosen = sb("lmax", [P, 1]), sb("first", [P, NE]), sb("chosen", [P, 1])
        onehot, hotT, hot_rep = sb("onehot", [P, NE]), sb("hotT", [NE, P]), sb("hot_rep", [NE, BT, 4, SQ])
        same, shut, mates = sb("same", [P, P]), sb("shut", [P, P]), sb("mates", [P, BT, SQ])
        count, single, several = sb("count", [P, 1]), sb("single", [P, 1]), sb("several", [P, 1])
        x_single = sb("x_single", [P, D])
        b_qk, s_bank, v_bank, p_bank, o_bank, m_bank = bank[0], bank[1:3], bank[3], bank[4], bank[5:7], bank[7]

        st = Steps(gsem("dve_steps"))
        passed_dve, passed_pool = gsem("passed_dve"), gsem("passed_pool")
        var_ready, rstd_ready, xn_ready = gsem("var_ready"), gsem("rstd_ready"), gsem("xn_ready")
        m_full, m_done = gsem("m_full"), gsem("m_done")
        qk_full, qk_done, v_full, v_done = gsem("qk_full"), gsem("qk_done"), gsem("v_full"), gsem("v_done")
        qbd_ready, vbd_ready, hot_ready = gsem("qbd_ready"), gsem("vbd_ready"), gsem("hot_ready")
        s_full, s_done, sub_ready, p_ready = gsem("s_full"), gsem("s_done"), gsem("sub_ready"), gsem("p_ready")
        pT_full, pT_done, o_full, o_done = gsem("pT_full"), gsem("pT_done"), gsem("o_full"), gsem("o_done")
        short_ready, x_done = gsem("short_ready"), gsem("x_done")

        order = []
        for t in range(NT + 1):
            for s in range(2):
                if t < NT:
                    order += [("xT", t, s), ("logits", t, s)] if s == 0 else []
                if s == 1 and t > 0:
                    order += [("shortT", t, s), ("fused", t, s)]
                if t < NT:
                    order += [("hot", t, s)] if s == 0 else [("same", t, s)]
                if (s == 1 and t < NT) or (s == 0 and t > 0):
                    order += [("oT", t, s), ("out", t, s)]
        misc = Uses(order)

        def tiles(eng, step, steps=None, per=None):
            for s in range(2):
                step(0, s)
            with eng.Fori(1, NT - 1) as t:
                if steps:
                    steps.enter(t, 1, per)
                for s in range(2):
                    step(t, s)
                if steps:
                    steps.leave(NT - 2)
            for t in (NT - 1, NT):
                for s in range(2):
                    step(t, s)

        def front(t):
            return there(t)

        def back(t, s):
            return there(t) if s == 1 else there(t - 1)

        with nc.Block() as block:
            @block.gpsimd
            def _(pool):
                def root(t):
                    pool.wait_ge(var_ready, t + 1)
                    nc.gpsimd.tensor_tensor(rstd[:], veps[:], c.half[:, 0:1], ALU.pow).then_inc(rstd_ready, 1)

                def step(t, s):
                    n = 2 * t + s
                    if front(t):
                        pool.wait_ge(qk_done, n + 1)
                        at_least(pool, s_full, n)
                        alone(pool, passed_pool)
                        spread_heads(nc.gpsimd, qbd, qT, c.quarter).then_inc(qbd_ready, 1)
                        pool.wait_ge(v_done, n + 1)
                        at_least(pool, o_full, n)
                        alone(pool, passed_pool)
                        spread_batches(nc.gpsimd, vbd, v, c).then_inc(vbd_ready, 1)
                    if s == 1 and there(t) and there(t + 1):
                        root(t + 1)

                root(0)
                tiles(pool, step)

            @block.scalar
            def _(act):
                act.wait_ge(loaded["segs"], 16 * len(GROUPS["segs"]))

                def step(t, s):
                    n = 2 * t + s
                    if s == 0 and front(t):
                        act.wait_ge(m_full, misc.filled("xT", t, 0))
                        nc.scalar.copy(xT[:], m_bank[:, 0:D].rearrange("p (k t) -> p k t", k=KT)).then_inc(m_done, 1)
                    if front(t):
                        bias = w[kinds[s] + "_bqk"]
                        act.wait_ge(qk_full, n + 1)
                        at_least(act, qbd_ready, n)
                        at_least(act, s_full, n)
                        for m in range(KT):
                            nc.scalar.activation(qT[:, m, :], b_qk[:, P * m:P * m + P], ACT.Identity,
                                                 bias=bias[:, m:m + 1])
                            at = P * (KT + m)
                            ins = nc.scalar.activation(kT[:, m, :], b_qk[:, at:at + P], ACT.Identity,
                                                       bias=bias[:, KT + m:KT + m + 1])
                        ins.then_inc(qk_done, 1)
                    if s == 1 and there(t - 1):
                        act.wait_ge(m_full, misc.filled("shortT", t, 1))
                        nc.scalar.copy(shortT[:], m_bank[:, 0:D].rearrange("p (k t) -> p k t", k=KT)) \
                            .then_inc(m_done, 1)
                    if back(t, s):
                        act.wait_ge(pT_full, n)
                        nc.scalar.copy(pT[:], p_bank[:].rearrange("p (g t) -> p g t", g=NG)).then_inc(pT_done, 1)
                    if s == 0 and front(t):
                        act.wait_ge(m_full, misc.filled("hot", t, 0))
                        src = m_bank[0:NE, 0:P]
                        nc.scalar.copy(hotT[:], src)
                        nc.scalar.copy(hot_rep[:], src.rearrange("e (b q) -> e b q", b=BT).unsqueeze(2)
                                       .broadcast_to([NE, BT, 4, SQ])).then_inc(m_done, 1)
                    if back(t, s):
                        act.wait_ge(m_full, misc.filled("oT", t, s))
                        nc.scalar.copy(oT[:], m_bank[:, 0:D].rearrange("p (k t) -> p k t", k=KT)).then_inc(m_done, 1)
                        if s == 1:
                            act.wait_ge(m_full, misc.filled("out", t, s))
                            for m in range(KT):
                                ins = nc.scalar.activation(longT[:, m, :], m_bank[:, P * m:P * m + P], ACT.Identity,
                                                           bias=w["lt_bo"][:, m:m + 1])
                            ins.then_inc(m_done, 1)
                    if front(t):
                        act.wait_ge(sub_ready, n + 1)
                        at_least(act, pT_full, n)
                        nc.scalar.activation(prob[:], score[:], ACT.Exp).then_inc(p_ready, 1)

                tiles(act, step)

            @block.tensor
            def _(pe):
                pe.wait_ge(loaded["segs"], 16 * len(GROUPS["segs"]))

                def free(kind, t, s):
                    at_least(pe, m_done, misc.filled(kind, t, s) - 1)

                def step(t, s):
                    n = 2 * t + s
                    if front(t):
                        weight = w[kinds[s] + "_qkv"]
                        if s == 0:
                            pe.wait_ge(xn_ready, t + 1)
                            free("xT", t, 0)
                            turn_tokens(nc, m_bank, xn, c).then_inc(m_full, 1)
                            pe.wait_ge(m_done, misc.filled("xT", t, 0))
                        at_least(pe, qk_done, n)
                        project_qk(nc, b_qk, weight, xT).then_inc(qk_full, 1)
                        at_least(pe, v_done, n)
                        project_tokens(nc, v_bank, xT, weight[:, :, 2 * D:3 * D]).then_inc(v_full, 1)
                        if s == 0:
                            free("logits", t, 0)
                            for k in range(KT):
                                ins = nc.tensor.matmul(m_bank[:, 0:NE], xT[:, k, :], w["protos"][:, k, :],
                                                       start=(k == 0), stop=(k == KT - 1))
                            ins.then_inc(m_full, 1)
                    if s == 1 and there(t - 1):
                        pe.wait_ge(short_ready, t)
                        free("shortT", t, 1)
                        turn_tokens(nc, m_bank, short, c).then_inc(m_full, 1)
                    if back(t, s):
                        pe.wait_ge(p_ready, n)
                        at_least(pe, pT_done, n - 1)
                        turn_probabilities(nc, p_bank, prob, c).then_inc(pT_full, 1)
                    if s == 1 and there(t - 1):
                        free("fused", t, 1)
                        for k in range(2 * KT):
                            lhs = (longT if k < KT else shortT)[:, k % KT, :]
                            ins = nc.tensor.matmul(m_bank[:, 0:D], lhs, w["fus"][:, k, :],
                                                   start=(k == 0), stop=(k == 2 * KT - 1))
                        ins.then_inc(m_full, 1)
                    if back(t, s):
                        pe.wait_ge(pT_done, n)
                        pe.wait_ge(vbd_ready, n)
                        at_least(pe, o_done, n - 1)
                        weigh_values(nc, o_bank, pT, vbd).then_inc(o_full, 1)
                    if s == 0 and front(t):
                        pe.wait_ge(hot_ready, t + 1)
                        free("hot", t, 0)
                        nc.tensor.transpose(m_bank[0:NE, 0:P], onehot[:], c.ident).then_inc(m_full, 1)
                    if s == 1 and front(t):
                        free("same", t, 1)
                        for b in range(BT):
                            nc.tensor.matmul(m_bank[:, SQ * b:SQ * b + SQ],
                                             hot_rep[:, b, :, :].rearrange("e h q -> e (h q)"),
                                             hotT[:, SQ * b:SQ * b + SQ], start=(b == 0), stop=True,
                                             skip_group_check=True)
                        nc.tensor.matmul(m_bank[:, P:2 * P], hotT[:], hotT[:], start=False, stop=True,
                                         skip_group_check=True).then_inc(m_full, 1)
                    if front(t):
                        pe.wait_ge(qbd_ready, n + 1)
                        at_least(pe, s_done, n)
                        for f in range(2):
                            ins = score_heads(nc, s_bank[f], qbd, kT, f, True)
                        ins.then_inc(s_full, 1)
                    if back(t, s):
                        pe.wait_ge(o_done, n)
                        free("oT", t, s)
                        heads_to_features(nc, m_bank, om, c).then_inc(m_full, 1)
                        free("out", t, s)
                        if s == 1:
                            for m in range(KT):
                                for k in range(KT):
                                    ins = nc.tensor.matmul(m_bank[:, P * m:P * m + P],
                                                           w["lt_o"][:, k, P * m:P * m + P], oT[:, k, :],
                                                           start=(m == 0 and k == 0), stop=True, skip_group_check=True)
                            ins.then_inc(m_full, 1)
                        else:
                            project_tokens(nc, m_bank, oT, w["st_o"]).then_inc(m_full, 1)

                tiles(pe, step)

            @block.vector
            def _(dve):
                def norm(t):
                    st.link(dve, nc.vector.bn_stats(stat[:], x[:, t, :]))
                    alone(dve, passed_dve)
                    st.link(dve, nc.vector.bn_aggr(mv[:], stat[:]))
                    nc.vector.tensor_scalar(veps[:], mv[:, 1:2], LN_EPS, None, ALU.add).then_inc(var_ready, 1)
                    dve.wait_ge(rstd_ready, t + 1)
                    nc.vector.tensor_scalar(xn[:], x[:, t, :], mv[:, 0:1], rstd[:], ALU.subtract, ALU.mult) \
                        .then_inc(xn_ready, 1)

                flat = [P, 16, SQ]
                flatten = "p g b k -> p (g b) k"

                def step(t, s):
                    n = 2 * t + s
                    if front(t):
                        dve.wait_ge(v_full, n + 1)
                        at_least(dve, vbd_ready, n)
                        nc.vector.tensor_tensor(v[:], v_bank[:, 0:D], w[kinds[s] + "_bv"][:], ALU.add) \
                            .then_inc(v_done, 1)
                    if s == 0 and front(t):
                        dve.wait_ge(m_full, misc.filled("logits", t, 0))
                        st.link(dve, nc.vector.tensor_reduce(lmax[:], m_bank[:, 0:NE], AX.X, ALU.max))
                        st.link(dve, nc.vector.tensor_scalar(first[:], m_bank[:, 0:NE], lmax[:], None, ALU.is_ge))
                        nc.vector.tensor_tensor(first[:], first[:], c.exp8, ALU.mult).then_inc(m_done, 1)
                        dve.wait_ge(m_done, misc.filled("logits", t, 0))
                        st.link(dve, nc.vector.tensor_reduce(chosen[:], first[:], AX.X, ALU.min))
                        nc.vector.tensor_scalar(onehot[:], c.exp8, chosen[:], None, ALU.is_equal).then_inc(hot_ready, 1)
                    if s == 1 and there(t - 1):
                        dve.wait_ge(m_full, misc.filled("fused", t, 1))
                        nc.vector.tensor_tensor(y[:], m_bank[:, 0:D], w["fus_b"][:], ALU.add).then_inc(m_done, 1)
                        dve.wait_ge(m_done, misc.filled("fused", t, 1))
                        nc.vector.tensor_tensor(x[:, t - 1, :], x[:, t - 1, :], y[:], ALU.add).then_inc(x_done, 1)
                    if back(t, s):
                        dve.wait_ge(p_ready, n)
                        st.link(dve, nc.vector.tensor_reduce(esum[:], prob[:].rearrange(flatten), AX.X, ALU.add))
                        st.link(dve, nc.vector.reciprocal(rden[:], esum[:]))
                        st.link(dve, nc.vector.tensor_tensor(
                            rmask[:].rearrange("p g b h -> p (g b) h"), rden[:].unsqueeze(2).broadcast_to([P, 16, 4]),
                            c.row.unsqueeze(1).broadcast_to([P, 16, 4]), ALU.mult))
                        dve.wait_ge(o_full, n)
                        own_heads(nc, om, o_bank, rmask).then_inc(o_done, 1)
                    if s == 1 and front(t):
                        dve.wait_ge(m_full, misc.filled("same", t, 1))
                        st.link(dve, nc.vector.tensor_copy(same[:], m_bank[:, 0:P]))
                        st.link(dve, nc.vector.tensor_scalar(shut[:], same[:], 1.0, 1e9, ALU.subtract, ALU.mult))
                        nc.vector.tensor_tensor(mates[:], m_bank[:, P:2 * P].rearrange("p (b k) -> p b k", b=BT),
                                                c.row.unsqueeze(2).broadcast_to([P, BT, SQ]), ALU.mult) \
                            .then_inc(m_done, 1)
                        dve.wait_ge(m_done, misc.filled("same", t, 1))
                        st.link(dve, nc.vector.tensor_reduce(count[:], mates[:], AX.XY, ALU.add))
                        st.link(dve, nc.vector.tensor_scalar(single[:], count[:], 1.0, None, ALU.is_equal))
                        st.link(dve, nc.vector.tensor_scalar(several[:], single[:], -1.0, 1.0, ALU.mult, ALU.add))
                        st.link(dve, nc.vector.tensor_scalar(x_single[:], xn[:], single[:], None, ALU.mult))
                    if front(t):
                        dve.wait_ge(s_full, n + 1)
                        at_least(dve, p_ready, n)
                        if s == 1:
                            for f in range(2):
                                ins = nc.vector.tensor_tensor(
                                    halves(score, f), s_bank[f][:, 0:D].rearrange("p (m t) -> p m t", m=KT),
                                    same[:].unsqueeze(1).broadcast_to([P, KT, P]), ALU.mult)
                            ins.then_inc(s_done, 1)
                            dve.wait_ge(s_done, n + 1)
                            group = "p g b k -> p g (b k)"
                            st.link(dve, nc.vector.tensor_tensor(
                                score[:].rearrange(group), score[:].rearrange(group),
                                shut[:].unsqueeze(1).broadcast_to([P, NG, P]), ALU.add))
                            st.link(dve, nc.vector.tensor_reduce(mx[:], score[:].rearrange(flatten), AX.X, ALU.max))
                            nc.vector.tensor_tensor(score[:].rearrange(flatten), score[:].rearrange(flatten),
                                                    mx[:].unsqueeze(2).broadcast_to(flat), ALU.subtract) \
                                .then_inc(sub_ready, 1)
                        else:
                            for f in range(2):
                                ins = nc.vector.tensor_reduce(
                                    mx[:, 8 * f:8 * f + 8], s_bank[f][:, 0:D].rearrange("p (n k) -> p n k", k=SQ),
                                    AX.X, ALU.max)
                            st.link(dve, ins)
                            for f in range(2):
                                ins = nc.vector.tensor_tensor(
                                    score[:].rearrange("p (m f) b k -> p f m b k", f=2)[:, f],
                                    s_bank[f][:, 0:D].rearrange("p (m b k) -> p m b k", m=KT, b=BT),
                                    mx[:, 8 * f:8 * f + 8].rearrange("p (m b) -> p m b", m=KT).unsqueeze(3)
                                    .broadcast_to([P, KT, BT, SQ]), ALU.subtract)
                                if f == 0:
                                    st.done(ins)
                            ins.then_inc(s_done, 1)
                            dve.wait_ge(s_done, n + 1)
                            dve.sem_inc(sub_ready, 1)
                    if back(t, s) and s == 0:
                        dve.wait_ge(m_full, misc.filled("out", t, 0))
                        nc.vector.tensor_tensor(short[:], m_bank[:, 0:D], w["st_bo"][:], ALU.add).then_inc(m_done, 1)
                        dve.wait_ge(m_done, misc.filled("out", t, 0))
                        nc.vector.scalar_tensor_tensor(short[:], short[:], several[:], x_single[:], ALU.mult, ALU.add) \
                            .then_inc(short_ready, 1)
                    if s == 1 and there(t) and there(t + 1):
                        norm(t + 1)

                dve.wait_ge(loaded["segs"], 16 * len(GROUPS["segs"]))
                norm(0)
                tiles(dve, step, steps=st, per=(3 + 3 + 2) + (3 + 6 + 2) + 2)


def experts(nc, a, sb_, sem, bank, c, x, w, loaded):
    with ExitStack() as own:
        def sb(name, shape, dt=F32):
            return sb_("ex_" + name, shape, dt, own)

        def esem(name):
            return sem("ex_" + name)

        T = NT * P
        NC = len(FCH)
        w1 = [sb(f"w1_{i}", [P, KT, 2 * FE]) for i in range(2)]
        w2 = [sb(f"w2_{i}", [P, NC, D]) for i in range(2)]
        stats, mv = sb("stats", [P, NT, 6]), sb("mv", [P, NT, 2])
        veps, rstd = sb("veps", [P, NT]), sb("rstd", [P, NT])
        xn, xT = sb("xn", [P, NT, D]), sb("xT", [P, KT, T])
        logit, raw, prob = sb("logit", [P, NT, NE]), sb("raw", [P, NT, NE]), sb("prob", [P, NT, NE])
        rest, tie, hot = sb("rest", [P, NT, NE]), sb("tie", [P, NT, NE]), [sb(f"hot{i}", [P, NT, NE]) for i in range(2)]
        most, which = sb("most", [P, NT]), sb("which", [P, NT])
        route = sb("route", [P, NE * NT])
        silu = [sb(f"silu{i}", [P, 512]) for i in range(2)]
        g = [sb(f"g{i}", [P, NC, T]) for i in range(2)]
        y_bank, o_bank = bank[0:4], bank[4:8]

        st = Steps(esem("dve_steps"))
        w1_loaded, w2_loaded = [esem("w1_loaded0"), esem("w1_loaded1")], [esem("w2_loaded0"), esem("w2_loaded1")]
        veps_ready, rstd_ready, xn_ready = esem("veps_ready"), esem("rstd_ready"), esem("xn_ready")
        xT_full, xT_done, l_full, l_done = esem("xT_full"), esem("xT_done"), esem("l_full"), esem("l_done")
        sub_ready, e_ready, passed_sp = esem("sub_ready"), esem("e_ready"), esem("passed_sp")
        up_full, silu_ready, g_ready = esem("up_full"), esem("silu_ready"), esem("g_ready")
        o_full, o_done = esem("o_full"), esem("o_done")
        PIECES = 2 * NC

        def schedule(up, down, eng, steps=None, per=None):
            up(0, 0, 1)
            up(1, 1, 1)
            down(0, 0, 1)
            up(2, 0, 2)
            down(1, 1, 1)
            with eng.Fori(1, NE // 2 - 1) as j:
                if steps:
                    steps.enter(j, 1, per)
                up(2 * j + 1, 1, j + 1)
                down(2 * j, 0, j + 1)
                up(2 * j + 2, 0, j + 2)
                down(2 * j + 1, 1, j + 1)
                if steps:
                    steps.leave(NE // 2 - 2)
            up(NE - 1, 1, NE // 2)
            down(NE - 2, 0, NE // 2)
            down(NE - 1, 1, NE // 2)

        with nc.Block() as block:
            @block.sync
            def _(sp):
                def weights(e, i):
                    sp.dma_start(w1[i][:], a["w1"][e]).then_inc(w1_loaded[i], 16)
                    sp.dma_start(w2[i][:, 0:2, :], a["w2"][e, 0:2 * P, :].rearrange("(c p) d -> p c d", p=P)) \
                        .then_inc(w2_loaded[i], 16)
                    sp.dma_start(w2[i][0:FE - 2 * P, 2, :], a["w2"][e, 2 * P:FE, :]).then_inc(w2_loaded[i], 16)

                weights(0, 0)
                weights(1, 1)
                with sp.Fori(1, NE // 2) as j:
                    for i in range(2):
                        sp.wait_ge(o_full, NT * (2 * j - 1 + i))
                        alone(sp, passed_sp)
                        weights(2 * j + i, i)

            @block.gpsimd
            def _(pool):
                pool.wait_ge(veps_ready, 1)
                nc.gpsimd.tensor_tensor(rstd[:], veps[:], c.half[:, 0:NT], ALU.pow).then_inc(rstd_ready, 1)

            @block.scalar
            def _(act):
                for i in range(NT // 2):
                    act.wait_ge(xT_full, i + 1)
                    src = bank[i % 2][:].rearrange("p (j k t) -> p j k t", j=2, k=KT)
                    for j in range(2):
                        at = P * (2 * i + j)
                        ins = nc.scalar.copy(xT[:, :, at:at + P], src[:, j, :, :])
                    ins.then_inc(xT_done, 1)
                act.wait_ge(sub_ready, 1)
                nc.scalar.activation(raw[:], logit[:], ACT.Exp).then_inc(e_ready, 1)

                def up(e, i, r):
                    for n in range(PIECES):
                        rows = FCH[n % NC][1]
                        act.wait_ge(up_full, PIECES * e + n + 1)
                        at_least(act, g_ready, PIECES * e + n - 1)
                        nc.scalar.activation(silu[n % 2][0:rows, :], y_bank[2 * (n % 2)][0:rows, :], ACT.Silu) \
                            .then_inc(silu_ready, 1)

                schedule(up, lambda e, i, r: None, act)

            @block.tensor
            def _(pe):
                pe.wait_ge(loaded["router"], 16)
                for i in range(NT // 2):
                    pe.wait_ge(xn_ready, i + 1)
                    at_least(pe, xT_done, i - 1)
                    for j in range(2):
                        ins = turn_tokens(nc, bank[i % 2][:, D * j:D * j + D], xn[:, 2 * i + j, :], c)
                    ins.then_inc(xT_full, 1)
                pe.wait_ge(xT_done, NT // 2)
                for t in range(NT):
                    for k in range(KT):
                        ins = nc.tensor.matmul(o_bank[3][:, NE * t:NE * t + NE], xT[:, k, P * t:P * t + P],
                                               w["router"][:, k, :], start=(t == 0 and k == 0), stop=True,
                                               skip_group_check=True)
                ins.then_inc(l_full, 1)

                def up(e, i, r):
                    pe.wait_ge(w1_loaded[i], 16 * r)
                    for n in range(PIECES):
                        h, ch = n // NC, n % NC
                        lo, rows = FCH[ch]
                        at_least(pe, g_ready, PIECES * e + n - 1)
                        for part in range(2):
                            for k in range(KT):
                                at = FE * part + lo
                                ins = nc.tensor.matmul(y_bank[2 * (n % 2) + part][0:rows, :], w1[i][:, k, at:at + rows],
                                                       xT[:, k, 512 * h:512 * h + 512], start=(k == 0),
                                                       stop=(k == KT - 1))
                        ins.then_inc(up_full, 1)

                def down(e, i, r):
                    pe.wait_ge(w2_loaded[i], 32 * r)
                    for t in range(NT):
                        if t % (NT // 2) == 0:
                            pe.wait_ge(g_ready, PIECES * e + NC * (2 * t // NT + 1))
                        at_least(pe, o_done, NT * e + t - 3)
                        for ch, (lo, rows) in enumerate(FCH):
                            ins = nc.tensor.matmul(o_bank[t % 4][:, 0:D], g[i][0:rows, ch, P * t:P * t + P],
                                                   w2[i][0:rows, ch, :], start=(ch == 0), stop=(ch == NC - 1))
                        ins.then_inc(o_full, 1)

                def first_down(e, i, r):
                    if isinstance(e, int) and e == 0:
                        pe.wait_ge(l_done, 1)
                    down(e, i, r)

                schedule(up, first_down, pe)

            @block.vector
            def _(dve):
                for t in range(NT):
                    ins = nc.vector.bn_stats(stats[:, t, :], x[:, t, :])
                st.link(dve, ins)
                for t in range(NT):
                    ins = nc.vector.bn_aggr(mv[:, t, :], stats[:, t, :])
                st.link(dve, ins)
                nc.vector.tensor_scalar(veps[:], mv[:, :, 1], LN_EPS, None, ALU.add).then_inc(veps_ready, 1)
                dve.wait_ge(rstd_ready, 1)
                for t in range(NT):
                    ins = nc.vector.tensor_scalar(xn[:, t, :], x[:, t, :], mv[:, t, 0:1], rstd[:, t:t + 1],
                                                  ALU.subtract, ALU.mult)
                    if t % 2:
                        ins.then_inc(xn_ready, 1)

                each = [P, NT, NE]
                dve.wait_ge(l_full, 1)
                nc.vector.tensor_copy(logit[:], o_bank[3][:, 0:NT * NE].rearrange("p (t e) -> p t e", t=NT)) \
                    .then_inc(l_done, 1)
                dve.wait_ge(l_done, 1)

                def over(v):
                    return v[:].unsqueeze(2).broadcast_to(each)

                st.link(dve, nc.vector.tensor_reduce(most[:], logit[:], AX.X, ALU.max))
                nc.vector.tensor_tensor(logit[:], logit[:], over(most), ALU.subtract).then_inc(sub_ready, 1)
                dve.wait_ge(e_ready, 1)
                st.link(dve, nc.vector.tensor_reduce(most[:], raw[:], AX.X, ALU.add))
                st.link(dve, nc.vector.reciprocal(which[:], most[:]))
                st.link(dve, nc.vector.tensor_tensor(prob[:], raw[:], over(which), ALU.mult))
                number = c.exp8.unsqueeze(1).broadcast_to(each)
                for k in range(2):
                    of = (prob, rest)[k]
                    st.link(dve, nc.vector.tensor_reduce(most[:], of[:], AX.X, ALU.max))
                    st.link(dve, nc.vector.tensor_tensor(tie[:], of[:], over(most), ALU.is_ge))
                    st.link(dve, nc.vector.tensor_tensor(tie[:], tie[:], number, ALU.mult))
                    st.link(dve, nc.vector.tensor_reduce(which[:], tie[:], AX.X, ALU.min))
                    st.link(dve, nc.vector.tensor_tensor(hot[k][:], number, over(which), ALU.is_equal))
                    if k == 0:
                        st.link(dve, nc.vector.scalar_tensor_tensor(rest[:], hot[0][:], -2.0, prob[:], ALU.mult, ALU.add))
                st.link(dve, nc.vector.tensor_tensor(hot[0][:], hot[0][:], hot[1][:], ALU.add))
                st.link(dve, nc.vector.tensor_tensor(route[:].rearrange("p (e t) -> p t e", e=NE), prob[:], hot[0][:],
                                                     ALU.mult))

                def up(e, i, r):
                    for n in range(PIECES):
                        h, ch = n // NC, n % NC
                        rows = FCH[ch][1]
                        dve.wait_ge(silu_ready, PIECES * e + n + 1)
                        nc.vector.tensor_tensor(g[i][0:rows, ch, 512 * h:512 * h + 512],
                                                y_bank[2 * (n % 2) + 1][0:rows, :], silu[n % 2][0:rows, :], ALU.mult) \
                            .then_inc(g_ready, 1)

                def down(e, i, r):
                    for t in range(NT):
                        dve.wait_ge(o_full, NT * e + t + 1)
                        at_least(dve, o_done, NT * (e - 1) + t + 1)
                        if isinstance(e, int):
                            p_route = route[:, NT * e + t:NT * e + t + 1]
                        else:
                            p_route = route[:, bass.ds(e * NT + t, 1)]
                        nc.vector.scalar_tensor_tensor(x[:, t, :], o_bank[t % 4][:, 0:D], p_route, x[:, t, :],
                                                       ALU.mult, ALU.add).then_inc(o_done, 1)

                schedule(up, down, dve)


def _blocks(weight):
    wt = np.asarray(weight).T
    return np.ascontiguousarray(wt.reshape(wt.shape[0] // P, P, wt.shape[1]).transpose(1, 0, 2))


def _plain(weight):
    wt = np.asarray(weight)
    return np.ascontiguousarray(wt.reshape(wt.shape[0] // P, P, wt.shape[1]).transpose(1, 0, 2))


def _column(vector):
    return np.ascontiguousarray(np.asarray(vector).reshape(-1, P).T)


def _constants():
    cst = np.zeros((P, C_END), np.float32)
    p = np.arange(P)[:, None]
    cst[:, C_ID:C_ID + P] = np.eye(P)
    cst[:, C_HEADQ:C_HEADQ + P] = (p % 64) // DH == np.arange(P)[None] // SQ
    cst[:, C_HEAD:C_HEAD + 4] = (p % 64) // DH == np.arange(4)[None]
    cst[:, C_QUARTER:C_QUARTER + 4] = cst[:, C_HEAD:C_HEAD + 4] * DH ** -0.5
    cst[:, C_ROW:C_ROW + 4] = p // SQ == np.arange(4)[None]
    cst[:, C_EQ:C_EQ + SQ] = p % SQ == np.arange(SQ)[None]
    cst[:, C_CAUSAL:C_CAUSAL + SQ] = np.where(np.arange(SQ)[None] > p % SQ, -1e9, 0.0)
    ratio = 2.0 ** (-8.0 / NH)
    cst[:, C_SLOPE:C_SLOPE + NG] = [[ratio ** (4 * g + q // SQ + 1) for g in range(NG)] for q in range(P)]
    cst[:, C_EXP8:C_EXP8 + 8] = np.arange(8)[None] - 8.0
    cst[0:16, C_LAST:C_LAST + 16] = np.eye(16)
    cst[:, C_HALF:C_HALF + 16] = -0.5
    cst[:, C_ONES:C_ONES + SQ] = 1.0
    return cst


def kernel(**inputs):
    import concourse.bacc as bacc
    from concourse.bass_utils import run_bass_kernel_spmd as run

    i = {k: np.asarray(v) for k, v in inputs.items()}
    ctx = i["ctx_1024"]
    host = {
        "cst": _constants(),
        "x": i["x"].reshape(NT, P, D).transpose(1, 0, 2),
        "ctx_T": ctx.transpose(0, 2, 1).reshape(NB, KT, P, SK).transpose(0, 2, 1, 3),
        "ctx": ctx,
        "ctx_rows": ctx[:, SK - 1, :].reshape(NT, BT, D),
        "ctx_last_T": ctx[:, SK - 1, :].T.reshape(KT, P, NB).transpose(1, 0, 2),
        "qpos_T": i["itok_BxS_8_8191"].T,
        "kpos": i["itok_BxS2_1_8191"],
        "mask": i["mask_BxSxS2_if1"],
        "xa_q": _blocks(i["L0_xattn_W_q"]), "xa_k": _blocks(i["L0_xattn_W_k"]),
        "xa_v": _blocks(i["L0_xattn_W_v"]), "xa_o": _blocks(i["L0_xattn_W_o"]),
        "ra_qkv": _plain(i["L0_attn_w_qkv"]), "ra_o": _plain(i["L0_attn_w_out"]),
        "ra_bqk": _column(i["L0_attn_b_qkv"][:2 * D]), "ra_bv": i["L0_attn_b_qkv"][2 * D:],
        "ra_bo": i["L0_attn_b_out"],
        "w_gate": i["L0_ffn_w_gate"].reshape(FT, P, D).transpose(1, 0, 2).reshape(P, -1, QB),
        "w_up": i["L0_ffn_w_up"].reshape(FT, P, D).transpose(1, 0, 2).reshape(P, -1, QB),
        "w_down": i["L0_ffn_w_down"].reshape(KT, P, FF).transpose(1, 0, 2).reshape(P, -1, QB),
        "cx_q": _blocks(i["L1_xattn_Wq"]), "cx_k": _plain(i["L1_xattn_Wk"]), "cx_v": _blocks(i["L1_xattn_Wv"]),
        "cx_bq": _column(i["L1_xattn_bq"]), "cx_bk": _column(i["L1_xattn_bk"]), "cx_bv": i["L1_xattn_bv"],
        "lt_qkv": _blocks(i["L1_attn_lt_w_in"]), "lt_o": _blocks(i["L1_attn_lt_w_out"]),
        "lt_bqk": _column(i["L1_attn_lt_b_in"][:2 * D]), "lt_bv": i["L1_attn_lt_b_in"][2 * D:],
        "lt_bo": _column(i["L1_attn_lt_b_out"]),
        "st_qkv": _blocks(i["L1_attn_st_w_in"]), "st_o": _blocks(i["L1_attn_st_w_out"]),
        "st_bqk": _column(i["L1_attn_st_b_in"][:2 * D]), "st_bv": i["L1_attn_st_b_in"][2 * D:],
        "st_bo": i["L1_attn_st_b_out"],
        "protos": _blocks(i["L1_attn_protos"]), "fus": _blocks(i["L1_attn_fus_w"]), "fus_b": i["L1_attn_fus_b"],
        "router": _plain(i["L1_ffn_router_weight"]),
        "w1": i["L1_ffn_w1"].reshape(NE, KT, P, 2 * FE).transpose(0, 2, 1, 3),
        "w2": i["L1_ffn_w2"],
    }
    nc = bacc.Bacc("TRN2", target_bir_lowering=False, num_devices=1)
    given, views = {}, {}
    for name, array in host.items():
        array = np.ascontiguousarray(array)
        given["in_" + name] = array
        view = nc.dram_tensor("in_" + name, array.shape, mybir.dt.from_np(array.dtype), kind="ExternalInput").ap()
        if array.ndim == 1:
            view = view.unsqueeze(0).broadcast_to([P, array.shape[0]])
        views[name] = view
    out = nc.dram_tensor("out", (P, NT, D), F32, kind="ExternalOutput").ap()
    build(nc, views, out)
    got = run(nc, [given], core_ids=[0]).results[0]["out"]
    return np.ascontiguousarray(np.asarray(got).transpose(1, 0, 2)).reshape(NB, SQ, D)
```

```python
from contextlib import ExitStack

import numpy as np
import concourse.bass as bass
from concourse import mybir

F32 = mybir.dt.float32
I32 = mybir.dt.int32
ALU = mybir.AluOpType
ACT = mybir.ActivationFunctionType
AX = mybir.AxisListType
RMAX = bass.bass_isa.ReduceOp.max

NB, SQ, D, SK = 32, 32, 256, 257
NH, DH = 16, 16
P = 128
NT = NB * SQ // P
BT = P // SQ
KT = D // P
NG = NH // 4
FF = 768
FT = FF // P
QB = 32
NE, FE = 8, 352
FCH = [(0, 128), (128, 128), (256, 96)]
ROUND = 1.5 * 2.0 ** 23
BIG = 3e38
LN_EPS = 1e-5

C_ID, C_HEADQ, C_HEAD, C_ROW, C_EQ, C_CAUSAL, C_SLOPE, C_EXP8, C_LAST, C_HALF, C_ONES, C_QUARTER = (
    0, 128, 256, 260, 264, 296, 328, 332, 340, 356, 372, 404)
C_END = 408


NBLK = 3 * KT * FF // QB


def at_least(eng, sem, value):
    if isinstance(value, int) and value <= 0:
        return
    eng.wait_ge(sem, value)


def alone(eng, sem):
    eng.sem_inc(sem, 1)


class Steps:

    def __init__(self, sem):
        self.sem, self.base, self.n = sem, 0, 0

    def enter(self, i, first, per):
        self.start, self.per, self.first = self.base + self.n, per, first
        self.base, self.n = self.start + (i - first) * per, 0

    def leave(self, count):
        assert self.n == self.per, (self.n, self.per)
        self.base, self.n = self.start + count * self.per, 0

    def done(self, ins):
        ins.then_inc(self.sem, 1)
        self.n += 1
        return self.base + self.n

    def now(self):
        return self.base + self.n

    def link(self, eng, ins):
        eng.wait_ge(self.sem, self.done(ins))



class Uses:

    def __init__(self, order):
        self.index, self.first = {}, {}
        for n, (kind, t, b) in enumerate(order):
            self.index[kind, t, b] = n + 1

    def filled(self, kind, t, b):
        if isinstance(t, int):
            return self.index[kind, t, b]
        return self.index[kind, 2, b] + (t - 2) * (self.index[kind, 3, b] - self.index[kind, 2, b])


def build(nc, a, out):
    with ExitStack() as ctx:
        def sb(name, shape, dt=F32, where=ctx):
            return where.enter_context(nc.sbuf_tensor(name, shape, dt))

        def sem(name):
            return ctx.enter_context(nc.semaphore(name))

        psum = ctx.enter_context(nc.psum_tensor("psum", [P, 8, 512], F32))
        bank = [psum[:, i, :] for i in range(8)]
        cst = sb("cst", [P, C_END])
        x = sb("x", [P, NT, D])
        w = {}
        for name in WEIGHTS:
            w[name] = sb("w_" + name, [P] + list(a[name].shape[1:]))
        wn = sb("wn", [P, NBLK, QB])
        c = Consts(cst)
        loaded = {name: sem("loaded_" + name) for name in GROUPS}
        x_loaded, stored = sem("x_loaded"), sem("stored")

        phases = [
            lambda s: distance_attention(nc, a, sb, s, bank, c, cst, x, w, loaded, x_loaded, wn),
            lambda s: ratio_attention(nc, a, sb, s, psum, bank, c, x, w, loaded),
            lambda s: quantised_ffn(nc, a, sb, s, bank, c, x, wn),
            lambda s: context_attention(nc, a, sb, s, bank, c, x, w, loaded),
            lambda s: segment_attention(nc, a, sb, s, psum, bank, c, x, w, loaded),
            lambda s: experts(nc, a, sb, s, bank, c, x, w, loaded),
        ]
        for phase in phases:
            own = []

            def phase_sem(name):
                own.append(nc.alloc_semaphore(name=name))
                return own[-1]

            phase(phase_sem)
            nc.clear_and_free_semaphores(own)
            nc.all_engine_barrier()
        with nc.Block() as block:
            @block.sync
            def _(sp):
                sp.dma_start(out, x[:]).then_inc(stored, 16)
                sp.wait_ge(stored, 16)


class Consts:

    def __init__(self, cst):
        self.ident = cst[:, C_ID:C_ID + P]
        self.headq = cst[:, C_HEADQ:C_HEADQ + P]
        self.head = cst[:, C_HEAD:C_HEAD + 4]
        self.row = cst[:, C_ROW:C_ROW + 4]
        self.eq = cst[:, C_EQ:C_EQ + SQ]
        self.causal = cst[:, C_CAUSAL:C_CAUSAL + SQ]
        self.slope = cst[:, C_SLOPE:C_SLOPE + NG]
        self.exp8 = cst[:, C_EXP8:C_EXP8 + 8]
        self.last = cst[0:16, C_LAST:C_LAST + 16]
        self.half = cst[:, C_HALF:C_HALF + 16]
        self.quarter = cst[:, C_QUARTER:C_QUARTER + 4]
        self.ones = cst[:, C_ONES:C_ONES + SQ]


GROUPS = {
    "xattn": ("xa_q", "xa_k", "xa_v", "xa_o"),
    "ratio": ("ra_qkv", "ra_o", "ra_bqk", "ra_bv", "ra_bo"),
    "cross": ("cx_q", "cx_k", "cx_v", "cx_bq", "cx_bk", "cx_bv"),
    "segs": ("lt_qkv", "lt_o", "lt_bqk", "lt_bv", "lt_bo", "st_qkv", "st_o", "st_bqk", "st_bv", "st_bo",
             "protos", "fus", "fus_b"),
    "router": ("router",),
}
WEIGHTS = sum(GROUPS.values(), ())


def distance_attention(nc, a, sb_, sem, bank, c, cst, x, w, loaded, x_loaded, wn):
    with ExitStack() as own:
        def sb(name, shape, dt=F32):
            return sb_(name, shape, dt, own)

        PER = NBLK // (BT * (NT - 2))
        round_by = sb("round_by", [P, 1])
        wmax, wscale, wrecip = sb("wmax", [P, NBLK]), sb("wscale", [P, NBLK]), sb("wrecip", [P, NBLK])
        last_T = sb("last_T", [P, KT, NB])
        last_rep = sb("last_rep", [P, KT, NB, NG])
        v_last = sb("v_last", [16, NT, D])

        qpos = sb("qpos", [P, NB], I32)
        qposf = sb("qposf", [P, NB])
        ctxT = [sb(f"ctxT{b}", [P, KT, SK]) for b in range(BT)]
        msk = [sb(f"msk{b}", [P, SK], I32) for b in range(BT)]
        kpos = [sb(f"kpos{b}", [P, SK], I32) for b in range(BT)]
        dist = [sb(f"dist{i}", [P, SK]) for i in range(2)]
        shut = sb("shut", [P, SK])
        bias = [sb(f"bias{i}", [P, NG, SK]) for i in range(2)]
        kT = [sb(f"kT{i}", [P, KT, SK]) for i in range(2)]
        v = [sb(f"v{b}", [P, 2, D]) for b in range(BT)]
        s_sb = [sb(f"s_sb{i}", [P, NG, SK]) for i in range(2)]
        prob = [sb(f"prob{i}", [P, NG, SK]) for i in range(2)]
        mx, negm = sb("mx", [P, BT, NG]), sb("negm", [P, BT, NG])
        esum, rden = sb("esum", [P, BT, NG]), sb("rden", [P, BT, NG])
        rmask = sb("rmask", [P, BT, NG, 4])
        pT = [sb(f"pT{i}", [P, NG, 2, P]) for i in range(2)]
        plast, plast_T = sb("plast", [P, BT, NG]), sb("plast_T", [16, P])
        vx = sb("vx", [16, BT, NG, 64])
        om = sb("om", [P, BT, NG, 64])
        oT, xn, xT = sb("oT", [P, KT, P]), sb("xn", [P, D]), sb("xT", [P, KT, P])
        stat, mv, rstd = sb("stat", [P, 6]), sb("mv", [P, 2]), sb("rstd", [P, 1])
        veps = sb("veps", [P, 1])
        qbd = sb("qbd", [P, KT, BT, 4, SQ])
        sc, pt, kv, oo = bank[0:2], bank[2:4], bank[4:6], bank[6:8]

        ctx_loaded = [sem(f"ctx_loaded{b}") for b in range(BT)]
        passed_sp, passed_dve, passed_pool = sem("xa_passed_sp"), sem("xa_passed_dve"), sem("xa_passed_pool")
        cst_loaded, wn_loaded, pos_loaded = sem("cst_loaded"), sem("wn_loaded"), sem("pos_loaded")
        wq_steps = Steps(sem("xa_dve_steps"))
        scales_ready, pool_steps = sem("scales_ready"), Steps(sem("xa_pool_steps"))
        last_ready, vl_full, vl_done = sem("last_ready"), sem("vl_full"), sem("vl_done")
        kv_full = [sem("kv0_full"), sem("kv1_full")]
        kv_done = [sem("kv0_done"), sem("kv1_done")]
        s_full, s_done = sem("s_full"), sem("s_done")
        negm_ready, p_ready = sem("negm_ready"), sem("p_ready")
        pt_full, pt_done = sem("pt_full"), sem("pt_done")
        pv_done, o_full, o_done = sem("pv_done"), sem("o_full"), sem("o_done")
        var_ready, rstd_ready, xn_ready = sem("var_ready"), sem("rstd_ready"), sem("xn_ready")
        rmask_ready, dist_ready, bias_ready = sem("rmask_ready"), sem("dist_ready"), sem("bias_ready")
        plast_ready, vx_ready = sem("plast_ready"), sem("vx_ready")

        use0, use1 = [], [("xT", -1, 2), ("q", -1, 3)]
        for t in range(NT + 1):
            for b in range(BT):
                if t < NT:
                    use0 += [("k", t, b), ("v", t, b)]
                if b == 1 and t > 0:
                    use1 += [("plast", t, b)]
                if t < NT:
                    use1 += [("k", t, b)]
                if b == 2 and t > 0:
                    use1 += [("oT", t, b)]
                if b == 2 and t < NT - 1:
                    use1 += [("xT", t, b)]
                if b == 3 and t > 0:
                    use1 += [("out", t, b)]
                if b == 3 and t < NT - 1:
                    use1 += [("q", t, b)]
        uses = [Uses(use0), Uses(use1)]

        def tiles(eng, step, steps=None, per=None):
            for b in range(BT):
                step(0, b)
            with eng.Fori(1, NT - 1) as t:
                if steps:
                    steps.enter(t, 1, per)
                for b in range(BT):
                    step(t, b)
                if steps:
                    steps.leave(NT - 2)
            for t in (NT - 1, NT):
                for b in range(BT):
                    step(t, b)

        def exists(t):
            return not isinstance(t, int) or 0 <= t < NT

        def before(t, b, lag):
            return t + (b - lag) // BT, (b - lag) % BT

        with nc.Block() as block:
            @block.sync
            def _(sp):
                sp.dma_start(cst[:], a["cst"]).then_inc(cst_loaded, 16)
                sp.dma_start(x[:], a["x"]).then_inc(x_loaded, 16)
                for name in GROUPS["xattn"]:
                    sp.dma_start(w[name][:], a[name]).then_inc(loaded["xattn"], 16)
                sp.dma_start(last_T[:], a["ctx_last_T"]).then_inc(pos_loaded, 16)
                for h in range(4):
                    sp.dma_start(qpos[SQ * h:SQ * h + SQ, :], a["qpos_T"]).then_inc(pos_loaded, 16)

                def context(t, b):
                    tt, bb = t - 1, b
                    if exists(tt) and not (isinstance(t, int) and t == 0):
                        sp.wait_ge(kv_full[0], uses[0].filled("v", tt, bb))
                        alone(sp, passed_sp)
                        sp.wait_ge(dist_ready, 4 * tt + bb + 1)
                        alone(sp, passed_sp)
                    sp.dma_start(ctxT[b][:], a["ctx_T"][BT * t + b]).then_inc(ctx_loaded[b], 16)
                    sp.dma_start(kpos[b][:], a["kpos"][BT * t + b].unsqueeze(0).broadcast_to([P, SK])) \
                        .then_inc(ctx_loaded[b], 16)
                    sp.dma_start(msk[b][:], a["mask"][BT * t + b].unsqueeze(0).broadcast_to([4, SQ, SK])) \
                        .then_inc(ctx_loaded[b], 16)

                for b in range(BT):
                    context(0, b)
                for n, name in enumerate(("w_gate", "w_up", "w_down")):
                    sp.dma_start(wn[:, n * NBLK // 3:(n + 1) * NBLK // 3, :], a[name]).then_inc(wn_loaded, 16)
                for g in ("ratio", "cross", "segs", "router"):
                    for name in GROUPS[g]:
                        sp.dma_start(w[name][:], a[name]).then_inc(loaded[g], 16)
                with sp.Fori(1, NT) as t:
                    for b in range(BT):
                        context(t, b)

            @block.gpsimd
            def _(pool):
                pool.wait_ge(pos_loaded, 80)
                nc.gpsimd.tensor_copy(last_rep[:], last_T[:].unsqueeze(3).broadcast_to([P, KT, NB, NG])) \
                    .then_inc(last_ready, 1)
                nc.gpsimd.tensor_copy(qposf[:], qpos[:]).then_inc(last_ready, 1)

                def root(t):
                    pool.wait_ge(var_ready, t + 1)
                    nc.gpsimd.tensor_tensor(rstd[:], veps[:], c.half[:, 0:1], ALU.pow).then_inc(rstd_ready, 1)

                def biases(t, b):
                    if not exists(t):
                        return
                    pool.wait_ge(dist_ready, 4 * t + b + 1)
                    at_least(pool, s_done, 16 * t + 4 * b + 4 - 8)
                    alone(pool, passed_pool)
                    for g in range(NG):
                        nc.gpsimd.tensor_scalar(bias[b % 2][:, g, :], dist[b % 2][:], c.slope[:, g:g + 1], 1.0,
                                                ALU.mult, ALU.mult).then_inc(bias_ready, 1)

                nc.gpsimd.memset(round_by[:], ROUND).then_inc(last_ready, 1)
                pool.wait_ge(last_ready, 3)
                pool.wait_ge(cst_loaded, 16)
                root(0)
                biases(0, 0)

                def quantise(t, b):
                    at = bass.ds((t - 1) * (BT * PER) + b * PER, PER)
                    blocks = wn[:, at, :]
                    each = [P, PER, QB]
                    for by, op in ((wrecip[:, at], ALU.mult), (round_by[:], ALU.add), (round_by[:], ALU.subtract),
                                   (wscale[:, at], ALU.mult)):
                        pool_steps.link(pool, nc.gpsimd.tensor_tensor(
                            blocks, blocks, by.unsqueeze(2).broadcast_to(each), op))
                        alone(pool, passed_pool)

                def step(t, b):
                    if b == 1 and exists(t + 1) and exists(t):
                        root(t + 1)
                    biases(*before(t, b, -1))
                    if not isinstance(t, int):
                        if b == 0:
                            pool.wait_ge(scales_ready, 3)
                        quantise(t, b)

                tiles(pool, step, pool_steps, BT * 4)

            @block.scalar
            def _(act):
                def xT_copy(t, b):
                    act.wait_ge(kv_full[1], uses[1].filled("xT", t, b))
                    nc.scalar.copy(xT[:], kv[1][:, 0:D].rearrange("p (k n) -> p k n", k=KT)) \
                        .then_inc(kv_done[1], 1)

                xT_copy(-1, 2)

                def keys(t, b, m):
                    act.wait_ge(kv_full[m], uses[m].filled("k", t, b))
                    at_least(act, s_full, 16 * t + 4 * b - 4)
                    nc.scalar.copy(kT[b % 2][:, m, :], kv[m][:, 0:SK]).then_inc(kv_done[m], 1)

                def exps(t, b, gs):
                    if not exists(t):
                        return
                    if gs[0] == 0:
                        act.wait_ge(negm_ready, 4 * t + b + 1)
                        at_least(act, pt_full, 8 * t + 2 * b + 2 - 4)
                        at_least(act, plast_ready, 4 * t + b + 1 - 2)
                        if b == 0:
                            at_least(act, rmask_ready, t)
                    for g in gs:
                        nc.scalar.activation(prob[b % 2][:, g, :], s_sb[b % 2][:, g, :], ACT.Exp,
                                             bias=negm[:, b, g:g + 1], accum_out=esum[:, b, g:g + 1]) \
                            .then_inc(p_ready, 1)

                def step(t, b):
                    if b == 1 and exists(t - 1):
                        act.wait_ge(kv_full[1], uses[1].filled("plast", t, b))
                        nc.scalar.copy(plast_T[:], kv[1][0:16, 0:P]).then_inc(kv_done[1], 1)
                    if exists(t):
                        keys(t, b, 0)
                    te, be = before(t, b, 1)
                    exps(te, be, (0, 1))
                    if exists(t):
                        keys(t, b, 1)
                        act.wait_ge(kv_full[0], uses[0].filled("v", t, b))
                        at_least(act, pv_done, 4 * t + b + 1 - BT)
                        nc.scalar.copy(v[b][:], kv[0][:].rearrange("p (k n) -> p k n", k=2)) \
                            .then_inc(kv_done[0], 1)
                    exps(te, be, (2, 3))
                    if b == 2 and exists(t - 1):
                        act.wait_ge(kv_full[1], uses[1].filled("oT", t, b))
                        nc.scalar.copy(oT[:], kv[1][:, 0:D].rearrange("p (k n) -> p k n", k=KT)) \
                            .then_inc(kv_done[1], 1)
                    if b == 2 and exists(t) and exists(t + 1):
                        xT_copy(t, b)

                tiles(act, step)

            @block.tensor
            def _(pe):
                pe.wait_ge(cst_loaded, 16)
                pe.wait_ge(last_ready, 1)
                pe.wait_ge(loaded["xattn"], 64)
                for t in range(NT):
                    at_least(pe, vl_done, t - 1)
                    for k in range(KT):
                        ins = nc.tensor.matmul(bank[2 + t % 2][0:16, 0:D],
                                               last_rep[:, k, BT * t:BT * t + BT, :].rearrange("p b g -> p (b g)"),
                                               w["xa_v"][:, k, :], start=(k == 0), stop=(k == KT - 1))
                    ins.then_inc(vl_full, 1)

                def turn_x(t, b):
                    pe.wait_ge(xn_ready, t + 2)
                    if not (isinstance(t, int) and t < 0):
                        pe.wait_ge(kv_done[1], uses[1].filled("xT", t, b) - 1)
                    for k in range(KT):
                        ins = nc.tensor.transpose(kv[1][:, P * k:P * k + P], xn[:, P * k:P * k + P], c.ident)
                    ins.then_inc(kv_full[1], 1)

                def queries(t, b):
                    pe.wait_ge(kv_done[1], uses[1].filled("q", t, b) - 1)
                    for m in range(KT):
                        for k in range(KT):
                            ins = nc.tensor.matmul(kv[1][:, P * m:P * m + P], w["xa_q"][:, k, P * m:P * m + P],
                                                   xT[:, k, :], start=(m == 0 and k == 0),
                                                   stop=(m == KT - 1 and k == KT - 1), skip_group_check=True)
                    ins.then_inc(kv_full[1], 1)

                turn_x(-1, 2)
                queries(-1, 3)
                pe.wait_ge(vl_done, NT)

                def keys(t, b, m):
                    at_least(pe, kv_done[m], uses[m].filled("k", t, b) - 1)
                    for k in range(KT):
                        ins = nc.tensor.matmul(kv[m][:, 0:SK], w["xa_k"][:, k, P * m:P * m + P], ctxT[b][:, k, :],
                                               start=(k == 0), stop=(k == KT - 1))
                    ins.then_inc(kv_full[m], 1)

                def values(t, b):
                    pe.wait_ge(kv_done[0], uses[0].filled("v", t, b) - 1)
                    for i in range(2):
                        for k in range(KT):
                            ins = nc.tensor.matmul(kv[0][:, D * i:D * i + D], ctxT[b][:, k, P * i:P * i + P],
                                                   w["xa_v"][:, k, :], start=(i == 0 and k == 0),
                                                   stop=(i == 1 and k == KT - 1), skip_group_check=True)
                    ins.then_inc(kv_full[0], 1)

                def scores(t, b, gs):
                    pe.wait_ge(kv_done[0], uses[0].filled("k", t, b))
                    pe.wait_ge(kv_done[1], uses[1].filled("k", t, b))
                    for g in gs:
                        lo = 64 * (g % 2)
                        at_least(pe, s_done, 16 * t + 4 * b + g - 1)
                        nc.tensor.matmul(sc[g % 2][:, 0:SK],
                                         qbd[lo:lo + 64, g // 2, b, :, :].rearrange("p h q -> p (h q)"),
                                         kT[b % 2][lo:lo + 64, g // 2, :], start=True, stop=True).then_inc(s_full, 1)

                def turn_p(t, b, j):
                    pe.wait_ge(p_ready, 16 * t + 4 * b + 2 * j + 2)
                    at_least(pe, pt_done, 8 * t + 2 * b + j + 1 - 2)
                    for g in (2 * j, 2 * j + 1):
                        for i in range(2):
                            at = 2 * P * (g % 2) + P * i
                            ins = nc.tensor.transpose(pt[j][:, at:at + P], prob[b % 2][:, g, P * i:P * i + P],
                                                      c.ident)
                    ins.then_inc(pt_full, 1)

                def weighted(t, b):
                    pe.wait_ge(pt_done, 8 * t + 2 * b + 2)
                    pe.wait_ge(kv_done[0], uses[0].filled("v", t, b))
                    if b == 0:
                        at_least(pe, o_done, t)
                    for g in range(NG):
                        for i in range(2):
                            at = D * (b % 2) + 64 * g
                            ins = nc.tensor.matmul(oo[b // 2][:, at:at + 64], pT[b % 2][:, g, i, :],
                                                   v[b][:, i, 64 * g:64 * g + 64],
                                                   start=(b % 2 == 0 and g == 0 and i == 0), stop=False,
                                                   skip_group_check=True)
                    ins.then_inc(pv_done, 1)

                def turn_last(t, b):
                    pe.wait_ge(plast_ready, 4 * t)
                    pe.wait_ge(kv_done[1], uses[1].filled("plast", t, b) - 1)
                    nc.tensor.transpose(kv[1][0:16, 0:P], plast[:].rearrange("p b g -> p (b g)"), c.ident) \
                        .then_inc(kv_full[1], 1)

                def weighted_last(t, b):
                    pe.wait_ge(kv_done[1], uses[1].filled("plast", t, b))
                    pe.wait_ge(vx_ready, t)
                    for i in range(2):
                        ins = nc.tensor.matmul(oo[i][:], plast_T[:],
                                               vx[:, 2 * i:2 * i + 2, :, :].rearrange("p b g d -> p (b g d)"),
                                               start=False, stop=True, skip_group_check=True)
                    ins.then_inc(o_full, 1)

                def heads_to_features(t, b):
                    pe.wait_ge(o_done, t)
                    pe.wait_ge(kv_done[1], uses[1].filled("oT", t, b) - 1)
                    for bb in range(BT):
                        for m in range(KT):
                            at = P * m + SQ * bb
                            ins = nc.tensor.matmul(kv[1][:, at:at + SQ],
                                                   om[:, bb, 2 * m:2 * m + 2, :].rearrange("p g d -> p (g d)"), c.eq,
                                                   start=(bb == 0 and m == 0), stop=True, skip_group_check=True)
                    ins.then_inc(kv_full[1], 1)

                def output(t, b):
                    pe.wait_ge(kv_done[1], uses[1].filled("out", t, b) - 1)
                    for k in range(KT):
                        ins = nc.tensor.matmul(kv[1][:, 0:D], oT[:, k, :], w["xa_o"][:, k, :],
                                               start=(k == 0), stop=(k == KT - 1))
                    ins.then_inc(kv_full[1], 1)

                def step(t, b):
                    if b == 1 and exists(t - 1):
                        turn_last(t, b)
                    if exists(t):
                        pe.wait_ge(ctx_loaded[b], 48 * (t + 1))
                        keys(t, b, 0)
                        keys(t, b, 1)
                        values(t, b)
                    if b == 3 and exists(t - 1):
                        output(t, b)
                    t1, b1 = before(t, b, 1)
                    for j in range(2):
                        if exists(t):
                            scores(t, b, (2 * j, 2 * j + 1))
                        if exists(t1):
                            turn_p(t1, b1, j)
                    if b == 2 and exists(t - 1):
                        heads_to_features(t, b)
                    t2, b2 = before(t, b, 2)
                    if exists(t2):
                        weighted(t2, b2)
                    if b == 1 and exists(t - 1):
                        weighted_last(t, b)
                    if b == 2 and exists(t) and exists(t + 1):
                        turn_x(t, b)
                    if b == 3 and exists(t) and exists(t + 1):
                        queries(t, b)

                tiles(pe, step)

            @block.vector
            def _(dve):
                st = wq_steps

                def norm_stats(t):
                    st.link(dve, nc.vector.bn_stats(stat[:], x[:, t, :]))
                    alone(dve, passed_dve)
                    st.link(dve, nc.vector.bn_aggr(mv[:], stat[:]))
                    nc.vector.tensor_scalar(veps[:], mv[:, 1:2], LN_EPS, None, ALU.add).then_inc(var_ready, 1)

                def norm(t):
                    dve.wait_ge(rstd_ready, t + 1)
                    if not isinstance(t, int) or t > 0:
                        dve.wait_ge(s_full, 16 * (t - 1) + 4)
                    nc.vector.tensor_scalar(xn[:], x[:, t, :], mv[:, 0:1], rstd[:], ALU.subtract, ALU.mult) \
                        .then_inc(xn_ready, 1)

                def distances(t, b):
                    if not exists(t):
                        return
                    dve.wait_ge(ctx_loaded[b], 48 * (t + 1))
                    at_least(dve, bias_ready, 16 * t + 4 * b + 4 - 8)
                    n = st.done(nc.vector.tensor_scalar(dist[b % 2][:], kpos[b][:], qcol(t, b), None, ALU.subtract))
                    n = st.done(nc.vector.tensor_scalar(shut[:], msk[b][:], 0.0, -BIG, ALU.is_equal, ALU.mult))
                    dve.wait_ge(st.sem, n)
                    nc.vector.scalar_tensor_tensor(dist[b % 2][:], shut[:], BIG, dist[b % 2][:], ALU.mult, ALU.add) \
                        .then_inc(dist_ready, 1)

                def qcol(t, b):
                    if isinstance(t, int):
                        return qposf[:, BT * t + b:BT * t + b + 1]
                    return qposf[:, bass.ds(t * BT + b, 1)]

                def rows_max(t, b):
                    dve.wait_ge(bias_ready, 16 * t + 4 * b + 4)
                    at_least(dve, p_ready, 16 * t + 4 * b + 4 - 8)
                    for g in range(NG):
                        dve.wait_ge(s_full, 16 * t + 4 * b + g + 1)
                        alone(dve, passed_dve)
                        nc.vector.tensor_tensor_reduce(s_sb[b % 2][:, g, :], sc[g % 2][:, 0:SK], bias[b % 2][:, g, :],
                                                       1.0, float("-inf"), ALU.add, ALU.max, mx[:, b, g:g + 1]) \
                            .then_inc(s_done, 1)
                    dve.wait_ge(s_done, 16 * t + 4 * b + 4)
                    nc.vector.tensor_scalar(negm[:, b, :], mx[:, b, :], -1.0, None, ALU.mult).then_inc(negm_ready, 1)

                def spread_queries(t):
                    dve.wait_ge(kv_full[1], uses[1].filled("q", t - 1, 3))
                    at_least(dve, s_full, 16 * t)
                    for m in range(KT):
                        src = kv[1][:, P * m:P * m + P].rearrange("p (b q) -> p b q", b=BT)
                        ins = nc.vector.tensor_tensor(
                            qbd[:, m, :, :, :], src.unsqueeze(2).broadcast_to([P, BT, 4, SQ]),
                            c.quarter.unsqueeze(1).unsqueeze(3).broadcast_to([P, BT, 4, SQ]), ALU.mult)
                    ins.then_inc(kv_done[1], 1)

                def copy_turned(t, b):
                    dve.wait_ge(p_ready, 16 * t + 4 * b + 4)
                    if b == 0:
                        at_least(dve, kv_full[1], 0 if isinstance(t, int) and t == 0
                                 else uses[1].filled("plast", t, 1))
                    nc.vector.tensor_copy(plast[:, b, :], prob[b % 2][:, :, SK - 1]).then_inc(plast_ready, 1)
                    at_least(dve, pv_done, 4 * t + b + 1 - 2)
                    for j in range(2):
                        dve.wait_ge(pt_full, 8 * t + 2 * b + j + 1)
                        nc.vector.tensor_copy(pT[b % 2][:, 2 * j:2 * j + 2, :, :],
                                              pt[j][:].rearrange("p (g i n) -> p g i n", g=2, i=2)) \
                            .then_inc(pt_done, 1)

                def spread_last(t):
                    if not (isinstance(t, int) and t == 0):
                        dve.wait_ge(o_full, t)
                    src = v_last[:, t, :].rearrange("p (g d) -> p g d", g=NG)
                    for b in range(BT):
                        ins = nc.vector.tensor_tensor(
                            vx[:, b, :, :], src, c.last[:, NG * b:NG * b + NG].unsqueeze(2).broadcast_to([16, NG, 64]),
                            ALU.mult)
                    ins.then_inc(vx_ready, 1)

                def weigh(t):
                    dve.wait_ge(p_ready, 16 * t + 16)
                    st.link(dve, nc.vector.tensor_scalar(rden[:], esum[:], 1.0, None, ALU.add))
                    st.link(dve, nc.vector.reciprocal(rden[:], rden[:]))
                    nc.vector.tensor_tensor(
                        rmask[:].rearrange("p b g h -> p (b g) h"),
                        rden[:].rearrange("p b g -> p (b g)").unsqueeze(2).broadcast_to([P, 16, 4]),
                        c.row.unsqueeze(1).broadcast_to([P, 16, 4]), ALU.mult).then_inc(rmask_ready, 1)

                def normalise(t):
                    dve.wait_ge(rmask_ready, t + 1)
                    dve.wait_ge(o_full, t + 1)
                    for i in range(2):
                        ins = nc.vector.tensor_tensor(
                            om[:, 2 * i:2 * i + 2, :, :].rearrange("p b g (h d) -> p (b g h) d", h=4),
                            oo[i][:].rearrange("p (n d) -> p n d", d=DH),
                            rmask[:, 2 * i:2 * i + 2, :, :].rearrange("p b g h -> p (b g h)").unsqueeze(2)
                            .broadcast_to([P, 32, DH]), ALU.mult)
                    ins.then_inc(o_done, 1)

                def add_output(t, tt):
                    dve.wait_ge(kv_full[1], uses[1].filled("out", t, 3))
                    nc.vector.tensor_tensor(x[:, tt, :], kv[1][:, 0:D], x[:, tt, :], ALU.add).then_inc(kv_done[1], 1)

                def scales(i):
                    at = slice(i * NBLK // 3, (i + 1) * NBLK // 3)
                    dve.wait_ge(wn_loaded, 48)
                    st.link(dve, nc.vector.tensor_reduce(wmax[:, at], wn[:, at, :], AX.X, ALU.max,
                                                         apply_absolute_value=True))
                    st.link(dve, nc.vector.tensor_scalar(wscale[:, at], wmax[:, at], 1.0 / 7.0, 1e-12, ALU.mult,
                                                         ALU.max))
                    nc.vector.reciprocal(wrecip[:, at], wscale[:, at]).then_inc(scales_ready, 1)

                def step(t, b):
                    t1, b1 = before(t, b, 1)
                    if isinstance(t, int) and t == 0 and b > 0:
                        scales(b - 1)
                    if b == 1 and exists(t - 1):
                        weigh(t - 1)
                    if b == 2 and exists(t - 1):
                        normalise(t - 1)
                    if b == 3 and exists(t - 1):
                        add_output(t, t - 1)
                    if exists(t):
                        rows_max(t, b)
                    if exists(t1):
                        copy_turned(t1, b1)
                    if b == 1 and exists(t) and exists(t + 1):
                        norm_stats(t + 1)
                        norm(t + 1)
                    if b == 3 and exists(t) and exists(t + 1):
                        spread_queries(t + 1)
                    if exists(t):
                        distances(*before(t, b, -1))
                    if b == 3 and exists(t):
                        spread_last(t)

                dve.wait_ge(cst_loaded, 16)
                for t in range(NT):
                    dve.wait_ge(vl_full, t + 1)
                    nc.vector.tensor_copy(v_last[:, t, :], bank[2 + t % 2][0:16, 0:D]).then_inc(vl_done, 1)
                dve.wait_ge(vl_done, NT)
                dve.wait_ge(last_ready, 2)
                dve.wait_ge(x_loaded, 16)
                norm_stats(0)
                norm(0)
                distances(0, 0)
                spread_queries(0)
                tiles(dve, step, st, 4 * 2 + 2 + 2)



def turn_tokens(nc, dst, src, c):
    for k in range(KT):
        ins = nc.tensor.transpose(dst[:, P * k:P * k + P], src[:, P * k:P * k + P], c.ident)
    return ins


def project_qk(nc, dst, weight, xT):
    for m in range(2 * KT):
        for k in range(KT):
            ins = nc.tensor.matmul(dst[:, P * m:P * m + P], weight[:, k, P * m:P * m + P], xT[:, k, :],
                                   start=(m == 0 and k == 0), stop=True, skip_group_check=True)
    return ins


def project_tokens(nc, dst, lhs_T, weight):
    n = weight.shape[1]
    for k in range(n):
        ins = nc.tensor.matmul(dst[:, 0:D], lhs_T[:, k, :], weight[:, k, :], start=(k == 0), stop=(k == n - 1))
    return ins


def spread_heads(eng, kbd, kT, head, m):
    src = kT[:, m, :].rearrange("p (b k) -> p b k", b=BT)
    return eng.tensor_tensor(kbd[:, m, :, :, :], src.unsqueeze(2).broadcast_to([P, BT, 4, SQ]),
                             head.unsqueeze(1).unsqueeze(3).broadcast_to([P, BT, 4, SQ]), ALU.mult)


def spread_batches(eng, vbd, v, c):
    for b in range(BT):
        ins = eng.tensor_tensor(vbd[:, b, :, 0:DH], v[:].rearrange("p (n d) -> p n d", d=DH),
                                c.row[:, b:b + 1].unsqueeze(2).broadcast_to([P, NH, DH]), ALU.mult)
    return ins


def per_batch(nc, dst, left, right, col, first):
    for m in range(KT):
        for b in range(BT):
            for f in range(2):
                lo, at = 64 * f, col + P * m
                ins = nc.tensor.matmul(dst[SQ * b:SQ * b + SQ, f, at:at + P], left(lo, m, b), right(lo, m, b),
                                       start=first and m == 0, stop=True, skip_group_check=True)
    return ins


def tokens(xT):
    return lambda lo, m, b: xT[lo:lo + 64, m, SQ * b:SQ * b + SQ]


def heads_apart(bd):
    return lambda lo, m, b: bd[lo:lo + 64, m, b, :, :].rearrange("p h k -> p (h k)")


def heads_of_banks():
    return [NG * KT * m + NG * f + h for f in range(2) for m in range(KT) for h in range(4)]


def in_banks(scores):
    return scores[:].rearrange("p (f n) k -> p f (n k)", f=2)


def weigh_values(nc, dst, pT, vbd):
    for i, n in enumerate(heads_of_banks()):
        for b in range(BT):
            ins = nc.tensor.matmul(dst[SQ * b:SQ * b + SQ, 17 * n:17 * n + 17], pT[:, i, :], vbd[:, b, n, :],
                                   start=(i == 0), stop=True, skip_group_check=True)
    return ins


def turn_blocks(nc, pT, prob):
    return nc.vector.transpose(pT[:].rearrange("p n q -> p (n q)"), prob[:].rearrange("p n k -> p (n k)"))


def over_sum(nc, o, src, rden):
    return nc.vector.tensor_tensor(o[:].rearrange("p (n d) -> p n d", d=DH),
                                   src[:, 0:17 * NH].rearrange("p (n e) -> p n e", e=17)[:, :, 0:DH],
                                   rden[:].unsqueeze(2).broadcast_to([P, NH, DH]), ALU.mult)


def sums_of(src):
    return src[:, 0:17 * NH].rearrange("p (n e) -> p n e", e=17)[:, :, DH]


def slots(eng, step, steps=None, per=None):
    for u in (-2, -1, 0):
        step(u)
    with eng.Fori(1, NT - 3) as u:
        if steps:
            steps.enter(u, 1, per)
        step(u)
        if steps:
            steps.leave(NT - 4)
    for u in range(NT - 3, NT):
        step(u)


def there(u, count=NT):
    return not isinstance(u, int) or 0 <= u < count


def ratio_attention(nc, a, sb_, sem, psum, bank, c, x, w, loaded):
    with ExitStack() as own:
        def sb(name, shape, dt=F32):
            return sb_("ra_" + name, shape, dt, own)

        def rsem(name):
            return sem("ra_" + name)

        xn, xT = sb("xn", [P, D]), sb("xT", [P, KT, P])
        stat, mv, veps, rstd = sb("stat", [P, 6]), sb("mv", [P, 2]), sb("veps", [P, 1]), sb("rstd", [P, 1])
        bq2, eps = sb("bq2", [P, KT]), sb("eps", [P, 1])
        qm2T, q2T, kT = sb("qm2T", [P, KT, P]), sb("q2T", [P, KT, P]), sb("kT", [P, KT, P])
        kbd, k2bd = sb("kbd", [P, KT, BT, 4, SQ]), sb("k2bd", [P, KT, BT, 4, SQ])
        v, vbd = sb("v", [P, D]), sb("vbd", [P, BT, NH, 17])
        num, den, prob = (sb(name, [P, NH, SQ]) for name in ("num", "den", "prob"))
        dot = sb("dot", [P, NH, SQ])
        mx, rden = sb("mx", [P, NH]), sb("rden", [P, NH])
        pT, o, oT = sb("pT", [P, NH, SQ]), sb("o", [P, D]), sb("oT", [P, KT, P])
        s_banks, x_bank, qk_bank, v_bank, o_bank, t_bank, y_bank = psum[:, 0:2, :], *bank[2:8]

        st, pst = Steps(rsem("dve_steps")), Steps(rsem("pool_steps"))
        passed_dve, passed_pool, passed_pe = rsem("passed_dve"), rsem("passed_pool"), rsem("passed_pe")
        var_ready, rstd_ready, xn_ready = rsem("var_ready"), rsem("rstd_ready"), rsem("xn_ready")
        xT_full, xT_done, qk_full = rsem("xT_full"), rsem("xT_done"), rsem("qk_full")
        k_ready, qk_done = rsem("k_ready"), rsem("qk_done")
        kbd_ready, k2_ready = [rsem("kbd0_ready"), rsem("kbd1_ready")], rsem("k2_ready")
        v_full, v_done, vbd_ready = rsem("v_full"), rsem("v_done"), rsem("vbd_ready")
        s_full, s_read, sub_ready, p_ready = rsem("s_full"), rsem("s_read"), rsem("sub_ready"), rsem("p_ready")
        pT_ready, o_full, o_done = rsem("pT_ready"), rsem("o_full"), rsem("o_done")
        oT_full, oT_done, y_full, y_done = rsem("oT_full"), rsem("oT_done"), rsem("y_full"), rsem("y_done")
        den_ready = rsem("den_ready")
        bias_added, sums_set, consts_set = rsem("bias_added"), rsem("sums_set"), rsem("consts_set")

        with nc.Block() as block:
            @block.gpsimd
            def _(pool):
                for b in range(BT):
                    ins = nc.gpsimd.tensor_copy(vbd[:, b, :, DH], c.row[:, b:b + 1].broadcast_to([P, NH]))
                ins.then_inc(sums_set, 1)

                def root(n):
                    pool.wait_ge(var_ready, n + 1)
                    nc.gpsimd.tensor_tensor(rstd[:], veps[:], c.half[:, 0:1], ALU.pow).then_inc(rstd_ready, 1)

                def step(u):
                    if there(u + 1):
                        pool.wait_ge(v_done, u + 2)
                        at_least(pool, o_full, u + 1)
                        alone(pool, passed_pool)
                        spread_batches(nc.gpsimd, vbd, v, c).then_inc(vbd_ready, 1)
                    if there(u + 2):
                        pool.wait_ge(k_ready, u + 3)
                        at_least(pool, s_full, u + 2)
                        alone(pool, passed_pool)
                        spread_heads(nc.gpsimd, kbd, kT, c.head, 1).then_inc(kbd_ready[1], 1)
                        pool.wait_ge(xn_ready, u + 3)
                        alone(pool, passed_pool)
                        nc.gpsimd.tensor_tensor(x[:, u + 2, :], x[:, u + 2, :], w["ra_bo"][:], ALU.add) \
                            .then_inc(bias_added, 1)
                    if there(u + 3):
                        root(u + 3)

                pool.wait_ge(loaded["ratio"], 16 * len(GROUPS["ratio"]))
                root(0)
                slots(pool, step)

            @block.scalar
            def _(act):
                act.wait_ge(loaded["ratio"], 16 * len(GROUPS["ratio"]))
                act.wait_ge(consts_set, 2)

                def step(u):
                    if there(u + 2):
                        n = u + 2
                        act.wait_ge(xT_full, n + 1)
                        at_least(act, v_full, n)
                        nc.scalar.copy(xT[:], x_bank[:, 0:D].rearrange("p (k t) -> p k t", k=KT)).then_inc(xT_done, 1)
                    if there(u + 1):
                        n = u + 1
                        act.wait_ge(s_full, n + 1)
                        at_least(act, p_ready, n)
                        nc.scalar.activation(in_banks(num), s_banks[:, :, 0:D], ACT.Square, scale=0.5)
                        nc.scalar.activation(in_banks(dot), s_banks[:, :, 0:D], ACT.Identity, bias=eps[:]) \
                            .then_inc(s_read, 1)
                    if there(u + 2):
                        n = u + 2
                        act.wait_ge(qk_full, n + 1)
                        at_least(act, s_full, n)
                        for m in range(KT):
                            at = P * (KT + m)
                            ins = nc.scalar.activation(kT[:, m, :], qk_bank[:, at:at + P], ACT.Identity,
                                                       bias=w["ra_bqk"][:, KT + m:KT + m + 1])
                        ins.then_inc(k_ready, 1)
                        for m in range(KT):
                            at = P * m
                            nc.scalar.activation(qm2T[:, m, :], qk_bank[:, at:at + P], ACT.Identity,
                                                 bias=bq2[:, m:m + 1], scale=-2.0)
                            ins = nc.scalar.activation(q2T[:, m, :], qk_bank[:, at:at + P], ACT.Square,
                                                       bias=w["ra_bqk"][:, m:m + 1])
                        ins.then_inc(qk_done, 1)
                    if there(u):
                        act.wait_ge(oT_full, u + 1)
                        at_least(act, y_full, u)
                        nc.scalar.copy(oT[:], t_bank[:, 0:D].rearrange("p (k t) -> p k t", k=KT)).then_inc(oT_done, 1)
                    if there(u + 2):
                        n = u + 2
                        act.wait_ge(kbd_ready[0], n + 1)
                        act.wait_ge(kbd_ready[1], n + 1)
                        nc.scalar.activation(k2bd[:], kbd[:], ACT.Square).then_inc(k2_ready, 1)
                    if there(u + 1):
                        n = u + 1
                        act.wait_ge(sub_ready, n + 1)
                        at_least(act, pT_ready, n)
                        nc.scalar.activation(prob[:], num[:], ACT.Exp).then_inc(p_ready, 1)

                slots(act, step)

            @block.tensor
            def _(pe):
                pe.wait_ge(loaded["ratio"], 16 * len(GROUPS["ratio"]))
                pe.wait_ge(sums_set, 1)

                def step(u):
                    if there(u + 1):
                        n = u + 1
                        pe.wait_ge(k2_ready, n + 1)
                        at_least(pe, den_ready, n)
                        alone(pe, passed_pe)
                        ones = lambda lo, m, b: c.ones[lo:lo + 64, :]
                        per_batch(nc, s_banks, tokens(qm2T), heads_apart(kbd), 0, True)
                        per_batch(nc, s_banks, ones, heads_apart(k2bd), D, False)
                        for m in range(KT):
                            for f in range(2):
                                lo, at = 64 * f, D + P * m
                                ins = nc.tensor.matmul(s_banks[:, f, at:at + P], q2T[lo:lo + 64, m, :],
                                                       c.headq[lo:lo + 64, :], start=False, stop=True,
                                                       skip_group_check=True)
                        ins.then_inc(s_full, 1)
                        at_least(pe, v_done, n)
                        project_tokens(nc, v_bank, xT, w["ra_qkv"][:, :, 2 * D:3 * D]).then_inc(v_full, 1)
                    if there(u + 2):
                        n = u + 2
                        pe.wait_ge(xn_ready, n + 1)
                        at_least(pe, xT_done, n)
                        turn_tokens(nc, x_bank, xn, c).then_inc(xT_full, 1)
                    if there(u):
                        pe.wait_ge(pT_ready, u + 1)
                        pe.wait_ge(vbd_ready, u + 1)
                        at_least(pe, o_done, u)
                        alone(pe, passed_pe)
                        weigh_values(nc, o_bank, pT, vbd).then_inc(o_full, 1)
                    if there(u + 2):
                        n = u + 2
                        pe.wait_ge(xT_done, n + 1)
                        at_least(pe, qk_done, n)
                        project_qk(nc, qk_bank, w["ra_qkv"], xT).then_inc(qk_full, 1)
                    if there(u):
                        pe.wait_ge(o_done, u + 1)
                        at_least(pe, oT_done, u)
                        turn_tokens(nc, t_bank, o, c).then_inc(oT_full, 1)
                        pe.wait_ge(oT_done, u + 1)
                        at_least(pe, y_done, u)
                        project_tokens(nc, y_bank, oT, w["ra_o"]).then_inc(y_full, 1)

                slots(pe, step)

            @block.vector
            def _(dve):
                def norm(n):
                    st.link(dve, nc.vector.bn_stats(stat[:], x[:, n, :]))
                    alone(dve, passed_dve)
                    st.link(dve, nc.vector.bn_aggr(mv[:], stat[:]))
                    nc.vector.tensor_scalar(veps[:], mv[:, 1:2], LN_EPS, None, ALU.add).then_inc(var_ready, 1)
                    dve.wait_ge(rstd_ready, n + 1)
                    at_least(dve, xT_full, n)
                    nc.vector.tensor_scalar(xn[:], x[:, n, :], mv[:, 0:1], rstd[:], ALU.subtract, ALU.mult) \
                        .then_inc(xn_ready, 1)

                flat = [P, NH, SQ]

                def step(u):
                    n = u + 1
                    if there(u):
                        dve.wait_ge(p_ready, u + 1)
                        at_least(dve, o_full, u)
                        alone(dve, passed_dve)
                        turn_blocks(nc, pT, prob).then_inc(pT_ready, 1)
                    if there(n):
                        dve.wait_ge(v_full, n + 1)
                        at_least(dve, vbd_ready, n)
                        nc.vector.tensor_tensor(v[:], v_bank[:, 0:D], w["ra_bv"][:], ALU.add).then_inc(v_done, 1)
                        dve.wait_ge(s_read, n + 1)
                        at_least(dve, sub_ready, n)
                        nc.vector.tensor_tensor(in_banks(den), s_banks[:, :, D:2 * D], in_banks(dot), ALU.add) \
                            .then_inc(den_ready, 1)
                        dve.wait_ge(den_ready, n + 1)
                        st.link(dve, nc.vector.reciprocal(den[:], den[:]))
                    if there(u):
                        dve.wait_ge(o_full, u + 1)
                        at_least(dve, oT_full, u)
                        st.link(dve, nc.vector.reciprocal(rden[:], sums_of(o_bank)))
                        over_sum(nc, o, o_bank, rden).then_inc(o_done, 1)
                    if there(n):
                        st.link(dve, nc.vector.tensor_tensor(num[:], num[:], den[:], ALU.mult))
                    if there(u + 2):
                        dve.wait_ge(k_ready, u + 3)
                        at_least(dve, s_full, u + 2)
                        spread_heads(nc.vector, kbd, kT, c.head, 0).then_inc(kbd_ready[0], 1)
                    if there(n):
                        st.link(dve, nc.vector.tensor_tensor(
                            num[:], num[:],
                            c.causal.unsqueeze(1).broadcast_to(flat), ALU.add))
                        st.link(dve, nc.vector.tensor_reduce(mx[:], num[:], AX.X, ALU.max))
                        nc.vector.tensor_tensor(num[:], num[:],
                                                mx[:].unsqueeze(2).broadcast_to(flat), ALU.subtract) \
                            .then_inc(sub_ready, 1)
                    if there(u + 3):
                        norm(u + 3)
                    if there(u):
                        dve.wait_ge(y_full, u + 1)
                        dve.wait_ge(bias_added, u + 1)
                        nc.vector.tensor_tensor(x[:, u, :], y_bank[:, 0:D], x[:, u, :], ALU.add).then_inc(y_done, 1)

                nc.vector.memset(eps[:], 1e-6).then_inc(consts_set, 1)
                dve.wait_ge(loaded["ratio"], 16 * len(GROUPS["ratio"]))
                nc.vector.tensor_scalar(bq2[:], w["ra_bqk"][:, 0:KT], -2.0, None, ALU.mult).then_inc(consts_set, 1)
                norm(0)
                slots(dve, step, steps=st, per=1 + 1 + 1 + 2 + 2)




def quantised_ffn(nc, a, sb_, sem, bank, c, x, wn):
    with ExitStack() as own:
        def sb(name, shape, dt=F32):
            return sb_("ff_" + name, shape, dt, own)

        def fsem(name):
            return sem("ff_" + name)

        T = NT * P
        stats, mv = sb("stats", [P, NT, 6]), sb("mv", [P, NT, 2])
        veps, rstd = sb("veps", [P, NT]), sb("rstd", [P, NT])
        xn, xT = sb("xn", [P, NT, D]), sb("xT", [P, KT, T])
        gate, up, sig = sb("gate", [P, FT, T]), sb("up", [P, FT, T]), sb("sig", [P, FT, T])
        X, G, U, H, O = range(5)
        peak, top = sb("peak", [P, 5, 2 * FT]), sb("top", [P, 5])
        topall, scale, inv = sb("topall", [P, 5]), sb("scale", [P, 5]), sb("inv", [P, 5])
        w_gate_T, w_up_T = sb("w_gate_T", [P, KT, FF]), sb("w_up_T", [P, KT, FF])
        w_down_T = sb("w_down_T", [P, FT, D])
        st = Steps(fsem("dve_steps"))
        wt_full, wt_done = fsem("wt_full"), fsem("wt_done")
        pool_steps = Steps(fsem("pool_steps"))
        veps_ready, rstd_ready = fsem("veps_ready"), fsem("rstd_ready")
        top_ready, topall_ready = [fsem(f"top_ready{i}") for i in range(5)], [fsem(f"topall_ready{i}") for i in range(5)]
        xn_ready, xT_full, xT_done = fsem("xn_ready"), fsem("xT_full"), fsem("xT_done")
        gu_full, gu_done, peak_done = fsem("gu_full"), fsem("gu_done"), fsem("peak_done")
        gate_ready, sig_ready, up_ready = fsem("gate_ready"), fsem("sig_ready"), fsem("up_ready")
        up_scale, o_ready, y_full = fsem("up_scale"), fsem("o_ready"), fsem("y_full")

        def turned(copy, n):
            src = bank[2 + n % 6][:].rearrange("p (j o) -> p j o", j=4)
            if n < 6:
                dst = (w_gate_T, w_up_T)[n // 3]
                return copy(dst[:].rearrange("p k (o q) -> p (k o) q", q=P)[:, 4 * (n % 3):4 * (n % 3) + 4, :], src)
            i = n - 6
            return copy(w_down_T[:].rearrange("p f (o q) -> p (f o) q", q=P)[:, 4 * i:4 * i + 4, :], src)

        with nc.Block() as block:
            @block.gpsimd
            def _(pool):
                pool.wait_ge(veps_ready, 1)
                nc.gpsimd.tensor_tensor(rstd[:], veps[:], c.half[:, 0:NT], ALU.pow).then_inc(rstd_ready, 1)

                def largest(i):
                    pool.wait_ge(top_ready[i], 1)
                    nc.gpsimd.partition_all_reduce(topall[:, i:i + 1], top[:, i:i + 1], P, RMAX) \
                        .then_inc(topall_ready[i], 1)

                for i in (X, G, U):
                    largest(i)
                pool.wait_ge(up_scale, 1)
                for m in range(FT):
                    pool_steps.link(pool, nc.gpsimd.tensor_scalar(up[:, m, :], up[:, m, :], inv[:, U:U + 1], ROUND,
                                                                  ALU.mult, ALU.add))
                    nc.gpsimd.tensor_scalar(up[:, m, :], up[:, m, :], -ROUND, scale[:, U:U + 1],
                                            ALU.add, ALU.mult).then_inc(up_ready, 1)
                for i in (H, O):
                    largest(i)

            @block.scalar
            def _(act):
                for n in range(9):
                    act.wait_ge(wt_full, n + 1)
                    turned(nc.scalar.copy, n).then_inc(wt_done, 1)
                for i in range(NT // 2):
                    act.wait_ge(xT_full, i + 1)
                    src = bank[i % 2][:].rearrange("p (j k t) -> p j k t", j=2, k=KT)
                    for j in range(2):
                        at = P * (2 * i + j)
                        ins = nc.scalar.copy(xT[:, :, at:at + P], src[:, j, :, :])
                    ins.then_inc(xT_done, 1)
                for n in range(4 * FT):
                    act.wait_ge(gu_full, n + 1)
                    dst = (gate, up)[n // (2 * FT)]
                    m, h = n // 2 % FT, n % 2
                    nc.scalar.copy(dst[:, m, 512 * h:512 * h + 512], bank[2 + n % 6][:]).then_inc(gu_done, 1)
                for m in range(FT):
                    act.wait_ge(gate_ready, m + 1)
                    nc.scalar.activation(sig[:, m, :], gate[:, m, :], ACT.Sigmoid).then_inc(sig_ready, 1)

            @block.tensor
            def _(pe):
                wgu = wn[:].rearrange("p (j b) q -> p j (b q)", j=3)
                for n in range(9):
                    at_least(pe, wt_done, n - 5)
                    for j in range(4):
                        if n < 6:
                            i = 4 * (n % 3) + j
                            src = wgu[:, n // 3, :].rearrange("p (o k q) -> p k o q", o=FT, k=KT)[:, i // FT, i % FT, :]
                        else:
                            i = 4 * (n - 6) + j
                            src = wgu[:, 2, :].rearrange("p (o f q) -> p f o q", o=KT, f=FT)[:, i // KT, i % KT, :]
                        ins = nc.tensor.transpose(bank[2 + n % 6][:, P * j:P * j + P], src, c.ident)
                    ins.then_inc(wt_full, 1)
                for i in range(NT // 2):
                    pe.wait_ge(xn_ready, i + 1)
                    at_least(pe, xT_done, i - 1)
                    for j in range(2):
                        ins = turn_tokens(nc, bank[i % 2][:, D * j:D * j + D], xn[:, 2 * i + j, :], c)
                    ins.then_inc(xT_full, 1)
                pe.wait_ge(xT_done, NT // 2)
                pe.wait_ge(wt_done, 9)
                for n in range(4 * FT):
                    wt = (w_gate_T, w_up_T)[n // (2 * FT)]
                    m, h = n // 2 % FT, n % 2
                    at_least(pe, gu_done, n - 5)
                    for k in range(KT):
                        ins = nc.tensor.matmul(bank[2 + n % 6][:], wt[:, k, P * m:P * m + P],
                                               xT[:, k, 512 * h:512 * h + 512], start=(k == 0), stop=(k == KT - 1))
                    ins.then_inc(gu_full, 1)
                pe.wait_ge(gu_done, 4 * FT)
                pe.wait_ge(o_ready, 2 * FT)
                for t in range(NT):
                    for f in range(FT):
                        ins = nc.tensor.matmul(bank[t][:, 0:D], gate[:, f, P * t:P * t + P], w_down_T[:, f, :],
                                               start=(f == 0), stop=(f == FT - 1))
                    ins.then_inc(y_full, 1)

            @block.vector
            def _(dve):
                for t in range(NT):
                    ins = nc.vector.bn_stats(stats[:, t, :], x[:, t, :])
                st.link(dve, ins)
                for t in range(NT):
                    ins = nc.vector.bn_aggr(mv[:, t, :], stats[:, t, :])
                st.link(dve, ins)
                nc.vector.tensor_scalar(veps[:], mv[:, :, 1], LN_EPS, None, ALU.add).then_inc(veps_ready, 1)
                dve.wait_ge(rstd_ready, 1)
                for t in range(NT):
                    ins = nc.vector.tensor_scalar(xn[:, t, :], x[:, t, :], mv[:, t, 0:1], rstd[:, t:t + 1],
                                                  ALU.subtract, ALU.mult)
                st.link(dve, ins)

                def scales(i, n):
                    nc.vector.tensor_reduce(top[:, i:i + 1], peak[:, i, 0:n], AX.X, ALU.max).then_inc(top_ready[i], 1)
                    dve.wait_ge(topall_ready[i], 1)
                    st.link(dve, nc.vector.tensor_scalar(scale[:, i:i + 1], topall[:, i:i + 1], 1.0 / 32767.0, 1e-12,
                                                         ALU.mult, ALU.max))
                    st.link(dve, nc.vector.reciprocal(inv[:, i:i + 1], scale[:, i:i + 1]))

                def rounded(piece, i):
                    st.link(dve, nc.vector.tensor_scalar(piece, piece, inv[:, i:i + 1], ROUND, ALU.mult, ALU.add))
                    return nc.vector.tensor_scalar(piece, piece, ROUND, scale[:, i:i + 1], ALU.subtract, ALU.mult)

                def magnitude(i, n, piece):
                    return nc.vector.tensor_reduce(peak[:, i, n:n + 1], piece, AX.XY if len(piece.shape) == 3 else AX.X,
                                                   ALU.max, apply_absolute_value=True)

                st.link(dve, magnitude(X, 0, xn[:]))
                scales(X, 1)
                for i in range(NT // 2):
                    rounded(xn[:, 2 * i:2 * i + 2, :], X).then_inc(xn_ready, 1)
                for n in range(4 * FT):
                    dve.wait_ge(gu_done, n + 1)
                    src = (gate, up)[n // (2 * FT)]
                    m, h = n // 2 % FT, n % 2
                    ins = magnitude((G, U)[n // (2 * FT)], n % (2 * FT), src[:, m, 512 * h:512 * h + 512])
                    if n % (2 * FT) == 2 * FT - 1:
                        st.link(dve, ins)
                        scales((G, U)[n // (2 * FT)], 2 * FT)
                        if n // (2 * FT) == 0:
                            for k in range(FT):
                                rounded(gate[:, k, :], G).then_inc(gate_ready, 1)
                dve.sem_inc(up_scale, 1)
                for m in range(FT):
                    dve.wait_ge(sig_ready, m + 1)
                    st.link(dve, nc.vector.tensor_scalar(sig[:, m, :], sig[:, m, :], 65536.0, ROUND, ALU.mult, ALU.add))
                    st.link(dve, nc.vector.tensor_scalar(sig[:, m, :], sig[:, m, :], ROUND, 65535.0,
                                                         ALU.subtract, ALU.min))
                    st.link(dve, nc.vector.scalar_tensor_tensor(gate[:, m, :], sig[:, m, :], 1.0 / 65536.0, gate[:, m, :],
                                                                ALU.mult, ALU.mult))
                    st.link(dve, magnitude(H, m, gate[:, m, :]))
                scales(H, FT)
                for m in range(FT):
                    st.link(dve, rounded(gate[:, m, :], H))
                    dve.wait_ge(up_ready, m + 1)
                    st.link(dve, nc.vector.tensor_tensor(gate[:, m, :], gate[:, m, :], up[:, m, :], ALU.mult))
                    st.link(dve, magnitude(O, m, gate[:, m, :]))
                scales(O, FT)
                for m in range(FT):
                    for h in range(2):
                        rounded(gate[:, m, 512 * h:512 * h + 512], O).then_inc(o_ready, 1)
                for t in range(NT):
                    dve.wait_ge(y_full, t + 1)
                    nc.vector.tensor_tensor(x[:, t, :], bank[t][:, 0:D], x[:, t, :], ALU.add)


def two_stage(eng, step, steps=None, per=None):
    step(-1)
    step(0)
    with eng.Fori(1, NT - 2) as u:
        if steps:
            steps.enter(u, 1, per)
        step(u)
        if steps:
            steps.leave(NT - 3)
    step(NT - 2)
    step(NT - 1)


def context_attention(nc, a, sb_, sem, bank, c, x, w, loaded):
    with ExitStack() as own:
        def sb(name, shape, dt=F32):
            return sb_("cx_" + name, shape, dt, own)

        def csem(name):
            return sem("cx_" + name)

        SCALE = D ** -0.5
        xn, xT = sb("xn", [P, D]), sb("xT", [P, KT, P])
        stat, mv, veps, rstd = sb("stat", [P, 6]), sb("mv", [P, 2]), sb("veps", [P, 1]), sb("rstd", [P, 1])
        ctxT = [sb(f"ctxT{b}", [P, KT, SK]) for b in range(BT)]
        cn = [sb(f"ctx{b}", [P, 2, D]) for b in range(BT)]
        last = sb("last", [BT, D])
        qT, qk, qb = sb("qT", [P, KT, P]), sb("qk", [P, KT, P]), sb("qb", [P, 1])
        mx, nb = sb("mx", [P, 1]), sb("nb", [P, 1])
        raw, esum, rden = sb("raw", [P, SK]), sb("esum", [P, 1]), sb("rden", [P, 1])
        prob, plast = sb("prob", [P, SK]), sb("plast", [P, BT])
        pT, plT = sb("pT", [P, 2, P]), sb("plT", [BT, P])
        aT, y = sb("aT", [P, KT, P]), sb("y", [P, D])
        x_bank, q_bank, k_bank, s_bank, p_bank, a_bank, y_bank = bank[0:7]

        st = Steps(csem("dve_steps"))
        passed_dve, passed_sp = csem("passed_dve"), csem("passed_sp")
        ctxT_loaded = [csem(f"ctxT_loaded{b}") for b in range(BT)]
        ctx_loaded = [csem(f"ctx_loaded{b}") for b in range(BT)]
        last_loaded = csem("last_loaded")
        var_ready, rstd_ready, xn_ready = csem("var_ready"), csem("rstd_ready"), csem("xn_ready")
        xT_full, xT_done, q_full, q_done = csem("xT_full"), csem("xT_done"), csem("q_full"), csem("q_done")
        k_full, k_done, qb_ready = csem("k_full"), csem("k_done"), csem("qb_ready")
        s_full, nb_ready, e_ready = csem("s_full"), csem("nb_ready"), csem("e_ready")
        p_ready, p_full, p_done = csem("p_ready"), csem("p_full"), csem("p_done")
        a_full, a_done, y_full, y_done = csem("a_full"), csem("a_done"), csem("y_full"), csem("y_done")

        with nc.Block() as block:
            @block.sync
            def _(sp):
                def turned(t):
                    for b in range(BT):
                        sp.dma_start(ctxT[b][:], a["ctx_T"][BT * t + b]).then_inc(ctxT_loaded[b], 16)

                def plain(t):
                    for b in range(BT):
                        sp.dma_start(cn[b][:], a["ctx"][BT * t + b, 0:SK - 1, :].rearrange("(i p) d -> p i d", p=P)) \
                            .then_inc(ctx_loaded[b], 16)
                    sp.dma_start(last[:], a["ctx_rows"][t]).then_inc(last_loaded, 16)

                turned(0)
                plain(0)
                with sp.Fori(1, NT) as t:
                    sp.wait_ge(s_full, t)
                    alone(sp, passed_sp)
                    turned(t)
                    sp.wait_ge(a_full, t)
                    alone(sp, passed_sp)
                    plain(t)

            @block.gpsimd
            def _(pool):
                def step(u):
                    if there(u + 2):
                        pool.wait_ge(var_ready, u + 3)
                        nc.gpsimd.tensor_tensor(rstd[:], veps[:], c.half[:, 0:1], ALU.pow).then_inc(rstd_ready, 1)

                pool.wait_ge(var_ready, 1)
                nc.gpsimd.tensor_tensor(rstd[:], veps[:], c.half[:, 0:1], ALU.pow).then_inc(rstd_ready, 1)
                two_stage(pool, step)

            @block.scalar
            def _(act):
                act.wait_ge(loaded["cross"], 16 * len(GROUPS["cross"]))

                def step(u):
                    n = u + 1
                    if there(n):
                        act.wait_ge(xT_full, n + 1)
                        nc.scalar.copy(xT[:], x_bank[:, 0:D].rearrange("p (k t) -> p k t", k=KT)).then_inc(xT_done, 1)
                        act.wait_ge(q_full, n + 1)
                        for m in range(KT):
                            ins = nc.scalar.activation(qT[:, m, :], q_bank[:, P * m:P * m + P], ACT.Identity,
                                                       bias=w["cx_bq"][:, m:m + 1])
                        ins.then_inc(q_done, 1)
                    if there(u):
                        act.wait_ge(p_full, u + 1)
                        at_least(act, a_full, u)
                        nc.scalar.copy(pT[:], p_bank[:, 0:2 * P].rearrange("p (i t) -> p i t", i=2))
                        nc.scalar.copy(plT[:], p_bank[0:BT, 2 * P:3 * P]).then_inc(p_done, 1)
                    if there(n):
                        act.wait_ge(k_full, n + 1)
                        at_least(act, qb_ready, n)
                        at_least(act, s_full, n)
                        nc.scalar.copy(qk[:], k_bank[:, 0:D].rearrange("p (k t) -> p k t", k=KT))
                        nc.scalar.mul(qb[:], k_bank[:, D:D + 1], SCALE).then_inc(k_done, 1)
                    if there(u):
                        act.wait_ge(a_full, u + 1)
                        nc.scalar.copy(aT[:], a_bank[:, 0:D].rearrange("p (k t) -> p k t", k=KT)).then_inc(a_done, 1)
                    if there(n):
                        act.wait_ge(nb_ready, n + 1)
                        at_least(act, p_ready, n)
                        nc.scalar.activation(raw[:], s_bank[:, 0:SK], ACT.Exp, bias=nb[:], scale=SCALE,
                                             accum_out=esum[:]).then_inc(e_ready, 1)

                two_stage(act, step)

            @block.tensor
            def _(pe):
                pe.wait_ge(loaded["cross"], 16 * len(GROUPS["cross"]))

                def step(u):
                    n = u + 1
                    if there(n):
                        pe.wait_ge(xn_ready, n + 1)
                        at_least(pe, xT_done, n)
                        turn_tokens(nc, x_bank, xn, c).then_inc(xT_full, 1)
                        pe.wait_ge(xT_done, n + 1)
                        at_least(pe, q_done, n)
                        for m in range(KT):
                            for k in range(KT):
                                ins = nc.tensor.matmul(q_bank[:, P * m:P * m + P], w["cx_q"][:, k, P * m:P * m + P],
                                                       xT[:, k, :], start=(m == 0 and k == 0), stop=True,
                                                       skip_group_check=True)
                        ins.then_inc(q_full, 1)
                    if there(u):
                        pe.wait_ge(p_ready, u + 1)
                        at_least(pe, p_done, u)
                        for i in range(2):
                            nc.tensor.transpose(p_bank[:, P * i:P * i + P], prob[:, P * i:P * i + P], c.ident)
                        nc.tensor.transpose(p_bank[0:BT, 2 * P:3 * P], plast[:], c.ident).then_inc(p_full, 1)
                    if there(n):
                        pe.wait_ge(q_done, n + 1)
                        at_least(pe, k_done, n)
                        for m in range(KT):
                            for k in range(KT):
                                nc.tensor.matmul(k_bank[:, P * m:P * m + P], w["cx_k"][:, k, P * m:P * m + P],
                                                 qT[:, k, :], start=(m == 0 and k == 0), stop=True,
                                                 skip_group_check=True)
                        for k in range(KT):
                            ins = nc.tensor.matmul(k_bank[:, D:D + 1], qT[:, k, :], w["cx_bk"][:, k:k + 1],
                                                   start=False, stop=True, skip_group_check=True)
                        ins.then_inc(k_full, 1)
                    if there(u):
                        pe.wait_ge(p_done, u + 1)
                        at_least(pe, a_done, u)
                        for b in range(BT):
                            pe.wait_ge(ctx_loaded[b], 16 * (u + 1))
                            for m in range(KT):
                                for i in range(2):
                                    at = P * m + SQ * b
                                    nc.tensor.matmul(a_bank[:, at:at + SQ], cn[b][:, i, P * m:P * m + P],
                                                     pT[:, i, SQ * b:SQ * b + SQ],
                                                     start=(b == 0 and m == 0 and i == 0), stop=False,
                                                     skip_group_check=True)
                        pe.wait_ge(last_loaded, 16 * (u + 1))
                        for m in range(KT):
                            ins = nc.tensor.matmul(a_bank[:, P * m:P * m + P], last[:, P * m:P * m + P], plT[:],
                                                   start=False, stop=True, skip_group_check=True)
                        ins.then_inc(a_full, 1)
                    if there(n):
                        pe.wait_ge(k_done, n + 1)
                        at_least(pe, e_ready, n)
                        for b in range(BT):
                            pe.wait_ge(ctxT_loaded[b], 16 * (n + 1))
                            for k in range(KT):
                                ins = nc.tensor.matmul(s_bank[SQ * b:SQ * b + SQ, 0:SK], qk[:, k, SQ * b:SQ * b + SQ],
                                                       ctxT[b][:, k, :], start=(k == 0), stop=(k == KT - 1))
                        ins.then_inc(s_full, 1)
                    if there(u):
                        pe.wait_ge(a_done, u + 1)
                        at_least(pe, y_done, u)
                        project_tokens(nc, y_bank, aT, w["cx_v"]).then_inc(y_full, 1)

                two_stage(pe, step)

            @block.vector
            def _(dve):
                def norm(u):
                    st.link(dve, nc.vector.bn_stats(stat[:], x[:, u, :]))
                    alone(dve, passed_dve)
                    st.link(dve, nc.vector.bn_aggr(mv[:], stat[:]))
                    nc.vector.tensor_scalar(veps[:], mv[:, 1:2], LN_EPS, None, ALU.add).then_inc(var_ready, 1)
                    dve.wait_ge(rstd_ready, u + 1)
                    at_least(dve, xT_full, u)
                    nc.vector.tensor_scalar(xn[:], x[:, u, :], mv[:, 0:1], rstd[:], ALU.subtract, ALU.mult) \
                        .then_inc(xn_ready, 1)

                def step(u):
                    n = u + 1
                    if there(u + 2) and not (isinstance(u, int) and u < 0):
                        norm(u + 2)
                    if there(n):
                        dve.wait_ge(s_full, n + 1)
                        dve.wait_ge(k_done, n + 1)
                        at_least(dve, e_ready, n)
                        st.link(dve, nc.vector.tensor_reduce(mx[:], s_bank[:, 0:SK], AX.X, ALU.max))
                        st.link(dve, nc.vector.tensor_scalar(mx[:], mx[:], SCALE, qb[:], ALU.mult, ALU.add))
                        nc.vector.tensor_tensor(nb[:], qb[:], mx[:], ALU.subtract).then_inc(nb_ready, 1)
                        dve.wait_ge(e_ready, n + 1)
                        at_least(dve, p_full, n)
                        st.link(dve, nc.vector.reciprocal(rden[:], esum[:]))
                        st.link(dve, nc.vector.tensor_scalar(prob[:], raw[:], rden[:], None, ALU.mult))
                        nc.vector.tensor_scalar(plast[:], c.row, prob[:, SK - 1:SK], None, ALU.mult) \
                            .then_inc(p_ready, 1)
                        dve.sem_inc(qb_ready, 1)
                    if there(u):
                        dve.wait_ge(y_full, u + 1)
                        st.link(dve, nc.vector.tensor_tensor(y[:], y_bank[:, 0:D], w["cx_bv"][:], ALU.add))
                        nc.vector.tensor_tensor(x[:, u, :], x[:, u, :], y[:], ALU.add).then_inc(y_done, 1)

                dve.wait_ge(loaded["cross"], 16 * len(GROUPS["cross"]))
                norm(0)
                norm(1)
                two_stage(dve, step, steps=st, per=2 + 4 + 1)
def segment_attention(nc, a, sb_, sem, psum, bank, c, x, w, loaded):
    with ExitStack() as own:
        def sb(name, shape, dt=F32):
            return sb_("sg_" + name, shape, dt, own)

        def gsem(name):
            return sem("sg_" + name)

        kinds = ("lt", "st")
        xn, xT = sb("xn", [P, D]), sb("xT", [P, KT, P])
        stat, mv, veps, rstd = sb("stat", [P, 6]), sb("mv", [P, 2]), sb("veps", [P, 1]), sb("rstd", [P, 1])
        qT, kT = sb("qT", [P, KT, P]), sb("kT", [P, KT, P])
        v, vbd, kbd = sb("v", [P, D]), sb("vbd", [P, BT, NH, 17]), sb("kbd", [P, KT, BT, 4, SQ])
        score, prob, pT = (sb(name, [P, NH, SQ]) for name in ("score", "prob", "pT"))
        mx, rden, o, oT = sb("mx", [P, NH]), sb("rden", [P, NH]), sb("o", [P, D]), sb("oT", [P, KT, P])
        longT, shortT, short = sb("longT", [P, KT, P]), sb("shortT", [P, KT, P]), sb("short", [P, D])
        lmax, first, chosen = sb("lmax", [P, 1]), sb("first", [P, NE]), sb("chosen", [P, 1])
        onehot, hotT = sb("onehot", [P, NE]), sb("hotT", [NE, P])
        same, shut = sb("same", [P, SQ]), sb("shut", [P, SQ])
        count, single, several = sb("count", [P, 1]), sb("single", [P, 1]), sb("several", [P, 1])
        x_single = sb("x_single", [P, D])
        s_banks, qk_bank, o_bank = psum[:, 0:2, :], bank[3], bank[5]
        x_part, logits, hot_part = bank[2][:, 0:D], bank[2][:, D:D + NE], bank[2][0:NE, 3 * P:4 * P]
        v_part, same_part = bank[4][:, 0:D], bank[4][:, D:D + SQ]
        t_part, short_part = bank[6][:, 0:D], bank[6][:, D:2 * D]
        y_part, fused_part = bank[7][:, 0:D], bank[7][:, D:2 * D]

        st = Steps(gsem("dve_steps"))
        passed_dve, passed_pool, passed_pe = gsem("passed_dve"), gsem("passed_pool"), gsem("passed_pe")
        var_ready, rstd_ready, xn_ready = gsem("var_ready"), gsem("rstd_ready"), gsem("xn_ready")
        xT_full, xT_done, logits_full, hot_ready = gsem("xT_full"), gsem("xT_done"), gsem("logits_full"), gsem("hot_ready")
        hot_full, hot_done, same_full, same_done = gsem("hot_full"), gsem("hot_done"), gsem("same_full"), gsem("same_done")
        short_ready, shT_full, shT_done = gsem("short_ready"), gsem("shT_full"), gsem("shT_done")
        fused_read = gsem("fused_read")
        fused_full, bias_added, sums_set = gsem("fused_full"), gsem("bias_added"), gsem("sums_set")
        qk_full, k_ready, qk_done = gsem("qk_full"), gsem("k_ready"), gsem("qk_done")
        kbd_ready = [gsem("kbd0_ready"), gsem("kbd1_ready")]
        v_full, v_done, vbd_ready = gsem("v_full"), gsem("v_done"), gsem("vbd_ready")
        s_full, sub_ready, p_ready, pT_ready = gsem("s_full"), gsem("sub_ready"), gsem("p_ready"), gsem("pT_ready")
        o_full, o_done, oT_full, oT_done = gsem("o_full"), gsem("o_done"), gsem("oT_full"), gsem("oT_done")
        y_full, y_done = gsem("y_full"), gsem("y_done")

        def steps_of_tiles(eng, step, steps=None, per=None):
            for t in (-1, 0):
                for s in range(2):
                    step(t, s)
            with eng.Fori(1, NT - 2) as t:
                if steps:
                    steps.enter(t, 1, per)
                for s in range(2):
                    step(t, s)
                if steps:
                    steps.leave(NT - 3)
            for t in range(NT - 2, NT + 1):
                for s in range(2):
                    step(t, s)

        def parts(t, s):
            return there(t), there(t + s), there(t + 1)

        with nc.Block() as block:
            @block.gpsimd
            def _(pool):
                for b in range(BT):
                    ins = nc.gpsimd.tensor_copy(vbd[:, b, :, DH], c.row[:, b:b + 1].broadcast_to([P, NH]))
                ins.then_inc(sums_set, 1)

                def root(t):
                    pool.wait_ge(var_ready, t + 1)
                    nc.gpsimd.tensor_tensor(rstd[:], veps[:], c.half[:, 0:1], ALU.pow).then_inc(rstd_ready, 1)

                def step(t, s):
                    u = 2 * t + s
                    has_c, has_b, has_a = parts(t, s)
                    if has_b:
                        pool.wait_ge(v_done, u + 2)
                        at_least(pool, o_full, u + 1)
                        alone(pool, passed_pool)
                        spread_batches(nc.gpsimd, vbd, v, c).then_inc(vbd_ready, 1)
                    if has_a:
                        pool.wait_ge(k_ready, u + 3)
                        at_least(pool, s_full, u + 2)
                        alone(pool, passed_pool)
                        spread_heads(nc.gpsimd, kbd, kT, c.quarter, 1).then_inc(kbd_ready[1], 1)
                    if s == 0 and has_a:
                        pool.wait_ge(xn_ready, t + 2)
                        alone(pool, passed_pool)
                        nc.gpsimd.tensor_tensor(x[:, t + 1, :], x[:, t + 1, :], w["fus_b"][:], ALU.add) \
                            .then_inc(bias_added, 1)
                    if s == 1 and has_a and there(t + 2):
                        root(t + 2)

                pool.wait_ge(loaded["segs"], 16 * len(GROUPS["segs"]))
                root(0)
                steps_of_tiles(pool, step)

            @block.scalar
            def _(act):
                act.wait_ge(loaded["segs"], 16 * len(GROUPS["segs"]))

                def step(t, s):
                    u = 2 * t + s
                    has_c, has_b, has_a = parts(t, s)
                    if s == 0 and has_a:
                        act.wait_ge(xT_full, t + 2)
                        at_least(act, v_full, u + 2)
                        at_least(act, qk_full, u + 2)
                        nc.scalar.copy(xT[:], x_part.rearrange("p (k t) -> p k t", k=KT)).then_inc(xT_done, 1)
                    if s == 0 and there(t - 1):
                        act.wait_ge(shT_full, t)
                        nc.scalar.copy(shortT[:], short_part.rearrange("p (k t) -> p k t", k=KT)).then_inc(shT_done, 1)
                    if has_a:
                        bias = w[kinds[s] + "_bqk"]
                        act.wait_ge(qk_full, u + 3)
                        at_least(act, s_full, u + 2)
                        for m in range(KT):
                            at = P * (KT + m)
                            ins = nc.scalar.activation(kT[:, m, :], qk_bank[:, at:at + P], ACT.Identity,
                                                       bias=bias[:, KT + m:KT + m + 1])
                        ins.then_inc(k_ready, 1)
                        for m in range(KT):
                            ins = nc.scalar.activation(qT[:, m, :], qk_bank[:, P * m:P * m + P], ACT.Identity,
                                                       bias=bias[:, m:m + 1])
                        ins.then_inc(qk_done, 1)
                    if s == 1 and has_a:
                        act.wait_ge(hot_full, t + 2)
                        nc.scalar.copy(hotT[:], hot_part).then_inc(hot_done, 1)
                    if has_c:
                        act.wait_ge(oT_full, u + 1)
                        at_least(act, y_full, u)
                        nc.scalar.copy(oT[:], t_part.rearrange("p (k t) -> p k t", k=KT)).then_inc(oT_done, 1)
                    if has_b:
                        act.wait_ge(sub_ready, u + 2)
                        at_least(act, pT_ready, u + 1)
                        nc.scalar.activation(prob[:], score[:], ACT.Exp).then_inc(p_ready, 1)
                    if has_c and s == 0:
                        act.wait_ge(y_full, u + 1)
                        at_least(act, fused_full, t)
                        for m in range(KT):
                            ins = nc.scalar.activation(longT[:, m, :], y_part[:, P * m:P * m + P], ACT.Identity,
                                                       bias=w["lt_bo"][:, m:m + 1])
                        ins.then_inc(y_done, 1)

                steps_of_tiles(act, step)

            @block.tensor
            def _(pe):
                pe.wait_ge(loaded["segs"], 16 * len(GROUPS["segs"]))
                pe.wait_ge(sums_set, 1)

                def step(t, s):
                    u = 2 * t + s
                    has_c, has_b, has_a = parts(t, s)
                    if has_b:
                        weight = w[kinds[1 - s] + "_qkv"]
                        pe.wait_ge(kbd_ready[0], u + 2)
                        pe.wait_ge(kbd_ready[1], u + 2)
                        pe.wait_ge(qk_done, u + 2)
                        at_least(pe, sub_ready, u + 1)
                        alone(pe, passed_pe)
                        per_batch(nc, s_banks, tokens(qT), heads_apart(kbd), 0, True).then_inc(s_full, 1)
                        at_least(pe, v_done, u + 1)
                        if s == 0:
                            at_least(pe, same_done, t + 1)
                        project_tokens(nc, v_part, xT, weight[:, :, 2 * D:3 * D]).then_inc(v_full, 1)
                    if s == 0 and has_a:
                        pe.wait_ge(xn_ready, t + 2)
                        at_least(pe, hot_done, t + 1)
                        turn_tokens(nc, x_part, xn, c).then_inc(xT_full, 1)
                    if s == 0 and there(t - 1):
                        pe.wait_ge(short_ready, t)
                        pe.wait_ge(oT_done, u)
                        turn_tokens(nc, short_part, short, c).then_inc(shT_full, 1)
                    if has_c:
                        pe.wait_ge(pT_ready, u + 1)
                        pe.wait_ge(vbd_ready, u + 1)
                        at_least(pe, o_done, u)
                        alone(pe, passed_pe)
                        weigh_values(nc, o_bank, pT, vbd).then_inc(o_full, 1)
                    if s == 1 and has_a:
                        pe.wait_ge(hot_ready, t + 2)
                        nc.tensor.transpose(hot_part, onehot[:], c.ident).then_inc(hot_full, 1)
                    if has_a:
                        if s == 0:
                            pe.wait_ge(xT_done, t + 2)
                        at_least(pe, qk_done, u + 2)
                        project_qk(nc, qk_bank, w[kinds[s] + "_qkv"], xT).then_inc(qk_full, 1)
                    if s == 0 and has_a:
                        for k in range(KT):
                            ins = nc.tensor.matmul(logits, xT[:, k, :], w["protos"][:, k, :],
                                                   start=(k == 0), stop=(k == KT - 1))
                        ins.then_inc(logits_full, 1)
                    if s == 0 and there(t - 1):
                        pe.wait_ge(shT_done, t)
                        pe.wait_ge(y_done, u)
                        for k in range(2 * KT):
                            lhs = (longT if k < KT else shortT)[:, k % KT, :]
                            ins = nc.tensor.matmul(fused_part, lhs, w["fus"][:, k, :],
                                                   start=(k == 0), stop=(k == 2 * KT - 1))
                        ins.then_inc(fused_full, 1)
                    if s == 1 and has_a:
                        pe.wait_ge(hot_done, t + 2)
                        pe.wait_ge(v_done, u + 2)
                        alone(pe, passed_pe)
                        for b in range(BT):
                            ins = nc.tensor.matmul(same_part[SQ * b:SQ * b + SQ, :], hotT[:, SQ * b:SQ * b + SQ],
                                                   hotT[:, SQ * b:SQ * b + SQ], start=True, stop=True,
                                                   skip_group_check=True)
                        ins.then_inc(same_full, 1)
                    if has_c:
                        pe.wait_ge(o_done, u + 1)
                        at_least(pe, oT_done, u)
                        turn_tokens(nc, t_part, o, c).then_inc(oT_full, 1)
                        pe.wait_ge(oT_done, u + 1)
                        at_least(pe, y_done, u)
                        if s == 0:
                            at_least(pe, fused_read, t)
                            for m in range(KT):
                                for k in range(KT):
                                    ins = nc.tensor.matmul(y_part[:, P * m:P * m + P],
                                                           w["lt_o"][:, k, P * m:P * m + P], oT[:, k, :],
                                                           start=(m == 0 and k == 0), stop=True, skip_group_check=True)
                            ins.then_inc(y_full, 1)
                        else:
                            project_tokens(nc, y_part, oT, w["st_o"]).then_inc(y_full, 1)

                steps_of_tiles(pe, step)

            @block.vector
            def _(dve):
                def norm(t):
                    st.link(dve, nc.vector.bn_stats(stat[:], x[:, t, :]))
                    alone(dve, passed_dve)
                    st.link(dve, nc.vector.bn_aggr(mv[:], stat[:]))
                    nc.vector.tensor_scalar(veps[:], mv[:, 1:2], LN_EPS, None, ALU.add).then_inc(var_ready, 1)
                    dve.wait_ge(rstd_ready, t + 1)
                    at_least(dve, xT_full, t)
                    nc.vector.tensor_scalar(xn[:], x[:, t, :], mv[:, 0:1], rstd[:], ALU.subtract, ALU.mult) \
                        .then_inc(xn_ready, 1)

                flat = [P, NH, SQ]

                def maximum_off(n):
                    st.link(dve, nc.vector.tensor_reduce(mx[:], score[:], AX.X, ALU.max))
                    nc.vector.tensor_tensor(score[:], score[:], mx[:].unsqueeze(2).broadcast_to(flat), ALU.subtract) \
                        .then_inc(sub_ready, 1)

                def step(t, s):
                    u = 2 * t + s
                    has_c, has_b, has_a = parts(t, s)
                    if has_c:
                        dve.wait_ge(p_ready, u + 1)
                        at_least(dve, o_full, u)
                        alone(dve, passed_dve)
                        turn_blocks(nc, pT, prob).then_inc(pT_ready, 1)
                    if has_b:
                        dve.wait_ge(v_full, u + 2)
                        at_least(dve, vbd_ready, u + 1)
                        nc.vector.tensor_tensor(v[:], v_part, w[kinds[1 - s] + "_bv"][:], ALU.add).then_inc(v_done, 1)
                        dve.wait_ge(s_full, u + 2)
                        at_least(dve, p_ready, u + 1)
                        in_heads = "p f (n k) -> p f n k"
                        banks = s_banks[:, :, 0:D].rearrange(in_heads, k=SQ)
                        each = [P, 2, NH // 2, SQ]
                        if s == 0:
                            for f in range(2):
                                ins = nc.vector.tensor_tensor(
                                    score[:, 8 * f:8 * f + 8, :], banks[:, f, :, :],
                                    same[:].unsqueeze(1).broadcast_to([P, NH // 2, SQ]), ALU.mult)
                                if f == 0:
                                    st.done(ins)
                            st.link(dve, ins)
                            st.link(dve, nc.vector.tensor_tensor(score[:], score[:],
                                                                 shut[:].unsqueeze(1).broadcast_to(flat), ALU.add))
                            maximum_off(u + 1)
                        else:
                            st.link(dve, nc.vector.tensor_reduce(mx[:].rearrange("p (f n) -> p f n", f=2), banks,
                                                                 AX.X, ALU.max))
                            nc.vector.tensor_tensor(
                                score[:].rearrange("p (f n) k -> p f n k", f=2), banks,
                                mx[:].rearrange("p (f n) -> p f n", f=2).unsqueeze(3).broadcast_to(each),
                                ALU.subtract).then_inc(sub_ready, 1)
                    if has_c:
                        dve.wait_ge(o_full, u + 1)
                        at_least(dve, oT_full, u)
                        st.link(dve, nc.vector.reciprocal(rden[:], sums_of(o_bank)))
                        over_sum(nc, o, o_bank, rden).then_inc(o_done, 1)
                    if has_a:
                        dve.wait_ge(k_ready, u + 3)
                        at_least(dve, s_full, u + 2)
                        spread_heads(nc.vector, kbd, kT, c.quarter, 0).then_inc(kbd_ready[0], 1)
                    if s == 0 and has_a:
                        dve.wait_ge(logits_full, t + 2)
                        st.link(dve, nc.vector.tensor_reduce(lmax[:], logits, AX.X, ALU.max))
                        st.link(dve, nc.vector.tensor_scalar(first[:], logits, lmax[:], None, ALU.is_ge))
                        st.link(dve, nc.vector.tensor_tensor(first[:], first[:], c.exp8, ALU.mult))
                        st.link(dve, nc.vector.tensor_reduce(chosen[:], first[:], AX.X, ALU.min))
                        nc.vector.tensor_scalar(onehot[:], c.exp8, chosen[:], None, ALU.is_equal).then_inc(hot_ready, 1)
                    if s == 0 and there(t - 1):
                        dve.wait_ge(fused_full, t)
                        dve.wait_ge(bias_added, t)
                        nc.vector.tensor_tensor(x[:, t - 1, :], fused_part, x[:, t - 1, :], ALU.add) \
                            .then_inc(fused_read, 1)
                    if has_c and s == 1:
                        dve.wait_ge(y_full, u + 1)
                        at_least(dve, shT_full, t)
                        nc.vector.tensor_tensor(short[:], y_part, w["st_bo"][:], ALU.add).then_inc(y_done, 1)
                        dve.wait_ge(y_done, u + 1)
                        nc.vector.scalar_tensor_tensor(short[:], short[:], several[:], x_single[:], ALU.mult, ALU.add) \
                            .then_inc(short_ready, 1)
                        dve.wait_ge(short_ready, t + 1)
                    if s == 1 and has_a:
                        dve.wait_ge(same_full, t + 2)
                        nc.vector.tensor_copy(same[:], same_part).then_inc(same_done, 1)
                        dve.wait_ge(same_done, t + 2)
                        st.link(dve, nc.vector.tensor_scalar(shut[:], same[:], 1.0, 1e9, ALU.subtract, ALU.mult))
                        st.link(dve, nc.vector.tensor_reduce(count[:], same[:], AX.X, ALU.add))
                        st.link(dve, nc.vector.tensor_scalar(single[:], count[:], 1.0, None, ALU.is_equal))
                        st.link(dve, nc.vector.tensor_scalar(several[:], single[:], -1.0, 1.0, ALU.mult, ALU.add))
                        st.link(dve, nc.vector.tensor_scalar(x_single[:], xn[:], single[:], None, ALU.mult))
                        if there(t + 2):
                            norm(t + 2)

                dve.wait_ge(loaded["segs"], 16 * len(GROUPS["segs"]))
                norm(0)
                steps_of_tiles(dve, step, steps=st, per=(3 + 1 + 1 + 4) + (1 + 1 + 5 + 2))




def experts(nc, a, sb_, sem, bank, c, x, w, loaded):
    with ExitStack() as own:
        def sb(name, shape, dt=F32):
            return sb_("ex_" + name, shape, dt, own)

        def esem(name):
            return sem("ex_" + name)

        T = NT * P
        NC = len(FCH)
        w1 = [sb(f"w1_{i}", [P, KT, 2 * FE]) for i in range(2)]
        w2 = [sb(f"w2_{i}", [P, NC, D]) for i in range(2)]
        stats, mv = sb("stats", [P, NT, 6]), sb("mv", [P, NT, 2])
        veps, rstd = sb("veps", [P, NT]), sb("rstd", [P, NT])
        xn, xT = sb("xn", [P, NT, D]), sb("xT", [P, KT, T])
        logit, raw, prob = sb("logit", [P, NT, NE]), sb("raw", [P, NT, NE]), sb("prob", [P, NT, NE])
        rest, tie, hot = sb("rest", [P, NT, NE]), sb("tie", [P, NT, NE]), [sb(f"hot{i}", [P, NT, NE]) for i in range(2)]
        most, which = sb("most", [P, NT]), sb("which", [P, NT])
        route = sb("route", [P, NE * NT])
        silu = [sb(f"silu{i}", [P, 512]) for i in range(2)]
        g = [sb(f"g{i}", [P, NC, T]) for i in range(2)]
        y_bank, o_bank = bank[0:4], bank[4:8]

        st = Steps(esem("dve_steps"))
        w1_loaded, w2_loaded = [esem("w1_loaded0"), esem("w1_loaded1")], [esem("w2_loaded0"), esem("w2_loaded1")]
        veps_ready, rstd_ready, xn_ready = esem("veps_ready"), esem("rstd_ready"), esem("xn_ready")
        xT_full, xT_done, l_full, l_done = esem("xT_full"), esem("xT_done"), esem("l_full"), esem("l_done")
        sub_ready, e_ready, passed_sp = esem("sub_ready"), esem("e_ready"), esem("passed_sp")
        up_full, silu_ready, g_ready = esem("up_full"), esem("silu_ready"), esem("g_ready")
        o_full, o_done = esem("o_full"), esem("o_done")
        PIECES = 2 * NC

        def schedule(up, down, eng, steps=None, per=None):
            up(0, 0, 1)
            up(1, 1, 1)
            down(0, 0, 1)
            up(2, 0, 2)
            down(1, 1, 1)
            with eng.Fori(1, NE // 2 - 1) as j:
                if steps:
                    steps.enter(j, 1, per)
                up(2 * j + 1, 1, j + 1)
                down(2 * j, 0, j + 1)
                up(2 * j + 2, 0, j + 2)
                down(2 * j + 1, 1, j + 1)
                if steps:
                    steps.leave(NE // 2 - 2)
            up(NE - 1, 1, NE // 2)
            down(NE - 2, 0, NE // 2)
            down(NE - 1, 1, NE // 2)

        with nc.Block() as block:
            @block.sync
            def _(sp):
                def up_weights(e, i):
                    sp.dma_start(w1[i][:], a["w1"][e]).then_inc(w1_loaded[i], 16)

                def down_weights(e, i):
                    sp.dma_start(w2[i][:, 0:2, :], a["w2"][e, 0:2 * P, :].rearrange("(c p) d -> p c d", p=P)) \
                        .then_inc(w2_loaded[i], 16)
                    sp.dma_start(w2[i][0:FE - 2 * P, 2, :], a["w2"][e, 2 * P:FE, :]).then_inc(w2_loaded[i], 16)

                for i in range(2):
                    up_weights(i, i)
                    down_weights(i, i)
                with sp.Fori(1, NE // 2) as j:
                    for i in range(2):
                        sp.wait_ge(up_full, PIECES * (2 * j - 1 + i))
                        alone(sp, passed_sp)
                        up_weights(2 * j + i, i)
                        sp.wait_ge(o_full, NT * (2 * j - 1 + i))
                        alone(sp, passed_sp)
                        down_weights(2 * j + i, i)

            @block.gpsimd
            def _(pool):
                pool.wait_ge(veps_ready, 1)
                nc.gpsimd.tensor_tensor(rstd[:], veps[:], c.half[:, 0:NT], ALU.pow).then_inc(rstd_ready, 1)

            @block.scalar
            def _(act):
                for i in range(NT // 2):
                    act.wait_ge(xT_full, i + 1)
                    src = bank[i % 2][:].rearrange("p (j k t) -> p j k t", j=2, k=KT)
                    for j in range(2):
                        at = P * (2 * i + j)
                        ins = nc.scalar.copy(xT[:, :, at:at + P], src[:, j, :, :])
                    ins.then_inc(xT_done, 1)
                act.wait_ge(sub_ready, 1)
                nc.scalar.activation(raw[:], logit[:], ACT.Exp).then_inc(e_ready, 1)

                def up(e, i, r):
                    for n in range(PIECES):
                        rows = FCH[n % NC][1]
                        act.wait_ge(up_full, PIECES * e + n + 1)
                        at_least(act, g_ready, PIECES * e + n - 1)
                        nc.scalar.activation(silu[n % 2][0:rows, :], y_bank[2 * (n % 2)][0:rows, :], ACT.Silu) \
                            .then_inc(silu_ready, 1)

                schedule(up, lambda e, i, r: None, act)

            @block.tensor
            def _(pe):
                pe.wait_ge(loaded["router"], 16)
                for i in range(NT // 2):
                    pe.wait_ge(xn_ready, i + 1)
                    at_least(pe, xT_done, i - 1)
                    for j in range(2):
                        ins = turn_tokens(nc, bank[i % 2][:, D * j:D * j + D], xn[:, 2 * i + j, :], c)
                    ins.then_inc(xT_full, 1)
                pe.wait_ge(xT_done, NT // 2)
                for t in range(NT):
                    for k in range(KT):
                        ins = nc.tensor.matmul(o_bank[3][:, NE * t:NE * t + NE], xT[:, k, P * t:P * t + P],
                                               w["router"][:, k, :], start=(t == 0 and k == 0), stop=True,
                                               skip_group_check=True)
                ins.then_inc(l_full, 1)

                def up(e, i, r):
                    pe.wait_ge(w1_loaded[i], 16 * r)
                    for n in range(PIECES):
                        h, ch = n // NC, n % NC
                        lo, rows = FCH[ch]
                        at_least(pe, g_ready, PIECES * e + n - 1)
                        for part in range(2):
                            for k in range(KT):
                                at = FE * part + lo
                                ins = nc.tensor.matmul(y_bank[2 * (n % 2) + part][0:rows, :], w1[i][:, k, at:at + rows],
                                                       xT[:, k, 512 * h:512 * h + 512], start=(k == 0),
                                                       stop=(k == KT - 1))
                        ins.then_inc(up_full, 1)

                def down(e, i, r):
                    pe.wait_ge(w2_loaded[i], 32 * r)
                    for t in range(NT):
                        if t % (NT // 2) == 0:
                            pe.wait_ge(g_ready, PIECES * e + NC * (2 * t // NT + 1))
                        at_least(pe, o_done, NT * e + t - 3)
                        for ch, (lo, rows) in enumerate(FCH):
                            ins = nc.tensor.matmul(o_bank[t % 4][:, 0:D], g[i][0:rows, ch, P * t:P * t + P],
                                                   w2[i][0:rows, ch, :], start=(ch == 0), stop=(ch == NC - 1))
                        ins.then_inc(o_full, 1)

                def first_down(e, i, r):
                    if isinstance(e, int) and e == 0:
                        pe.wait_ge(l_done, 1)
                    down(e, i, r)

                schedule(up, first_down, pe)

            @block.vector
            def _(dve):
                for t in range(NT):
                    ins = nc.vector.bn_stats(stats[:, t, :], x[:, t, :])
                st.link(dve, ins)
                for t in range(NT):
                    ins = nc.vector.bn_aggr(mv[:, t, :], stats[:, t, :])
                st.link(dve, ins)
                nc.vector.tensor_scalar(veps[:], mv[:, :, 1], LN_EPS, None, ALU.add).then_inc(veps_ready, 1)
                dve.wait_ge(rstd_ready, 1)
                for t in range(NT):
                    ins = nc.vector.tensor_scalar(xn[:, t, :], x[:, t, :], mv[:, t, 0:1], rstd[:, t:t + 1],
                                                  ALU.subtract, ALU.mult)
                    if t % 2:
                        ins.then_inc(xn_ready, 1)

                each = [P, NT, NE]
                dve.wait_ge(l_full, 1)
                nc.vector.tensor_copy(logit[:], o_bank[3][:, 0:NT * NE].rearrange("p (t e) -> p t e", t=NT)) \
                    .then_inc(l_done, 1)
                dve.wait_ge(l_done, 1)

                def over(v):
                    return v[:].unsqueeze(2).broadcast_to(each)

                st.link(dve, nc.vector.tensor_reduce(most[:], logit[:], AX.X, ALU.max))
                nc.vector.tensor_tensor(logit[:], logit[:], over(most), ALU.subtract).then_inc(sub_ready, 1)
                dve.wait_ge(e_ready, 1)
                st.link(dve, nc.vector.tensor_reduce(most[:], raw[:], AX.X, ALU.add))
                st.link(dve, nc.vector.reciprocal(which[:], most[:]))
                st.link(dve, nc.vector.tensor_tensor(prob[:], raw[:], over(which), ALU.mult))
                number = c.exp8.unsqueeze(1).broadcast_to(each)
                for k in range(2):
                    of = (prob, rest)[k]
                    st.link(dve, nc.vector.tensor_reduce(most[:], of[:], AX.X, ALU.max))
                    st.link(dve, nc.vector.tensor_tensor(tie[:], of[:], over(most), ALU.is_ge))
                    st.link(dve, nc.vector.tensor_tensor(tie[:], tie[:], number, ALU.mult))
                    st.link(dve, nc.vector.tensor_reduce(which[:], tie[:], AX.X, ALU.min))
                    st.link(dve, nc.vector.tensor_tensor(hot[k][:], number, over(which), ALU.is_equal))
                    if k == 0:
                        st.link(dve, nc.vector.scalar_tensor_tensor(rest[:], hot[0][:], -2.0, prob[:], ALU.mult, ALU.add))
                st.link(dve, nc.vector.tensor_tensor(hot[0][:], hot[0][:], hot[1][:], ALU.add))
                st.link(dve, nc.vector.tensor_tensor(route[:].rearrange("p (e t) -> p t e", e=NE), prob[:], hot[0][:],
                                                     ALU.mult))

                def up(e, i, r):
                    for n in range(PIECES):
                        h, ch = n // NC, n % NC
                        rows = FCH[ch][1]
                        dve.wait_ge(silu_ready, PIECES * e + n + 1)
                        nc.vector.tensor_tensor(g[i][0:rows, ch, 512 * h:512 * h + 512],
                                                y_bank[2 * (n % 2) + 1][0:rows, :], silu[n % 2][0:rows, :], ALU.mult) \
                            .then_inc(g_ready, 1)

                def down(e, i, r):
                    for t in range(NT):
                        dve.wait_ge(o_full, NT * e + t + 1)
                        at_least(dve, o_done, NT * (e - 1) + t + 1)
                        if isinstance(e, int):
                            p_route = route[:, NT * e + t:NT * e + t + 1]
                        else:
                            p_route = route[:, bass.ds(e * NT + t, 1)]
                        nc.vector.scalar_tensor_tensor(x[:, t, :], o_bank[t % 4][:, 0:D], p_route, x[:, t, :],
                                                       ALU.mult, ALU.add).then_inc(o_done, 1)

                schedule(up, down, dve)


def _blocks(weight):
    wt = np.asarray(weight).T
    return np.ascontiguousarray(wt.reshape(wt.shape[0] // P, P, wt.shape[1]).transpose(1, 0, 2))


def _plain(weight):
    wt = np.asarray(weight)
    return np.ascontiguousarray(wt.reshape(wt.shape[0] // P, P, wt.shape[1]).transpose(1, 0, 2))


def _column(vector):
    return np.ascontiguousarray(np.asarray(vector).reshape(-1, P).T)


def _constants():
    cst = np.zeros((P, C_END), np.float32)
    p = np.arange(P)[:, None]
    cst[:, C_ID:C_ID + P] = np.eye(P)
    cst[:, C_HEADQ:C_HEADQ + P] = (p % 64) // DH == np.arange(P)[None] // SQ
    cst[:, C_HEAD:C_HEAD + 4] = (p % 64) // DH == np.arange(4)[None]
    cst[:, C_QUARTER:C_QUARTER + 4] = cst[:, C_HEAD:C_HEAD + 4] * DH ** -0.5
    cst[:, C_ROW:C_ROW + 4] = p // SQ == np.arange(4)[None]
    cst[:, C_EQ:C_EQ + SQ] = p % SQ == np.arange(SQ)[None]
    cst[:, C_CAUSAL:C_CAUSAL + SQ] = np.where(np.arange(SQ)[None] > p % SQ, -1e9, 0.0)
    ratio = 2.0 ** (-8.0 / NH)
    cst[:, C_SLOPE:C_SLOPE + NG] = [[ratio ** (4 * g + q // SQ + 1) for g in range(NG)] for q in range(P)]
    cst[:, C_EXP8:C_EXP8 + 8] = np.arange(8)[None] - 8.0
    cst[0:16, C_LAST:C_LAST + 16] = np.eye(16)
    cst[:, C_HALF:C_HALF + 16] = -0.5
    cst[:, C_ONES:C_ONES + SQ] = 1.0
    return cst


def kernel(**inputs):
    import concourse.bacc as bacc
    from concourse.bass_utils import run_bass_kernel_spmd as run

    i = {k: np.asarray(v) for k, v in inputs.items()}
    ctx = i["ctx_1024"]
    host = {
        "cst": _constants(),
        "x": i["x"].reshape(NT, P, D).transpose(1, 0, 2),
        "ctx_T": ctx.transpose(0, 2, 1).reshape(NB, KT, P, SK).transpose(0, 2, 1, 3),
        "ctx": ctx,
        "ctx_rows": ctx[:, SK - 1, :].reshape(NT, BT, D),
        "ctx_last_T": ctx[:, SK - 1, :].T.reshape(KT, P, NB).transpose(1, 0, 2),
        "qpos_T": i["itok_BxS_8_8191"].T,
        "kpos": i["itok_BxS2_1_8191"],
        "mask": i["mask_BxSxS2_if1"],
        "xa_q": _blocks(i["L0_xattn_W_q"]), "xa_k": _blocks(i["L0_xattn_W_k"]),
        "xa_v": _blocks(i["L0_xattn_W_v"]), "xa_o": _blocks(i["L0_xattn_W_o"]),
        "ra_qkv": _plain(i["L0_attn_w_qkv"]), "ra_o": _plain(i["L0_attn_w_out"]),
        "ra_bqk": _column(i["L0_attn_b_qkv"][:2 * D]), "ra_bv": i["L0_attn_b_qkv"][2 * D:],
        "ra_bo": i["L0_attn_b_out"],
        "w_gate": i["L0_ffn_w_gate"].reshape(FT, P, D).transpose(1, 0, 2).reshape(P, -1, QB),
        "w_up": i["L0_ffn_w_up"].reshape(FT, P, D).transpose(1, 0, 2).reshape(P, -1, QB),
        "w_down": i["L0_ffn_w_down"].reshape(KT, P, FF).transpose(1, 0, 2).reshape(P, -1, QB),
        "cx_q": _blocks(i["L1_xattn_Wq"]), "cx_k": _plain(i["L1_xattn_Wk"]), "cx_v": _blocks(i["L1_xattn_Wv"]),
        "cx_bq": _column(i["L1_xattn_bq"]), "cx_bk": _column(i["L1_xattn_bk"]), "cx_bv": i["L1_xattn_bv"],
        "lt_qkv": _blocks(i["L1_attn_lt_w_in"]), "lt_o": _blocks(i["L1_attn_lt_w_out"]),
        "lt_bqk": _column(i["L1_attn_lt_b_in"][:2 * D]), "lt_bv": i["L1_attn_lt_b_in"][2 * D:],
        "lt_bo": _column(i["L1_attn_lt_b_out"]),
        "st_qkv": _blocks(i["L1_attn_st_w_in"]), "st_o": _blocks(i["L1_attn_st_w_out"]),
        "st_bqk": _column(i["L1_attn_st_b_in"][:2 * D]), "st_bv": i["L1_attn_st_b_in"][2 * D:],
        "st_bo": i["L1_attn_st_b_out"],
        "protos": _blocks(i["L1_attn_protos"]), "fus": _blocks(i["L1_attn_fus_w"]), "fus_b": i["L1_attn_fus_b"],
        "router": _plain(i["L1_ffn_router_weight"]),
        "w1": i["L1_ffn_w1"].reshape(NE, KT, P, 2 * FE).transpose(0, 2, 1, 3),
        "w2": i["L1_ffn_w2"],
    }
    nc = bacc.Bacc("TRN2", target_bir_lowering=False, num_devices=1)
    given, views = {}, {}
    for name, array in host.items():
        array = np.ascontiguousarray(array)
        given["in_" + name] = array
        view = nc.dram_tensor("in_" + name, array.shape, mybir.dt.from_np(array.dtype), kind="ExternalInput").ap()
        if array.ndim == 1:
            view = view.unsqueeze(0).broadcast_to([P, array.shape[0]])
        views[name] = view
    out = nc.dram_tensor("out", (P, NT, D), F32, kind="ExternalOutput").ap()
    build(nc, views, out)
    got = run(nc, [given], core_ids=[0]).results[0]["out"]
    return np.ascontiguousarray(np.asarray(got).transpose(1, 0, 2)).reshape(NB, SQ, D)
```

```python
from contextlib import ExitStack

import numpy as np
import concourse.bass as bass
from concourse import mybir

F32 = mybir.dt.float32
I32 = mybir.dt.int32
ALU = mybir.AluOpType
ACT = mybir.ActivationFunctionType
AX = mybir.AxisListType
RMAX = bass.bass_isa.ReduceOp.max

NB, SQ, D, SK = 32, 32, 256, 257
NH, DH = 16, 16
P = 128
NT = NB * SQ // P
BT = P // SQ
KT = D // P
NG = NH // 4
FF = 768
FT = FF // P
QB = 32
NE, FE = 8, 352
FCH = [(0, 128), (128, 128), (256, 96)]
ROUND = 1.5 * 2.0 ** 23
BIG = 3e38
LN_EPS = 1e-5

C_ID, C_HEADQ, C_HEAD, C_ROW, C_EQ, C_CAUSAL, C_SLOPE, C_EXP8, C_LAST, C_HALF, C_ONES, C_QUARTER, C_HEAD8 = (
    0, 128, 256, 260, 264, 296, 328, 332, 340, 356, 372, 404, 408)
C_END = 416


NBLK = 3 * KT * FF // QB


def at_least(eng, sem, value):
    if isinstance(value, int) and value <= 0:
        return
    eng.wait_ge(sem, value)


def alone(eng, sem):
    eng.sem_inc(sem, 1)


class Steps:

    def __init__(self, sem):
        self.sem, self.base, self.n = sem, 0, 0

    def enter(self, i, first, per):
        self.start, self.per, self.first = self.base + self.n, per, first
        self.base, self.n = self.start + (i - first) * per, 0

    def leave(self, count):
        assert self.n == self.per, (self.n, self.per)
        self.base, self.n = self.start + count * self.per, 0

    def done(self, ins):
        ins.then_inc(self.sem, 1)
        self.n += 1
        return self.base + self.n

    def now(self):
        return self.base + self.n

    def link(self, eng, ins):
        eng.wait_ge(self.sem, self.done(ins))



class Uses:

    def __init__(self, order):
        self.index, self.first = {}, {}
        for n, (kind, t, b) in enumerate(order):
            self.index[kind, t, b] = n + 1

    def filled(self, kind, t, b):
        if isinstance(t, int):
            return self.index[kind, t, b]
        return self.index[kind, 2, b] + (t - 2) * (self.index[kind, 3, b] - self.index[kind, 2, b])


def build(nc, a, out):
    with ExitStack() as ctx:
        def sb(name, shape, dt=F32, where=ctx):
            return where.enter_context(nc.sbuf_tensor(name, shape, dt))

        def sem(name):
            return ctx.enter_context(nc.semaphore(name))

        psum = ctx.enter_context(nc.psum_tensor("psum", [P, 8, 512], F32))
        bank = [psum[:, i, :] for i in range(8)]
        cst = sb("cst", [P, C_END])
        x = sb("x", [P, NT, D])
        w = {}
        for name in WEIGHTS:
            w[name] = sb("w_" + name, [P] + list(a[name].shape[1:]))
        wn = sb("wn", [P, NBLK, QB])
        c = Consts(cst)
        loaded = {name: sem("loaded_" + name) for name in GROUPS}
        x_loaded, stored = sem("x_loaded"), sem("stored")

        phases = [
            lambda s: distance_attention(nc, a, sb, s, bank, c, cst, x, w, loaded, x_loaded, wn),
            lambda s: ratio_attention(nc, a, sb, s, psum, bank, c, x, w, loaded),
            lambda s: quantised_ffn(nc, a, sb, s, bank, c, x, wn),
            lambda s: context_attention(nc, a, sb, s, bank, c, x, w, loaded),
            lambda s: segment_attention(nc, a, sb, s, psum, bank, c, x, w, loaded),
            lambda s: experts(nc, a, sb, s, bank, c, x, w, loaded),
        ]
        for phase in phases:
            own = []

            def phase_sem(name):
                own.append(nc.alloc_semaphore(name=name))
                return own[-1]

            phase(phase_sem)
            nc.clear_and_free_semaphores(own)
            nc.all_engine_barrier()
        with nc.Block() as block:
            @block.sync
            def _(sp):
                sp.dma_start(out, x[:]).then_inc(stored, 16)
                sp.wait_ge(stored, 16)


class Consts:

    def __init__(self, cst):
        self.ident = cst[:, C_ID:C_ID + P]
        self.head = cst[:, C_HEAD:C_HEAD + 4]
        self.row = cst[:, C_ROW:C_ROW + 4]
        self.eq = cst[:, C_EQ:C_EQ + SQ]
        self.causal = cst[:, C_CAUSAL:C_CAUSAL + SQ]
        self.slope = cst[:, C_SLOPE:C_SLOPE + NG]
        self.exp8 = cst[:, C_EXP8:C_EXP8 + 8]
        self.last = cst[0:16, C_LAST:C_LAST + 16]
        self.half = cst[:, C_HALF:C_HALF + 16]
        self.head8 = cst[:, C_HEAD8:C_HEAD8 + 8]
        self.quarter = cst[:, C_QUARTER:C_QUARTER + 4]
        self.ones = cst[:, C_ONES:C_ONES + SQ]


GROUPS = {
    "xattn": ("xa_q", "xa_k", "xa_v", "xa_o"),
    "ratio": ("ra_qkv", "ra_o", "ra_bqk", "ra_bv", "ra_bo"),
    "cross": ("cx_q", "cx_k", "cx_v", "cx_bq", "cx_bk", "cx_bv"),
    "segs": ("lt_qkv", "lt_o", "lt_bqk", "lt_bv", "lt_bo", "st_qkv", "st_o", "st_bqk", "st_bv", "st_bo",
             "protos", "fus", "fus_b"),
    "router": ("router",),
}
WEIGHTS = sum(GROUPS.values(), ())


def distance_attention(nc, a, sb_, sem, bank, c, cst, x, w, loaded, x_loaded, wn):
    with ExitStack() as own:
        def sb(name, shape, dt=F32):
            return sb_(name, shape, dt, own)

        PER = NBLK // (BT * (NT - 2))
        round_by = sb("round_by", [P, 1])
        wmax, wscale, wrecip = sb("wmax", [P, NBLK]), sb("wscale", [P, NBLK]), sb("wrecip", [P, NBLK])
        last_T = sb("last_T", [P, KT, NB])
        last_rep = sb("last_rep", [P, KT, NB, NG])
        v_last = sb("v_last", [16, NT, D])

        qpos = sb("qpos", [P, NB], I32)
        qposf = sb("qposf", [P, NB])
        ctxT = [sb(f"ctxT{b}", [P, KT, SK]) for b in range(BT)]
        msk = [sb(f"msk{b}", [P, SK], I32) for b in range(BT)]
        kpos = [sb(f"kpos{b}", [P, SK], I32) for b in range(BT)]
        dist = [sb(f"dist{i}", [P, SK]) for i in range(2)]
        shut = sb("shut", [P, SK])
        bias = [sb(f"bias{i}", [P, NG, SK]) for i in range(2)]
        kT = [sb(f"kT{i}", [P, KT, SK]) for i in range(2)]
        v = [sb(f"v{b}", [P, 2, D]) for b in range(BT)]
        s_sb = [sb(f"s_sb{i}", [P, NG, SK]) for i in range(2)]
        prob = [sb(f"prob{i}", [P, NG, SK]) for i in range(2)]
        mx, negm = sb("mx", [P, BT, NG]), sb("negm", [P, BT, NG])
        esum, rden = sb("esum", [P, BT, NG]), sb("rden", [P, BT, NG])
        rmask = sb("rmask", [P, BT, NG, 4])
        pT = [sb(f"pT{i}", [P, NG, 2, P]) for i in range(2)]
        plast, plast_T = sb("plast", [P, BT, NG]), sb("plast_T", [16, P])
        vx = sb("vx", [16, BT, NG, 64])
        om = sb("om", [P, BT, NG, 64])
        oT, xn, xT = sb("oT", [P, KT, P]), sb("xn", [P, D]), sb("xT", [P, KT, P])
        stat, mv, rstd = sb("stat", [P, 6]), sb("mv", [P, 2]), sb("rstd", [P, 1])
        veps = sb("veps", [P, 1])
        qbd = sb("qbd", [P, KT, BT, 4, SQ])
        sc, pt, kv, oo = bank[0:2], bank[2:4], bank[4:6], bank[6:8]

        ctx_loaded = [sem(f"ctx_loaded{b}") for b in range(BT)]
        passed_sp, passed_dve, passed_pool = sem("xa_passed_sp"), sem("xa_passed_dve"), sem("xa_passed_pool")
        cst_loaded, wn_loaded, pos_loaded = sem("cst_loaded"), sem("wn_loaded"), sem("pos_loaded")
        wq_steps = Steps(sem("xa_dve_steps"))
        scales_ready, pool_steps = sem("scales_ready"), Steps(sem("xa_pool_steps"))
        last_ready, vl_full, vl_done = sem("last_ready"), sem("vl_full"), sem("vl_done")
        kv_full = [sem("kv0_full"), sem("kv1_full")]
        kv_done = [sem("kv0_done"), sem("kv1_done")]
        s_full, s_done = sem("s_full"), sem("s_done")
        negm_ready, p_ready = sem("negm_ready"), sem("p_ready")
        pt_full, pt_done = sem("pt_full"), sem("pt_done")
        pv_done, o_full, o_done = sem("pv_done"), sem("o_full"), sem("o_done")
        var_ready, rstd_ready, xn_ready = sem("var_ready"), sem("rstd_ready"), sem("xn_ready")
        rmask_ready, dist_ready, bias_ready = sem("rmask_ready"), sem("dist_ready"), sem("bias_ready")
        plast_ready, vx_ready = sem("plast_ready"), sem("vx_ready")

        use0, use1 = [], [("xT", -1, 2), ("q", -1, 3)]
        for t in range(NT + 1):
            for b in range(BT):
                if t < NT:
                    use0 += [("k", t, b), ("v", t, b)]
                if b == 1 and t > 0:
                    use1 += [("plast", t, b)]
                if t < NT:
                    use1 += [("k", t, b)]
                if b == 2 and t > 0:
                    use1 += [("oT", t, b)]
                if b == 2 and t < NT - 1:
                    use1 += [("xT", t, b)]
                if b == 3 and t > 0:
                    use1 += [("out", t, b)]
                if b == 3 and t < NT - 1:
                    use1 += [("q", t, b)]
        uses = [Uses(use0), Uses(use1)]

        def tiles(eng, step, steps=None, per=None):
            for b in range(BT):
                step(0, b)
            with eng.Fori(1, NT - 1) as t:
                if steps:
                    steps.enter(t, 1, per)
                for b in range(BT):
                    step(t, b)
                if steps:
                    steps.leave(NT - 2)
            for t in (NT - 1, NT):
                for b in range(BT):
                    step(t, b)

        def exists(t):
            return not isinstance(t, int) or 0 <= t < NT

        def before(t, b, lag):
            return t + (b - lag) // BT, (b - lag) % BT

        with nc.Block() as block:
            @block.sync
            def _(sp):
                sp.dma_start(cst[:], a["cst"]).then_inc(cst_loaded, 16)
                sp.dma_start(x[:], a["x"]).then_inc(x_loaded, 16)
                for name in GROUPS["xattn"]:
                    sp.dma_start(w[name][:], a[name]).then_inc(loaded["xattn"], 16)
                sp.dma_start(last_T[:], a["ctx_last_T"]).then_inc(pos_loaded, 16)
                for h in range(4):
                    sp.dma_start(qpos[SQ * h:SQ * h + SQ, :], a["qpos_T"]).then_inc(pos_loaded, 16)

                def context(t, b):
                    tt, bb = t - 1, b
                    if exists(tt) and not (isinstance(t, int) and t == 0):
                        sp.wait_ge(kv_full[0], uses[0].filled("v", tt, bb))
                        alone(sp, passed_sp)
                        sp.wait_ge(dist_ready, 4 * tt + bb + 1)
                        alone(sp, passed_sp)
                    sp.dma_start(ctxT[b][:], a["ctx_T"][BT * t + b]).then_inc(ctx_loaded[b], 16)
                    sp.dma_start(kpos[b][:], a["kpos"][BT * t + b].unsqueeze(0).broadcast_to([P, SK])) \
                        .then_inc(ctx_loaded[b], 16)
                    sp.dma_start(msk[b][:], a["mask"][BT * t + b].unsqueeze(0).broadcast_to([4, SQ, SK])) \
                        .then_inc(ctx_loaded[b], 16)

                for b in range(BT):
                    context(0, b)
                for n, name in enumerate(("w_gate", "w_up", "w_down")):
                    sp.dma_start(wn[:, n * NBLK // 3:(n + 1) * NBLK // 3, :], a[name]).then_inc(wn_loaded, 16)
                for g in ("ratio", "cross", "segs", "router"):
                    for name in GROUPS[g]:
                        sp.dma_start(w[name][:], a[name]).then_inc(loaded[g], 16)
                with sp.Fori(1, NT) as t:
                    for b in range(BT):
                        context(t, b)

            @block.gpsimd
            def _(pool):
                pool.wait_ge(pos_loaded, 80)
                nc.gpsimd.tensor_copy(last_rep[:], last_T[:].unsqueeze(3).broadcast_to([P, KT, NB, NG])) \
                    .then_inc(last_ready, 1)
                nc.gpsimd.tensor_copy(qposf[:], qpos[:]).then_inc(last_ready, 1)

                def root(t):
                    pool.wait_ge(var_ready, t + 1)
                    nc.gpsimd.tensor_tensor(rstd[:], veps[:], c.half[:, 0:1], ALU.pow).then_inc(rstd_ready, 1)

                def biases(t, b):
                    if not exists(t):
                        return
                    pool.wait_ge(dist_ready, 4 * t + b + 1)
                    at_least(pool, s_done, 16 * t + 4 * b + 4 - 8)
                    alone(pool, passed_pool)
                    for g in range(NG):
                        nc.gpsimd.tensor_scalar(bias[b % 2][:, g, :], dist[b % 2][:], c.slope[:, g:g + 1], 1.0,
                                                ALU.mult, ALU.mult).then_inc(bias_ready, 1)

                nc.gpsimd.memset(round_by[:], ROUND).then_inc(last_ready, 1)
                pool.wait_ge(last_ready, 3)
                pool.wait_ge(cst_loaded, 16)
                root(0)
                biases(0, 0)

                def quantise(t, b):
                    at = bass.ds((t - 1) * (BT * PER) + b * PER, PER)
                    blocks = wn[:, at, :]
                    each = [P, PER, QB]
                    for by, op in ((wrecip[:, at], ALU.mult), (round_by[:], ALU.add), (round_by[:], ALU.subtract),
                                   (wscale[:, at], ALU.mult)):
                        pool_steps.link(pool, nc.gpsimd.tensor_tensor(
                            blocks, blocks, by.unsqueeze(2).broadcast_to(each), op))
                        alone(pool, passed_pool)

                def step(t, b):
                    if b == 1 and exists(t + 1) and exists(t):
                        root(t + 1)
                    biases(*before(t, b, -1))
                    if not isinstance(t, int):
                        if b == 0:
                            pool.wait_ge(scales_ready, 3)
                        quantise(t, b)

                tiles(pool, step, pool_steps, BT * 4)

            @block.scalar
            def _(act):
                def xT_copy(t, b):
                    act.wait_ge(kv_full[1], uses[1].filled("xT", t, b))
                    nc.scalar.copy(xT[:], kv[1][:, 0:D].rearrange("p (k n) -> p k n", k=KT)) \
                        .then_inc(kv_done[1], 1)

                xT_copy(-1, 2)

                def keys(t, b, m):
                    act.wait_ge(kv_full[m], uses[m].filled("k", t, b))
                    at_least(act, s_full, 16 * t + 4 * b - 4)
                    nc.scalar.copy(kT[b % 2][:, m, :], kv[m][:, 0:SK]).then_inc(kv_done[m], 1)

                def exps(t, b, gs):
                    if not exists(t):
                        return
                    if gs[0] == 0:
                        act.wait_ge(negm_ready, 4 * t + b + 1)
                        at_least(act, pt_full, 8 * t + 2 * b + 2 - 4)
                        at_least(act, plast_ready, 4 * t + b + 1 - 2)
                        if b == 0:
                            at_least(act, rmask_ready, t)
                    for g in gs:
                        nc.scalar.activation(prob[b % 2][:, g, :], s_sb[b % 2][:, g, :], ACT.Exp,
                                             bias=negm[:, b, g:g + 1], accum_out=esum[:, b, g:g + 1]) \
                            .then_inc(p_ready, 1)

                def step(t, b):
                    if b == 1 and exists(t - 1):
                        act.wait_ge(kv_full[1], uses[1].filled("plast", t, b))
                        nc.scalar.copy(plast_T[:], kv[1][0:16, 0:P]).then_inc(kv_done[1], 1)
                    if exists(t):
                        keys(t, b, 0)
                    te, be = before(t, b, 1)
                    exps(te, be, (0, 1))
                    if exists(t):
                        keys(t, b, 1)
                        act.wait_ge(kv_full[0], uses[0].filled("v", t, b))
                        at_least(act, pv_done, 4 * t + b + 1 - BT)
                        nc.scalar.copy(v[b][:], kv[0][:].rearrange("p (k n) -> p k n", k=2)) \
                            .then_inc(kv_done[0], 1)
                    exps(te, be, (2, 3))
                    if b == 2 and exists(t - 1):
                        act.wait_ge(kv_full[1], uses[1].filled("oT", t, b))
                        nc.scalar.copy(oT[:], kv[1][:, 0:D].rearrange("p (k n) -> p k n", k=KT)) \
                            .then_inc(kv_done[1], 1)
                    if b == 2 and exists(t) and exists(t + 1):
                        xT_copy(t, b)

                tiles(act, step)

            @block.tensor
            def _(pe):
                pe.wait_ge(cst_loaded, 16)
                pe.wait_ge(last_ready, 1)
                pe.wait_ge(loaded["xattn"], 64)
                for t in range(NT):
                    at_least(pe, vl_done, t - 1)
                    for k in range(KT):
                        ins = nc.tensor.matmul(bank[2 + t % 2][0:16, 0:D],
                                               last_rep[:, k, BT * t:BT * t + BT, :].rearrange("p b g -> p (b g)"),
                                               w["xa_v"][:, k, :], start=(k == 0), stop=(k == KT - 1))
                    ins.then_inc(vl_full, 1)

                def turn_x(t, b):
                    pe.wait_ge(xn_ready, t + 2)
                    if not (isinstance(t, int) and t < 0):
                        pe.wait_ge(kv_done[1], uses[1].filled("xT", t, b) - 1)
                    for k in range(KT):
                        ins = nc.tensor.transpose(kv[1][:, P * k:P * k + P], xn[:, P * k:P * k + P], c.ident)
                    ins.then_inc(kv_full[1], 1)

                def queries(t, b):
                    pe.wait_ge(kv_done[1], uses[1].filled("q", t, b) - 1)
                    for m in range(KT):
                        for k in range(KT):
                            ins = nc.tensor.matmul(kv[1][:, P * m:P * m + P], w["xa_q"][:, k, P * m:P * m + P],
                                                   xT[:, k, :], start=(m == 0 and k == 0),
                                                   stop=(m == KT - 1 and k == KT - 1), skip_group_check=True)
                    ins.then_inc(kv_full[1], 1)

                turn_x(-1, 2)
                queries(-1, 3)
                pe.wait_ge(vl_done, NT)

                def keys(t, b, m):
                    at_least(pe, kv_done[m], uses[m].filled("k", t, b) - 1)
                    for k in range(KT):
                        ins = nc.tensor.matmul(kv[m][:, 0:SK], w["xa_k"][:, k, P * m:P * m + P], ctxT[b][:, k, :],
                                               start=(k == 0), stop=(k == KT - 1))
                    ins.then_inc(kv_full[m], 1)

                def values(t, b):
                    pe.wait_ge(kv_done[0], uses[0].filled("v", t, b) - 1)
                    for i in range(2):
                        for k in range(KT):
                            ins = nc.tensor.matmul(kv[0][:, D * i:D * i + D], ctxT[b][:, k, P * i:P * i + P],
                                                   w["xa_v"][:, k, :], start=(i == 0 and k == 0),
                                                   stop=(i == 1 and k == KT - 1), skip_group_check=True)
                    ins.then_inc(kv_full[0], 1)

                def scores(t, b, gs):
                    pe.wait_ge(kv_done[0], uses[0].filled("k", t, b))
                    pe.wait_ge(kv_done[1], uses[1].filled("k", t, b))
                    for g in gs:
                        lo = 64 * (g % 2)
                        at_least(pe, s_done, 16 * t + 4 * b + g - 1)
                        nc.tensor.matmul(sc[g % 2][:, 0:SK],
                                         qbd[lo:lo + 64, g // 2, b, :, :].rearrange("p h q -> p (h q)"),
                                         kT[b % 2][lo:lo + 64, g // 2, :], start=True, stop=True).then_inc(s_full, 1)

                def turn_p(t, b, j):
                    pe.wait_ge(p_ready, 16 * t + 4 * b + 2 * j + 2)
                    at_least(pe, pt_done, 8 * t + 2 * b + j + 1 - 2)
                    for g in (2 * j, 2 * j + 1):
                        for i in range(2):
                            at = 2 * P * (g % 2) + P * i
                            ins = nc.tensor.transpose(pt[j][:, at:at + P], prob[b % 2][:, g, P * i:P * i + P],
                                                      c.ident)
                    ins.then_inc(pt_full, 1)

                def weighted(t, b):
                    pe.wait_ge(pt_done, 8 * t + 2 * b + 2)
                    pe.wait_ge(kv_done[0], uses[0].filled("v", t, b))
                    if b == 0:
                        at_least(pe, o_done, t)
                    for g in range(NG):
                        for i in range(2):
                            at = D * (b % 2) + 64 * g
                            ins = nc.tensor.matmul(oo[b // 2][:, at:at + 64], pT[b % 2][:, g, i, :],
                                                   v[b][:, i, 64 * g:64 * g + 64],
                                                   start=(b % 2 == 0 and g == 0 and i == 0), stop=False,
                                                   skip_group_check=True)
                    ins.then_inc(pv_done, 1)

                def turn_last(t, b):
                    pe.wait_ge(plast_ready, 4 * t)
                    pe.wait_ge(kv_done[1], uses[1].filled("plast", t, b) - 1)
                    nc.tensor.transpose(kv[1][0:16, 0:P], plast[:].rearrange("p b g -> p (b g)"), c.ident) \
                        .then_inc(kv_full[1], 1)

                def weighted_last(t, b):
                    pe.wait_ge(kv_done[1], uses[1].filled("plast", t, b))
                    pe.wait_ge(vx_ready, t)
                    for i in range(2):
                        ins = nc.tensor.matmul(oo[i][:], plast_T[:],
                                               vx[:, 2 * i:2 * i + 2, :, :].rearrange("p b g d -> p (b g d)"),
                                               start=False, stop=True, skip_group_check=True)
                    ins.then_inc(o_full, 1)

                def heads_to_features(t, b):
                    pe.wait_ge(o_done, t)
                    pe.wait_ge(kv_done[1], uses[1].filled("oT", t, b) - 1)
                    for bb in range(BT):
                        for m in range(KT):
                            at = P * m + SQ * bb
                            ins = nc.tensor.matmul(kv[1][:, at:at + SQ],
                                                   om[:, bb, 2 * m:2 * m + 2, :].rearrange("p g d -> p (g d)"), c.eq,
                                                   start=(bb == 0 and m == 0), stop=True, skip_group_check=True)
                    ins.then_inc(kv_full[1], 1)

                def output(t, b):
                    pe.wait_ge(kv_done[1], uses[1].filled("out", t, b) - 1)
                    for k in range(KT):
                        ins = nc.tensor.matmul(kv[1][:, 0:D], oT[:, k, :], w["xa_o"][:, k, :],
                                               start=(k == 0), stop=(k == KT - 1))
                    ins.then_inc(kv_full[1], 1)

                def step(t, b):
                    if b == 1 and exists(t - 1):
                        turn_last(t, b)
                    if exists(t):
                        pe.wait_ge(ctx_loaded[b], 48 * (t + 1))
                        keys(t, b, 0)
                        keys(t, b, 1)
                        values(t, b)
                    if b == 3 and exists(t - 1):
                        output(t, b)
                    t1, b1 = before(t, b, 1)
                    for j in range(2):
                        if exists(t):
                            scores(t, b, (2 * j, 2 * j + 1))
                        if exists(t1):
                            turn_p(t1, b1, j)
                    if b == 2 and exists(t - 1):
                        heads_to_features(t, b)
                    t2, b2 = before(t, b, 2)
                    if exists(t2):
                        weighted(t2, b2)
                    if b == 1 and exists(t - 1):
                        weighted_last(t, b)
                    if b == 2 and exists(t) and exists(t + 1):
                        turn_x(t, b)
                    if b == 3 and exists(t) and exists(t + 1):
                        queries(t, b)

                tiles(pe, step)

            @block.vector
            def _(dve):
                st = wq_steps

                def norm_stats(t):
                    st.link(dve, nc.vector.bn_stats(stat[:], x[:, t, :]))
                    alone(dve, passed_dve)
                    st.link(dve, nc.vector.bn_aggr(mv[:], stat[:]))
                    nc.vector.tensor_scalar(veps[:], mv[:, 1:2], LN_EPS, None, ALU.add).then_inc(var_ready, 1)

                def norm(t):
                    dve.wait_ge(rstd_ready, t + 1)
                    if not isinstance(t, int) or t > 0:
                        dve.wait_ge(s_full, 16 * (t - 1) + 4)
                    nc.vector.tensor_scalar(xn[:], x[:, t, :], mv[:, 0:1], rstd[:], ALU.subtract, ALU.mult) \
                        .then_inc(xn_ready, 1)

                def distances(t, b):
                    if not exists(t):
                        return
                    dve.wait_ge(ctx_loaded[b], 48 * (t + 1))
                    at_least(dve, bias_ready, 16 * t + 4 * b + 4 - 8)
                    n = st.done(nc.vector.tensor_scalar(dist[b % 2][:], kpos[b][:], qcol(t, b), None, ALU.subtract))
                    n = st.done(nc.vector.tensor_scalar(shut[:], msk[b][:], 0.0, -BIG, ALU.is_equal, ALU.mult))
                    dve.wait_ge(st.sem, n)
                    nc.vector.scalar_tensor_tensor(dist[b % 2][:], shut[:], BIG, dist[b % 2][:], ALU.mult, ALU.add) \
                        .then_inc(dist_ready, 1)

                def qcol(t, b):
                    if isinstance(t, int):
                        return qposf[:, BT * t + b:BT * t + b + 1]
                    return qposf[:, bass.ds(t * BT + b, 1)]

                def rows_max(t, b):
                    dve.wait_ge(bias_ready, 16 * t + 4 * b + 4)
                    at_least(dve, p_ready, 16 * t + 4 * b + 4 - 8)
                    for g in range(NG):
                        dve.wait_ge(s_full, 16 * t + 4 * b + g + 1)
                        alone(dve, passed_dve)
                        nc.vector.tensor_tensor_reduce(s_sb[b % 2][:, g, :], sc[g % 2][:, 0:SK], bias[b % 2][:, g, :],
                                                       1.0, float("-inf"), ALU.add, ALU.max, mx[:, b, g:g + 1]) \
                            .then_inc(s_done, 1)
                    dve.wait_ge(s_done, 16 * t + 4 * b + 4)
                    nc.vector.tensor_scalar(negm[:, b, :], mx[:, b, :], -1.0, None, ALU.mult).then_inc(negm_ready, 1)

                def spread_queries(t):
                    dve.wait_ge(kv_full[1], uses[1].filled("q", t - 1, 3))
                    at_least(dve, s_full, 16 * t)
                    for m in range(KT):
                        src = kv[1][:, P * m:P * m + P].rearrange("p (b q) -> p b q", b=BT)
                        ins = nc.vector.tensor_tensor(
                            qbd[:, m, :, :, :], src.unsqueeze(2).broadcast_to([P, BT, 4, SQ]),
                            c.quarter.unsqueeze(1).unsqueeze(3).broadcast_to([P, BT, 4, SQ]), ALU.mult)
                    ins.then_inc(kv_done[1], 1)

                def copy_turned(t, b):
                    dve.wait_ge(p_ready, 16 * t + 4 * b + 4)
                    if b == 0:
                        at_least(dve, kv_full[1], 0 if isinstance(t, int) and t == 0
                                 else uses[1].filled("plast", t, 1))
                    nc.vector.tensor_copy(plast[:, b, :], prob[b % 2][:, :, SK - 1]).then_inc(plast_ready, 1)
                    at_least(dve, pv_done, 4 * t + b + 1 - 2)
                    for j in range(2):
                        dve.wait_ge(pt_full, 8 * t + 2 * b + j + 1)
                        nc.vector.tensor_copy(pT[b % 2][:, 2 * j:2 * j + 2, :, :],
                                              pt[j][:].rearrange("p (g i n) -> p g i n", g=2, i=2)) \
                            .then_inc(pt_done, 1)

                def spread_last(t):
                    if not (isinstance(t, int) and t == 0):
                        dve.wait_ge(o_full, t)
                    src = v_last[:, t, :].rearrange("p (g d) -> p g d", g=NG)
                    for b in range(BT):
                        ins = nc.vector.tensor_tensor(
                            vx[:, b, :, :], src, c.last[:, NG * b:NG * b + NG].unsqueeze(2).broadcast_to([16, NG, 64]),
                            ALU.mult)
                    ins.then_inc(vx_ready, 1)

                def weigh(t):
                    dve.wait_ge(p_ready, 16 * t + 16)
                    st.link(dve, nc.vector.tensor_scalar(rden[:], esum[:], 1.0, None, ALU.add))
                    st.link(dve, nc.vector.reciprocal(rden[:], rden[:]))
                    nc.vector.tensor_tensor(
                        rmask[:].rearrange("p b g h -> p (b g) h"),
                        rden[:].rearrange("p b g -> p (b g)").unsqueeze(2).broadcast_to([P, 16, 4]),
                        c.row.unsqueeze(1).broadcast_to([P, 16, 4]), ALU.mult).then_inc(rmask_ready, 1)

                def normalise(t):
                    dve.wait_ge(rmask_ready, t + 1)
                    dve.wait_ge(o_full, t + 1)
                    for i in range(2):
                        ins = nc.vector.tensor_tensor(
                            om[:, 2 * i:2 * i + 2, :, :].rearrange("p b g (h d) -> p (b g h) d", h=4),
                            oo[i][:].rearrange("p (n d) -> p n d", d=DH),
                            rmask[:, 2 * i:2 * i + 2, :, :].rearrange("p b g h -> p (b g h)").unsqueeze(2)
                            .broadcast_to([P, 32, DH]), ALU.mult)
                    ins.then_inc(o_done, 1)

                def add_output(t, tt):
                    dve.wait_ge(kv_full[1], uses[1].filled("out", t, 3))
                    nc.vector.tensor_tensor(x[:, tt, :], kv[1][:, 0:D], x[:, tt, :], ALU.add).then_inc(kv_done[1], 1)

                def scales(i):
                    at = slice(i * NBLK // 3, (i + 1) * NBLK // 3)
                    dve.wait_ge(wn_loaded, 48)
                    st.link(dve, nc.vector.tensor_reduce(wmax[:, at], wn[:, at, :], AX.X, ALU.max,
                                                         apply_absolute_value=True))
                    st.link(dve, nc.vector.tensor_scalar(wscale[:, at], wmax[:, at], 1.0 / 7.0, 1e-12, ALU.mult,
                                                         ALU.max))
                    nc.vector.reciprocal(wrecip[:, at], wscale[:, at]).then_inc(scales_ready, 1)

                def step(t, b):
                    t1, b1 = before(t, b, 1)
                    if isinstance(t, int) and t == 0 and b > 0:
                        scales(b - 1)
                    if b == 1 and exists(t - 1):
                        weigh(t - 1)
                    if b == 2 and exists(t - 1):
                        normalise(t - 1)
                    if b == 3 and exists(t - 1):
                        add_output(t, t - 1)
                    if exists(t):
                        rows_max(t, b)
                    if exists(t1):
                        copy_turned(t1, b1)
                    if b == 1 and exists(t) and exists(t + 1):
                        norm_stats(t + 1)
                        norm(t + 1)
                    if b == 3 and exists(t) and exists(t + 1):
                        spread_queries(t + 1)
                    if exists(t):
                        distances(*before(t, b, -1))
                    if b == 3 and exists(t):
                        spread_last(t)

                dve.wait_ge(cst_loaded, 16)
                for t in range(NT):
                    dve.wait_ge(vl_full, t + 1)
                    nc.vector.tensor_copy(v_last[:, t, :], bank[2 + t % 2][0:16, 0:D]).then_inc(vl_done, 1)
                dve.wait_ge(vl_done, NT)
                dve.wait_ge(last_ready, 2)
                dve.wait_ge(x_loaded, 16)
                norm_stats(0)
                norm(0)
                distances(0, 0)
                spread_queries(0)
                tiles(dve, step, st, 4 * 2 + 2 + 2)



def turn_tokens(nc, dst, src, c):
    for k in range(KT):
        ins = nc.tensor.transpose(dst[:, P * k:P * k + P], src[:, P * k:P * k + P], c.ident)
    return ins


def project_qk(nc, dst, weight, xT):
    for m in range(2 * KT):
        for k in range(KT):
            ins = nc.tensor.matmul(dst[:, P * m:P * m + P], weight[:, k, P * m:P * m + P], xT[:, k, :],
                                   start=(m == 0 and k == 0), stop=True, skip_group_check=True)
    return ins


def project_tokens(nc, dst, lhs_T, weight):
    n = weight.shape[1]
    for k in range(n):
        ins = nc.tensor.matmul(dst[:, 0:D], lhs_T[:, k, :], weight[:, k, :], start=(k == 0), stop=(k == n - 1))
    return ins


def spread_heads(eng, kbd, kT, head):
    src = kT[:].rearrange("p (b k) -> p b k", b=BT)
    return eng.tensor_tensor(kbd, src.unsqueeze(2).broadcast_to([P, BT, 4, SQ]),
                             head.unsqueeze(1).unsqueeze(3).broadcast_to([P, BT, 4, SQ]), ALU.mult)


def spread_batches(eng, vbd, v, c):
    for i in range(NG):
        at = D // NG * (KT * (i % KT) + i // KT)
        ins = eng.tensor_tensor(vbd[:, i, :, :], v[:, at:at + 64].unsqueeze(1).broadcast_to([P, BT, 64]),
                                c.row.unsqueeze(2).broadcast_to([P, BT, 64]), ALU.mult)
    return ins


def per_batch(nc, dst, left, right, col, first):
    for m in range(KT):
        for b in range(BT):
            for f in range(2):
                lo, at = 64 * f, col + P * m
                ins = nc.tensor.matmul(dst[SQ * b:SQ * b + SQ, f, at:at + P], left(lo, m, b), right(lo, m, b),
                                       start=first and m == 0, stop=True, skip_group_check=True)
    return ins


def tokens(xT):
    return lambda lo, m, b: xT[lo:lo + 64, m, SQ * b:SQ * b + SQ]


def heads_apart(bd):
    return lambda lo, m, b: bd[lo:lo + 64, m, b, :, :].rearrange("p h k -> p (h k)")


def in_banks(scores):
    return scores[:].rearrange("p (f n) k -> p f (n k)", f=2)


def weigh_values(nc, dst, sums, pT, vbd, c):
    for i in range(NG):
        weights = pT[:, 4 * i:4 * i + 4, :].rearrange("p h q -> p (h q)")
        at = D * (i % 2)
        nc.tensor.matmul(dst[:, i // 2, at:at + D], weights, vbd[:, i, :, :].rearrange("p b d -> p (b d)"),
                         start=(i % 2 == 0), stop=True, skip_group_check=True)
        ins = nc.tensor.matmul(sums[:, BT * i:BT * i + BT], weights, c.row, start=(i == 0), stop=True,
                               skip_group_check=True)
    return ins


def turn_blocks(nc, pT, prob):
    return nc.vector.transpose(pT[:].rearrange("p n q -> p (n q)"), prob[:].rearrange("p n k -> p (n k)"))


def own_heads(nc, o, src, rden):
    for h in range(4):
        own = slice(SQ * h, SQ * h + SQ)
        ins = nc.vector.tensor_tensor(
            o[own, :].rearrange("p (b i d) -> p i b d", b=BT, i=NG),
            src[own, :, :].rearrange("p j (i b n) -> p (j i) b n", i=2, b=BT)[:, :, :, DH * h:DH * h + DH],
            rden[own, :].rearrange("p (i b) -> p i b", b=BT).unsqueeze(3).broadcast_to([SQ, NG, BT, DH]), ALU.mult)
    return ins


def to_features(nc, oT, o):
    return nc.vector.transpose(oT[:].rearrange("p j (b q) -> p b j q", b=BT),
                               o[:].rearrange("p (b j n) -> p b j n", b=BT, j=2))


def slots(eng, step, steps=None, per=None):
    for u in (-2, -1, 0):
        step(u)
    with eng.Fori(1, NT - 3) as u:
        if steps:
            steps.enter(u, 1, per)
        step(u)
        if steps:
            steps.leave(NT - 4)
    for u in range(NT - 3, NT + 1):
        step(u)


def there(u, count=NT):
    return not isinstance(u, int) or 0 <= u < count


def ratio_attention(nc, a, sb_, sem, psum, bank, c, x, w, loaded):
    with ExitStack() as own:
        def sb(name, shape, dt=F32):
            return sb_("ra_" + name, shape, dt, own)

        def rsem(name):
            return sem("ra_" + name)

        xn, xT = sb("xn", [P, D]), sb("xT", [P, KT, P])
        stat, mv, veps, rstd = sb("stat", [P, 6]), sb("mv", [P, 2]), sb("veps", [P, 1]), sb("rstd", [P, 1])
        bq2, q_norm = sb("bq2", [P, KT]), sb("q_norm", [P, NH])
        qm2T, q2T, kT = sb("qm2T", [P, KT, P]), sb("q2T", [P, KT, P]), sb("kT", [P, P])
        kbd, k2bd = sb("kbd", [P, KT, BT, 4, SQ]), sb("k2bd", [P, KT, BT, 4, SQ])
        v, vbd = sb("v", [P, D]), sb("vbd", [P, NG, BT, 64])
        num, den, prob = (sb(name, [P, NH, SQ]) for name in ("num", "den", "prob"))
        square, dot = sb("square", [P, NH, SQ]), sb("dot", [P, NH, SQ])
        mx, rden = sb("mx", [P, NH]), sb("rden", [P, NG * BT])
        pT, o, oT = sb("pT", [P, NH, SQ]), sb("o", [P, D]), sb("oT", [P, KT, P])
        s_banks, x_bank, qk_bank, v_bank, o_banks, y_bank = psum[:, 0:2, :], *bank[2:5], psum[:, 5:7, :], bank[7]
        sums, q_sums = x_bank[:, D:D + NG * BT], v_bank[:, D:D + NH]

        st = Steps(rsem("dve_steps"))
        passed_dve, passed_pool, passed_pe = rsem("passed_dve"), rsem("passed_pool"), rsem("passed_pe")
        var_ready, rstd_ready, xn_ready = rsem("var_ready"), rsem("rstd_ready"), rsem("xn_ready")
        xT_full, xT_done, qk_full = rsem("xT_full"), rsem("xT_done"), rsem("qk_full")
        k_ready, qk_done = rsem("k_ready"), rsem("qk_done")
        kbd_ready, k2_ready = [rsem("kbd0_ready"), rsem("kbd1_ready")], rsem("k2_ready")
        bias_of_head = sb("bias_of_head", [P, 4])
        v_full, v_done, vbd_ready = rsem("v_full"), rsem("v_done"), rsem("vbd_ready")
        s_full, s_read, sub_ready, p_ready = rsem("s_full"), rsem("s_read"), rsem("sub_ready"), rsem("p_ready")
        pT_ready, o_full, o_done = rsem("pT_ready"), rsem("o_full"), rsem("o_done")
        oT_ready, y_full, y_done = rsem("oT_ready"), rsem("y_full"), rsem("y_done")
        den_ready, inverse_ready = rsem("den_ready"), rsem("inverse_ready")
        ratio_ready, masked_ready = rsem("ratio_ready"), rsem("masked_ready")
        bias_added, consts_set = rsem("bias_added"), rsem("consts_set")

        with nc.Block() as block:
            @block.gpsimd
            def _(pool):
                def root(n):
                    pool.wait_ge(var_ready, n + 1)
                    nc.gpsimd.tensor_tensor(rstd[:], veps[:], c.half[:, 0:1], ALU.pow).then_inc(rstd_ready, 1)

                def step(u):
                    if there(u + 3):
                        root(u + 3)
                    if there(u + 2):
                        pool.wait_ge(k_ready, u + 3)
                        at_least(pool, s_full, u + 2)
                        alone(pool, passed_pool)
                        spread_heads(nc.gpsimd, kbd[:, 0, :, :, :], kT, c.head).then_inc(kbd_ready[0], 1)
                        pool.wait_ge(xn_ready, u + 3)
                        alone(pool, passed_pool)
                        nc.gpsimd.tensor_tensor(x[:, u + 2, :], x[:, u + 2, :], w["ra_bo"][:], ALU.add) \
                            .then_inc(bias_added, 1)
                    if there(u + 1):
                        pool.wait_ge(inverse_ready, u + 2)
                        at_least(pool, p_ready, u + 1)
                        nc.gpsimd.tensor_tensor(num[:], square[:], den[:], ALU.mult).then_inc(ratio_ready, 1)
                        pool.wait_ge(ratio_ready, u + 2)
                        nc.gpsimd.tensor_tensor(num[:], num[:], c.causal.unsqueeze(1).broadcast_to([P, NH, SQ]),
                                                ALU.add).then_inc(masked_ready, 1)
                        pool.wait_ge(v_done, u + 2)
                        at_least(pool, o_full, u + 1)
                        alone(pool, passed_pool)
                        spread_batches(nc.gpsimd, vbd, v, c).then_inc(vbd_ready, 1)

                pool.wait_ge(loaded["ratio"], 16 * len(GROUPS["ratio"]))
                root(0)
                slots(pool, step)

            @block.scalar
            def _(act):
                act.wait_ge(loaded["ratio"], 16 * len(GROUPS["ratio"]))
                act.wait_ge(consts_set, 1)

                def step(u):
                    if there(u + 1):
                        n = u + 1
                        act.wait_ge(s_full, n + 1)
                        at_least(act, ratio_ready, n)
                        at_least(act, den_ready, n)
                        nc.scalar.activation(in_banks(square), s_banks[:, :, 0:D], ACT.Square, scale=0.5)
                        nc.scalar.copy(in_banks(dot), s_banks[:, :, 0:D]).then_inc(s_read, 1)
                    if there(u + 2):
                        n = u + 2
                        act.wait_ge(xT_full, n + 1)
                        at_least(act, v_full, n)
                        nc.scalar.copy(xT[:], x_bank[:, 0:D].rearrange("p (k t) -> p k t", k=KT)).then_inc(xT_done, 1)
                    if there(u):
                        act.wait_ge(sub_ready, u + 1)
                        at_least(act, pT_ready, u)
                        nc.scalar.activation(prob[:], num[:], ACT.Exp).then_inc(p_ready, 1)
                    if there(u + 2):
                        n = u + 2
                        act.wait_ge(qk_full, n + 1)
                        at_least(act, s_full, n)
                        at = P * KT
                        nc.scalar.activation(kT[:], qk_bank[:, at:at + P], ACT.Identity,
                                             bias=w["ra_bqk"][:, KT:KT + 1]).then_inc(k_ready, 1)
                        for h in range(4):
                            ins = nc.scalar.activation(
                                kbd[:, 1, :, h, :], qk_bank[:, at + P:at + 2 * P].rearrange("p (b k) -> p b k", b=BT),
                                ACT.Identity, bias=bias_of_head[:, h:h + 1], scale=c.head[:, h:h + 1])
                        ins.then_inc(kbd_ready[1], 1)
                        for m in range(KT):
                            at = P * m
                            nc.scalar.activation(qm2T[:, m, :], qk_bank[:, at:at + P], ACT.Identity,
                                                 bias=bq2[:, m:m + 1], scale=-2.0)
                            ins = nc.scalar.activation(q2T[:, m, :], qk_bank[:, at:at + P], ACT.Square,
                                                       bias=w["ra_bqk"][:, m:m + 1])
                        ins.then_inc(qk_done, 1)
                    if there(u + 2):
                        n = u + 2
                        for m in (1, 0):
                            act.wait_ge(kbd_ready[m], n + 1)
                            ins = nc.scalar.activation(k2bd[:, m, :, :, :], kbd[:, m, :, :, :], ACT.Square)
                        ins.then_inc(k2_ready, 1)

                slots(act, step)

            @block.tensor
            def _(pe):
                pe.wait_ge(loaded["ratio"], 16 * len(GROUPS["ratio"]))

                def step(u):
                    if there(u + 1):
                        n = u + 1
                        pe.wait_ge(kbd_ready[0], n + 1)
                        pe.wait_ge(kbd_ready[1], n + 1)
                        pe.wait_ge(qk_done, n + 1)
                        at_least(pe, den_ready, n)
                        alone(pe, passed_pe)
                        ones = lambda lo, m, b: c.ones[lo:lo + 64, :]
                        per_batch(nc, s_banks, tokens(qm2T), heads_apart(kbd), 0, True)
                        pe.wait_ge(k2_ready, n + 1)
                        alone(pe, passed_pe)
                        per_batch(nc, s_banks, ones, heads_apart(k2bd), D, False).then_inc(s_full, 1)
                        at_least(pe, v_done, n)
                        project_tokens(nc, v_bank, xT, w["ra_qkv"][:, :, 2 * D:3 * D])
                        for m in range(KT):
                            ins = nc.tensor.matmul(q_sums.rearrange("p (f m h) -> p f m h", f=2, m=KT)[:, :, m, :],
                                                   q2T[:, m, :], c.head8, start=False, stop=True,
                                                   skip_group_check=True)
                        ins.then_inc(v_full, 1)
                    if there(u + 2):
                        n = u + 2
                        pe.wait_ge(xn_ready, n + 1)
                        at_least(pe, o_done, n - 2)
                        turn_tokens(nc, x_bank, xn, c).then_inc(xT_full, 1)
                    if there(u - 1):
                        pe.wait_ge(oT_ready, u)
                        at_least(pe, y_done, u - 1)
                        project_tokens(nc, y_bank, oT, w["ra_o"]).then_inc(y_full, 1)
                    if there(u + 2):
                        n = u + 2
                        pe.wait_ge(xT_done, n + 1)
                        at_least(pe, qk_done, n)
                        project_qk(nc, qk_bank, w["ra_qkv"], xT).then_inc(qk_full, 1)
                    if there(u):
                        pe.wait_ge(pT_ready, u + 1)
                        pe.wait_ge(vbd_ready, u + 1)
                        at_least(pe, o_done, u)
                        weigh_values(nc, o_banks, sums, pT, vbd, c).then_inc(o_full, 1)

                slots(pe, step)

            @block.vector
            def _(dve):
                def norm_stats(n):
                    st.link(dve, nc.vector.bn_stats(stat[:], x[:, n, :]))
                    alone(dve, passed_dve)
                    st.link(dve, nc.vector.bn_aggr(mv[:], stat[:]))
                    nc.vector.tensor_scalar(veps[:], mv[:, 1:2], LN_EPS, None, ALU.add).then_inc(var_ready, 1)

                def norm_apply(n):
                    dve.wait_ge(rstd_ready, n + 1)
                    at_least(dve, xT_full, n)
                    nc.vector.tensor_scalar(xn[:], x[:, n, :], mv[:, 0:1], rstd[:], ALU.subtract, ALU.mult) \
                        .then_inc(xn_ready, 1)

                flat = [P, NH, SQ]

                def step(u):
                    n = u + 1
                    if there(u):
                        dve.wait_ge(masked_ready, u + 1)
                        st.link(dve, nc.vector.tensor_reduce(mx[:], num[:], AX.X, ALU.max))
                        nc.vector.tensor_tensor(num[:], num[:], mx[:].unsqueeze(2).broadcast_to(flat), ALU.subtract) \
                            .then_inc(sub_ready, 1)
                    if there(u + 3):
                        norm_stats(u + 3)
                    if there(u):
                        dve.wait_ge(p_ready, u + 1)
                        at_least(dve, o_full, u)
                        alone(dve, passed_dve)
                        turn_blocks(nc, pT, prob).then_inc(pT_ready, 1)
                    if there(n):
                        dve.wait_ge(v_full, n + 1)
                        at_least(dve, vbd_ready, n)
                        st.link(dve, nc.vector.tensor_scalar(q_norm[:], q_sums, 1e-6, None, ALU.add))
                        dve.wait_ge(s_read, n + 1)
                        at_least(dve, ratio_ready, n)
                        nc.vector.tensor_tensor(in_banks(den), s_banks[:, :, D:2 * D], in_banks(dot), ALU.add) \
                            .then_inc(den_ready, 1)
                        dve.wait_ge(den_ready, n + 1)
                        st.link(dve, nc.vector.tensor_tensor(den[:], den[:], q_norm[:].unsqueeze(2).broadcast_to(flat),
                                                             ALU.add))
                        nc.vector.tensor_tensor(v[:], v_bank[:, 0:D], w["ra_bv"][:], ALU.add).then_inc(v_done, 1)
                    if there(n):
                        nc.vector.reciprocal(den[:], den[:]).then_inc(inverse_ready, 1)
                    if there(u - 1):
                        dve.wait_ge(y_full, u)
                        dve.wait_ge(bias_added, u)
                        nc.vector.tensor_tensor(x[:, u - 1, :], y_bank[:, 0:D], x[:, u - 1, :], ALU.add) \
                            .then_inc(y_done, 1)
                    if there(u + 3):
                        norm_apply(u + 3)
                    if there(u):
                        dve.wait_ge(o_full, u + 1)
                        st.link(dve, nc.vector.reciprocal(rden[:], sums))
                        own_heads(nc, o, o_banks, rden).then_inc(o_done, 1)
                        dve.wait_ge(o_done, u + 1)
                        at_least(dve, y_full, u)
                        alone(dve, passed_dve)
                        to_features(nc, oT, o).then_inc(oT_ready, 1)

                dve.wait_ge(loaded["ratio"], 16 * len(GROUPS["ratio"]))
                nc.vector.tensor_scalar(bias_of_head[:], c.head, w["ra_bqk"][:, KT + 1:KT + 2], None, ALU.mult)
                nc.vector.tensor_scalar(bq2[:], w["ra_bqk"][:, 0:KT], -2.0, None, ALU.mult).then_inc(consts_set, 1)
                norm_stats(0)
                norm_apply(0)
                slots(dve, step, steps=st, per=2 + 1 + 1 + 1 + 1)




def quantised_ffn(nc, a, sb_, sem, bank, c, x, wn):
    with ExitStack() as own:
        def sb(name, shape, dt=F32):
            return sb_("ff_" + name, shape, dt, own)

        def fsem(name):
            return sem("ff_" + name)

        T = NT * P
        stats, mv = sb("stats", [P, NT, 6]), sb("mv", [P, NT, 2])
        veps, rstd = sb("veps", [P, NT]), sb("rstd", [P, NT])
        xn, xT = sb("xn", [P, NT, D]), sb("xT", [P, KT, T])
        gate, up, sig = sb("gate", [P, FT, T]), sb("up", [P, FT, T]), sb("sig", [P, FT, T])
        X, G, U, H, O = range(5)
        peak, top = sb("peak", [P, 5, 2 * FT]), sb("top", [P, 5])
        topall, scale, inv = sb("topall", [P, 5]), sb("scale", [P, 5]), sb("inv", [P, 5])
        w_gate_T, w_up_T = sb("w_gate_T", [P, KT, FF]), sb("w_up_T", [P, KT, FF])
        w_down_T = sb("w_down_T", [P, FT, D])
        st = Steps(fsem("dve_steps"))
        wt_full, wt_done = fsem("wt_full"), fsem("wt_done")
        pool_steps = Steps(fsem("pool_steps"))
        veps_ready, rstd_ready = fsem("veps_ready"), fsem("rstd_ready")
        top_ready, topall_ready = [fsem(f"top_ready{i}") for i in range(5)], [fsem(f"topall_ready{i}") for i in range(5)]
        xn_ready, xT_full, xT_done = fsem("xn_ready"), fsem("xT_full"), fsem("xT_done")
        gu_full, gu_done = fsem("gu_full"), fsem("gu_done")
        scale_set = [fsem(f"scale_set{i}") for i in range(5)]
        gate_ready, sig_ready, up_1, up_ready = fsem("gate_ready"), fsem("sig_ready"), fsem("up_1"), fsem("up_ready")
        h_1, h_ready, o_1, o_ready, y_full = fsem("h_1"), fsem("h_ready"), fsem("o_1"), fsem("o_ready"), fsem("y_full")
        act_steps, round_by = Steps(fsem("act_steps")), sb("round_by", [P, 1])
        round_set = fsem("round_set")

        def turned(copy, n):
            src = bank[2 + n % 6][:].rearrange("p (j o) -> p j o", j=4)
            if n < 6:
                dst = (w_gate_T, w_up_T)[n // 3]
                return copy(dst[:].rearrange("p k (o q) -> p (k o) q", q=P)[:, 4 * (n % 3):4 * (n % 3) + 4, :], src)
            i = n - 6
            return copy(w_down_T[:].rearrange("p f (o q) -> p (f o) q", q=P)[:, 4 * i:4 * i + 4, :], src)

        with nc.Block() as block:
            @block.gpsimd
            def _(pool):
                pool.wait_ge(veps_ready, 1)
                nc.gpsimd.tensor_tensor(rstd[:], veps[:], c.half[:, 0:NT], ALU.pow).then_inc(rstd_ready, 1)

                def largest(i):
                    pool.wait_ge(top_ready[i], 1)
                    nc.gpsimd.partition_all_reduce(topall[:, i:i + 1], top[:, i:i + 1], P, RMAX) \
                        .then_inc(topall_ready[i], 1)

                def back(piece, i):
                    return nc.gpsimd.tensor_scalar(piece, piece, -ROUND, scale[:, i:i + 1], ALU.add, ALU.mult)

                largest(X)
                largest(G)
                pool.wait_ge(scale_set[G], 1)
                for m in range(FT):
                    pool_steps.link(pool, nc.gpsimd.tensor_scalar(gate[:, m, :], gate[:, m, :], inv[:, G:G + 1], ROUND,
                                                                  ALU.mult, ALU.add))
                    back(gate[:, m, :], G).then_inc(gate_ready, 1)
                largest(U)
                largest(H)
                for m in range(FT):
                    pool.wait_ge(up_1, m + 1)
                    back(up[:, m, :], U).then_inc(up_ready, 1)
                    pool.wait_ge(h_1, m + 1)
                    back(gate[:, m, :], H).then_inc(h_ready, 1)
                largest(O)

            @block.scalar
            def _(act):
                for n in range(9):
                    act.wait_ge(wt_full, n + 1)
                    turned(nc.scalar.copy, n).then_inc(wt_done, 1)
                for i in range(NT // 2):
                    act.wait_ge(xT_full, i + 1)
                    src = bank[i % 2][:].rearrange("p (j k t) -> p j k t", j=2, k=KT)
                    for j in range(2):
                        at = P * (2 * i + j)
                        ins = nc.scalar.copy(xT[:, :, at:at + P], src[:, j, :, :])
                    ins.then_inc(xT_done, 1)
                act.wait_ge(round_set, 1)
                for n in range(4 * FT):
                    act.wait_ge(gu_full, n + 1)
                    dst = (gate, up)[n // (2 * FT)]
                    m, h = n // 2 % FT, n % 2
                    nc.scalar.copy(dst[:, m, 512 * h:512 * h + 512], bank[2 + n % 6][:]).then_inc(gu_done, 1)
                    if n >= 2 * FT and h == 1:
                        act.wait_ge(gate_ready, m + 1)
                        act_steps.link(act, nc.scalar.activation(sig[:, m, :], gate[:, m, :], ACT.Sigmoid))
                        nc.scalar.activation(sig[:, m, :], sig[:, m, :], ACT.Identity, bias=round_by[:],
                                             scale=65536.0).then_inc(sig_ready, 1)

                def to_integers(piece, i):
                    return nc.scalar.activation(piece, piece, ACT.Identity, bias=round_by[:], scale=inv[:, i:i + 1])

                act.wait_ge(scale_set[U], 1)
                act.wait_ge(scale_set[H], 1)
                for m in range(FT):
                    to_integers(up[:, m, :], U).then_inc(up_1, 1)
                    to_integers(gate[:, m, :], H).then_inc(h_1, 1)
                act.wait_ge(scale_set[O], 1)
                for q in range(4):
                    for m in range(FT):
                        to_integers(gate[:, m, T // 4 * q:T // 4 * (q + 1)], O).then_inc(o_1, 1)

            @block.tensor
            def _(pe):
                wgu = wn[:].rearrange("p (j b) q -> p j (b q)", j=3)
                for n in range(9):
                    at_least(pe, wt_done, n - 5)
                    for j in range(4):
                        if n < 6:
                            i = 4 * (n % 3) + j
                            src = wgu[:, n // 3, :].rearrange("p (o k q) -> p k o q", o=FT, k=KT)[:, i // FT, i % FT, :]
                        else:
                            i = 4 * (n - 6) + j
                            src = wgu[:, 2, :].rearrange("p (o f q) -> p f o q", o=KT, f=FT)[:, i // KT, i % KT, :]
                        ins = nc.tensor.transpose(bank[2 + n % 6][:, P * j:P * j + P], src, c.ident)
                    ins.then_inc(wt_full, 1)
                for i in range(NT // 2):
                    pe.wait_ge(xn_ready, i + 1)
                    at_least(pe, xT_done, i - 1)
                    for j in range(2):
                        ins = turn_tokens(nc, bank[i % 2][:, D * j:D * j + D], xn[:, 2 * i + j, :], c)
                    ins.then_inc(xT_full, 1)
                pe.wait_ge(xT_done, NT // 2)
                pe.wait_ge(wt_done, 9)
                for n in range(4 * FT):
                    wt = (w_gate_T, w_up_T)[n // (2 * FT)]
                    m, h = n // 2 % FT, n % 2
                    at_least(pe, gu_done, n - 5)
                    for k in range(KT):
                        ins = nc.tensor.matmul(bank[2 + n % 6][:], wt[:, k, P * m:P * m + P],
                                               xT[:, k, 512 * h:512 * h + 512], start=(k == 0), stop=(k == KT - 1))
                    ins.then_inc(gu_full, 1)
                pe.wait_ge(gu_done, 4 * FT)
                for t in range(NT):
                    if t % (NT // 4) == 0:
                        pe.wait_ge(o_ready, FT * (4 * t // NT + 1))
                    for f in range(FT):
                        ins = nc.tensor.matmul(bank[t][:, 0:D], gate[:, f, P * t:P * t + P], w_down_T[:, f, :],
                                               start=(f == 0), stop=(f == FT - 1))
                    ins.then_inc(y_full, 1)

            @block.vector
            def _(dve):
                nc.vector.memset(round_by[:], ROUND).then_inc(round_set, 1)
                for t in range(NT):
                    ins = nc.vector.bn_stats(stats[:, t, :], x[:, t, :])
                st.link(dve, ins)
                for t in range(NT):
                    ins = nc.vector.bn_aggr(mv[:, t, :], stats[:, t, :])
                st.link(dve, ins)
                nc.vector.tensor_scalar(veps[:], mv[:, :, 1], LN_EPS, None, ALU.add).then_inc(veps_ready, 1)
                dve.wait_ge(rstd_ready, 1)
                for t in range(NT):
                    ins = nc.vector.tensor_scalar(xn[:, t, :], x[:, t, :], mv[:, t, 0:1], rstd[:, t:t + 1],
                                                  ALU.subtract, ALU.mult)
                st.link(dve, ins)

                def scales(i, n):
                    nc.vector.tensor_reduce(top[:, i:i + 1], peak[:, i, 0:n], AX.X, ALU.max).then_inc(top_ready[i], 1)
                    dve.wait_ge(topall_ready[i], 1)
                    st.link(dve, nc.vector.tensor_scalar(scale[:, i:i + 1], topall[:, i:i + 1], 1.0 / 32767.0, 1e-12,
                                                         ALU.mult, ALU.max))
                    nc.vector.reciprocal(inv[:, i:i + 1], scale[:, i:i + 1]).then_inc(scale_set[i], 1)

                def rounded(piece, i):
                    st.link(dve, nc.vector.tensor_scalar(piece, piece, inv[:, i:i + 1], ROUND, ALU.mult, ALU.add))
                    return nc.vector.tensor_scalar(piece, piece, ROUND, scale[:, i:i + 1], ALU.subtract, ALU.mult)

                def magnitude(i, n, piece):
                    return nc.vector.tensor_reduce(peak[:, i, n:n + 1], piece, AX.XY if len(piece.shape) == 3 else AX.X,
                                                   ALU.max, apply_absolute_value=True)

                st.link(dve, magnitude(X, 0, xn[:]))
                scales(X, 1)
                dve.wait_ge(scale_set[X], 1)
                for i in range(NT // 2):
                    rounded(xn[:, 2 * i:2 * i + 2, :], X).then_inc(xn_ready, 1)
                def largest_of(i, n, src):
                    dve.wait_ge(gu_done, n + 1 + (2 * FT if i == U else 0))
                    return magnitude(i, n, src[:, n // 2, 512 * (n % 2):512 * (n % 2) + 512])

                for n in range(2 * FT):
                    ins = largest_of(G, n, gate)
                st.link(dve, ins)
                scales(G, 2 * FT)
                for m in range(FT):
                    for h in range(2):
                        st.done(largest_of(U, 2 * m + h, up))
                    dve.wait_ge(sig_ready, m + 1)
                    st.link(dve, nc.vector.tensor_scalar(sig[:, m, :], sig[:, m, :], ROUND, 65535.0,
                                                         ALU.subtract, ALU.min))
                    st.link(dve, nc.vector.scalar_tensor_tensor(gate[:, m, :], sig[:, m, :], 1.0 / 65536.0, gate[:, m, :],
                                                                ALU.mult, ALU.mult))
                    st.link(dve, magnitude(H, m, gate[:, m, :]))
                scales(U, 2 * FT)
                scales(H, FT)
                for m in range(FT):
                    dve.wait_ge(h_ready, m + 1)
                    dve.wait_ge(up_ready, m + 1)
                    st.link(dve, nc.vector.tensor_tensor(gate[:, m, :], gate[:, m, :], up[:, m, :], ALU.mult))
                    st.link(dve, magnitude(O, m, gate[:, m, :]))
                scales(O, FT)
                for q in range(4):
                    for m in range(FT):
                        dve.wait_ge(o_1, FT * q + m + 1)
                        piece = gate[:, m, T // 4 * q:T // 4 * (q + 1)]
                        nc.vector.tensor_scalar(piece, piece, ROUND, scale[:, O:O + 1], ALU.subtract, ALU.mult) \
                            .then_inc(o_ready, 1)
                for t in range(NT):
                    dve.wait_ge(y_full, t + 1)
                    nc.vector.tensor_tensor(x[:, t, :], bank[t][:, 0:D], x[:, t, :], ALU.add)


def two_stage(eng, step, steps=None, per=None):
    step(-1)
    step(0)
    with eng.Fori(1, NT - 2) as u:
        if steps:
            steps.enter(u, 1, per)
        step(u)
        if steps:
            steps.leave(NT - 3)
    for u in range(NT - 2, NT + 1):
        step(u)


def context_attention(nc, a, sb_, sem, bank, c, x, w, loaded):
    with ExitStack() as own:
        def sb(name, shape, dt=F32):
            return sb_("cx_" + name, shape, dt, own)

        def csem(name):
            return sem("cx_" + name)

        SCALE = D ** -0.5
        xn, xT = sb("xn", [P, D]), sb("xT", [P, KT, P])
        stat, mv, veps, rstd = sb("stat", [P, 6]), sb("mv", [P, 2]), sb("veps", [P, 1]), sb("rstd", [P, 1])
        ctxT = [sb(f"ctxT{b}", [P, KT, SK]) for b in range(BT)]
        cn = [sb(f"ctx{b}", [P, 2, D]) for b in range(BT)]
        last = sb("last", [BT, D])
        qT, qk, qb = sb("qT", [P, KT, P]), sb("qk", [P, KT, P]), sb("qb", [P, 1])
        mx, nb = sb("mx", [P, 1]), sb("nb", [P, 1])
        raw, esum, rden = sb("raw", [P, SK]), sb("esum", [P, 1]), sb("rden", [P, 1])
        prob, plast = sb("prob", [P, SK]), sb("plast", [P, BT])
        pT, plT = sb("pT", [P, 2, P]), sb("plT", [BT, P])
        mix, mixT, y = sb("mix", [P, D]), sb("mixT", [P, KT, P]), sb("y", [P, D])
        x_bank, q_bank, k_bank, s_bank, p_bank, a_bank, y_bank, mixT_bank = bank[0:8]

        st = Steps(csem("dve_steps"))
        passed_dve, passed_sp = csem("passed_dve"), csem("passed_sp")
        ctxT_loaded = [csem(f"ctxT_loaded{b}") for b in range(BT)]
        ctx_loaded = [csem(f"ctx_loaded{b}") for b in range(BT)]
        last_loaded = csem("last_loaded")
        var_ready, rstd_ready, xn_ready = csem("var_ready"), csem("rstd_ready"), csem("xn_ready")
        xT_full, xT_done, q_full, q_done = csem("xT_full"), csem("xT_done"), csem("q_full"), csem("q_done")
        k_full, k_done, qb_ready = csem("k_full"), csem("k_done"), csem("qb_ready")
        s_full, nb_ready, e_ready = csem("s_full"), csem("nb_ready"), csem("e_ready")
        p_ready, p_full, p_done = csem("p_ready"), csem("p_full"), csem("p_done")
        a_full, a_done, y_full, y_done = csem("a_full"), csem("a_done"), csem("y_full"), csem("y_done")
        mixT_full, mixT_done = csem("mixT_full"), csem("mixT_done")

        with nc.Block() as block:
            @block.sync
            def _(sp):
                def turned(t):
                    for b in range(BT):
                        sp.dma_start(ctxT[b][:], a["ctx_T"][BT * t + b]).then_inc(ctxT_loaded[b], 16)

                def plain(t):
                    for b in range(BT):
                        sp.dma_start(cn[b][:], a["ctx"][BT * t + b, 0:SK - 1, :].rearrange("(i p) d -> p i d", p=P)) \
                            .then_inc(ctx_loaded[b], 16)
                    sp.dma_start(last[:], a["ctx_rows"][t]).then_inc(last_loaded, 16)

                turned(0)
                plain(0)
                with sp.Fori(1, NT) as t:
                    sp.wait_ge(s_full, t)
                    alone(sp, passed_sp)
                    turned(t)
                    sp.wait_ge(a_full, t)
                    alone(sp, passed_sp)
                    plain(t)

            @block.gpsimd
            def _(pool):
                def step(u):
                    if there(u + 2):
                        pool.wait_ge(var_ready, u + 3)
                        nc.gpsimd.tensor_tensor(rstd[:], veps[:], c.half[:, 0:1], ALU.pow).then_inc(rstd_ready, 1)

                pool.wait_ge(var_ready, 1)
                nc.gpsimd.tensor_tensor(rstd[:], veps[:], c.half[:, 0:1], ALU.pow).then_inc(rstd_ready, 1)
                two_stage(pool, step)

            @block.scalar
            def _(act):
                act.wait_ge(loaded["cross"], 16 * len(GROUPS["cross"]))

                def step(u):
                    n = u + 1
                    if there(n):
                        act.wait_ge(xT_full, n + 1)
                        nc.scalar.copy(xT[:], x_bank[:, 0:D].rearrange("p (k t) -> p k t", k=KT)).then_inc(xT_done, 1)
                        act.wait_ge(q_full, n + 1)
                        for m in range(KT):
                            ins = nc.scalar.activation(qT[:, m, :], q_bank[:, P * m:P * m + P], ACT.Identity,
                                                       bias=w["cx_bq"][:, m:m + 1])
                        ins.then_inc(q_done, 1)
                    if there(u):
                        act.wait_ge(p_full, u + 1)
                        at_least(act, a_full, u)
                        nc.scalar.copy(pT[:], p_bank[:, 0:2 * P].rearrange("p (i t) -> p i t", i=2))
                        nc.scalar.copy(plT[:], p_bank[0:BT, 2 * P:3 * P]).then_inc(p_done, 1)
                    if there(n):
                        act.wait_ge(k_full, n + 1)
                        at_least(act, qb_ready, n)
                        at_least(act, s_full, n)
                        nc.scalar.copy(qk[:], k_bank[:, 0:D].rearrange("p (k t) -> p k t", k=KT))
                        nc.scalar.mul(qb[:], k_bank[:, D:D + 1], SCALE).then_inc(k_done, 1)
                    if there(u):
                        act.wait_ge(a_full, u + 1)
                        at_least(act, mixT_full, u)
                        nc.scalar.copy(mix[:], a_bank[:, 0:D]).then_inc(a_done, 1)
                        act.wait_ge(mixT_full, u + 1)
                        at_least(act, y_full, u)
                        nc.scalar.copy(mixT[:], mixT_bank[:, 0:D].rearrange("p (k t) -> p k t", k=KT)) \
                            .then_inc(mixT_done, 1)
                    if there(n):
                        act.wait_ge(nb_ready, n + 1)
                        at_least(act, p_ready, n)
                        nc.scalar.activation(raw[:], s_bank[:, 0:SK], ACT.Exp, bias=nb[:], scale=SCALE,
                                             accum_out=esum[:]).then_inc(e_ready, 1)

                two_stage(act, step)

            @block.tensor
            def _(pe):
                pe.wait_ge(loaded["cross"], 16 * len(GROUPS["cross"]))

                def step(u):
                    n = u + 1
                    if there(n):
                        pe.wait_ge(xn_ready, n + 1)
                        at_least(pe, xT_done, n)
                        turn_tokens(nc, x_bank, xn, c).then_inc(xT_full, 1)
                    if there(u - 1):
                        pe.wait_ge(mixT_done, u)
                        at_least(pe, y_done, u - 1)
                        project_tokens(nc, y_bank, mixT, w["cx_v"]).then_inc(y_full, 1)
                    if there(n):
                        pe.wait_ge(xT_done, n + 1)
                        at_least(pe, q_done, n)
                        for m in range(KT):
                            for k in range(KT):
                                ins = nc.tensor.matmul(q_bank[:, P * m:P * m + P], w["cx_q"][:, k, P * m:P * m + P],
                                                       xT[:, k, :], start=(m == 0 and k == 0), stop=True,
                                                       skip_group_check=True)
                        ins.then_inc(q_full, 1)
                    if there(u):
                        pe.wait_ge(p_ready, u + 1)
                        at_least(pe, p_done, u)
                        for i in range(2):
                            nc.tensor.transpose(p_bank[:, P * i:P * i + P], prob[:, P * i:P * i + P], c.ident)
                        nc.tensor.transpose(p_bank[0:BT, 2 * P:3 * P], plast[:], c.ident).then_inc(p_full, 1)
                    if there(n):
                        pe.wait_ge(q_done, n + 1)
                        at_least(pe, k_done, n)
                        for m in range(KT):
                            for k in range(KT):
                                nc.tensor.matmul(k_bank[:, P * m:P * m + P], w["cx_k"][:, k, P * m:P * m + P],
                                                 qT[:, k, :], start=(m == 0 and k == 0), stop=True,
                                                 skip_group_check=True)
                        for k in range(KT):
                            ins = nc.tensor.matmul(k_bank[:, D:D + 1], qT[:, k, :], w["cx_bk"][:, k:k + 1],
                                                   start=False, stop=True, skip_group_check=True)
                        ins.then_inc(k_full, 1)
                    if there(u):
                        pe.wait_ge(p_done, u + 1)
                        at_least(pe, a_done, u)
                        for b in range(BT):
                            pe.wait_ge(ctx_loaded[b], 16 * (u + 1))
                            for i in range(2):
                                nc.tensor.matmul(a_bank[SQ * b:SQ * b + SQ, 0:D], pT[:, i, SQ * b:SQ * b + SQ],
                                                 cn[b][:, i, :], start=(i == 0), stop=False, skip_group_check=True)
                        pe.wait_ge(last_loaded, 16 * (u + 1))
                        nc.tensor.matmul(a_bank[:, 0:D], plT[:], last[:], start=False, stop=True,
                                         skip_group_check=True).then_inc(a_full, 1)
                    if there(n):
                        pe.wait_ge(k_done, n + 1)
                        at_least(pe, e_ready, n)
                        for b in range(BT):
                            pe.wait_ge(ctxT_loaded[b], 16 * (n + 1))
                            for k in range(KT):
                                ins = nc.tensor.matmul(s_bank[SQ * b:SQ * b + SQ, 0:SK], qk[:, k, SQ * b:SQ * b + SQ],
                                                       ctxT[b][:, k, :], start=(k == 0), stop=(k == KT - 1))
                        ins.then_inc(s_full, 1)
                    if there(u):
                        pe.wait_ge(a_done, u + 1)
                        at_least(pe, mixT_done, u)
                        turn_tokens(nc, mixT_bank, mix, c).then_inc(mixT_full, 1)

                two_stage(pe, step)

            @block.vector
            def _(dve):
                def norm(u):
                    st.link(dve, nc.vector.bn_stats(stat[:], x[:, u, :]))
                    alone(dve, passed_dve)
                    st.link(dve, nc.vector.bn_aggr(mv[:], stat[:]))
                    nc.vector.tensor_scalar(veps[:], mv[:, 1:2], LN_EPS, None, ALU.add).then_inc(var_ready, 1)
                    dve.wait_ge(rstd_ready, u + 1)
                    at_least(dve, xT_full, u)
                    nc.vector.tensor_scalar(xn[:], x[:, u, :], mv[:, 0:1], rstd[:], ALU.subtract, ALU.mult) \
                        .then_inc(xn_ready, 1)

                def step(u):
                    n = u + 1
                    if there(u + 2) and not (isinstance(u, int) and u < 0):
                        norm(u + 2)
                    if there(u - 1):
                        dve.wait_ge(y_full, u)
                        st.link(dve, nc.vector.tensor_tensor(y[:], y_bank[:, 0:D], w["cx_bv"][:], ALU.add))
                        nc.vector.tensor_tensor(x[:, u - 1, :], x[:, u - 1, :], y[:], ALU.add).then_inc(y_done, 1)
                    if there(n):
                        dve.wait_ge(s_full, n + 1)
                        dve.wait_ge(k_done, n + 1)
                        at_least(dve, e_ready, n)
                        st.link(dve, nc.vector.tensor_reduce(mx[:], s_bank[:, 0:SK], AX.X, ALU.max))
                        st.link(dve, nc.vector.tensor_scalar(mx[:], mx[:], SCALE, qb[:], ALU.mult, ALU.add))
                        nc.vector.tensor_tensor(nb[:], qb[:], mx[:], ALU.subtract).then_inc(nb_ready, 1)
                        dve.wait_ge(e_ready, n + 1)
                        at_least(dve, p_full, n)
                        st.link(dve, nc.vector.reciprocal(rden[:], esum[:]))
                        st.link(dve, nc.vector.tensor_scalar(prob[:], raw[:], rden[:], None, ALU.mult))
                        nc.vector.tensor_scalar(plast[:], c.row, prob[:, SK - 1:SK], None, ALU.mult) \
                            .then_inc(p_ready, 1)
                        dve.sem_inc(qb_ready, 1)

                dve.wait_ge(loaded["cross"], 16 * len(GROUPS["cross"]))
                norm(0)
                norm(1)
                two_stage(dve, step, steps=st, per=2 + 4 + 1)
def segment_attention(nc, a, sb_, sem, psum, bank, c, x, w, loaded):
    with ExitStack() as own:
        def sb(name, shape, dt=F32):
            return sb_("sg_" + name, shape, dt, own)

        def gsem(name):
            return sem("sg_" + name)

        kinds = ("lt", "st")
        xn, xT = sb("xn", [P, D]), sb("xT", [P, KT, P])
        stat, mv, veps, rstd = sb("stat", [P, 6]), sb("mv", [P, 2]), sb("veps", [P, 1]), sb("rstd", [P, 1])
        qT, kT = sb("qT", [P, KT, P]), sb("kT", [P, KT, P])
        v, vbd, kbd = sb("v", [P, D]), sb("vbd", [P, NG, BT, 64]), sb("kbd", [P, KT, BT, 4, SQ])
        score, prob, pT = (sb(name, [P, NH, SQ]) for name in ("score", "prob", "pT"))
        mx, rden, o, oT = sb("mx", [P, NH]), sb("rden", [P, NG * BT]), sb("o", [P, D]), sb("oT", [P, KT, P])
        longT, shortT, short = sb("longT", [P, KT, P]), sb("shortT", [P, KT, P]), sb("short", [P, D])
        lmax, first, chosen = sb("lmax", [P, 1]), sb("first", [P, NE]), sb("chosen", [P, 1])
        onehot, hotT = sb("onehot", [P, NE]), sb("hotT", [NE, P])
        same, shut = sb("same", [P, SQ]), sb("shut", [P, SQ])
        count, single, several = sb("count", [P, 1]), sb("single", [P, 1]), sb("several", [P, 1])
        x_kept, x_single = sb("x_kept", [P, D]), sb("x_single", [P, D])
        s_banks, qk_bank, o_banks = psum[:, 0:2, :], bank[3], psum[:, 5:7, :]
        x_part, hot_part = bank[2][:, 0:D], bank[2][0:NE, 3 * P:4 * P]
        sums, logits = bank[2][:, D:D + NG * BT], bank[4][:, D + SQ:D + SQ + NE]
        v_part, same_part = bank[4][:, 0:D], bank[4][:, D:D + SQ]
        y_part, fused_part, short_part = bank[7][:, 0:D], bank[7][:, 0:D], bank[7][:, D:2 * D]

        st = Steps(gsem("dve_steps"))
        passed_dve, passed_pool, passed_pe = gsem("passed_dve"), gsem("passed_pool"), gsem("passed_pe")
        var_ready, rstd_ready, xn_ready = gsem("var_ready"), gsem("rstd_ready"), gsem("xn_ready")
        xT_full, xT_done, logits_full, hot_ready = gsem("xT_full"), gsem("xT_done"), gsem("logits_full"), gsem("hot_ready")
        hot_full, hot_done, same_full, same_done = gsem("hot_full"), gsem("hot_done"), gsem("same_full"), gsem("same_done")
        short_ready, shT_full, shT_done = gsem("short_ready"), gsem("shT_full"), gsem("shT_done")
        fused_read, x_kept_ready, single_ready = gsem("fused_read"), gsem("x_kept_ready"), gsem("single_ready")
        fused_full, bias_added, sums_read = gsem("fused_full"), gsem("bias_added"), gsem("sums_read")
        qk_full, k_ready, qk_done = gsem("qk_full"), gsem("k_ready"), gsem("qk_done")
        kbd_ready = gsem("kbd_ready")
        v_full, v_done, vbd_ready = gsem("v_full"), gsem("v_done"), gsem("vbd_ready")
        s_full, sub_ready, p_ready, pT_ready = gsem("s_full"), gsem("sub_ready"), gsem("p_ready"), gsem("pT_ready")
        o_full, o_done, oT_ready = gsem("o_full"), gsem("o_done"), gsem("oT_ready")
        y_full, y_done = gsem("y_full"), gsem("y_done")

        def steps_of_tiles(eng, step, steps=None, per=None):
            for t in (-1, 0):
                for s in range(2):
                    step(t, s)
            with eng.Fori(1, NT - 2) as t:
                if steps:
                    steps.enter(t, 1, per)
                for s in range(2):
                    step(t, s)
                if steps:
                    steps.leave(NT - 3)
            for t in range(NT - 2, NT + 1):
                for s in range(2):
                    step(t, s)

        def parts(t, s):
            return there(t), there(t + s), there(t + 1)

        with nc.Block() as block:
            @block.gpsimd
            def _(pool):
                def root(t):
                    pool.wait_ge(var_ready, t + 1)
                    nc.gpsimd.tensor_tensor(rstd[:], veps[:], c.half[:, 0:1], ALU.pow).then_inc(rstd_ready, 1)

                def step(t, s):
                    u = 2 * t + s
                    has_c, has_b, has_a = parts(t, s)
                    if s == 1 and has_a and there(t + 2):
                        root(t + 2)
                    if has_a:
                        pool.wait_ge(k_ready, u + 3)
                        at_least(pool, s_full, u + 2)
                        alone(pool, passed_pool)
                        for m in range(KT):
                            ins = spread_heads(nc.gpsimd, kbd[:, m, :, :, :], kT[:, m, :], c.quarter)
                        ins.then_inc(kbd_ready, 1)
                    if s == 0 and has_a:
                        pool.wait_ge(xn_ready, t + 2)
                        alone(pool, passed_pool)
                        nc.gpsimd.tensor_tensor(x[:, t + 1, :], x[:, t + 1, :], w["fus_b"][:], ALU.add) \
                            .then_inc(bias_added, 1)
                    if has_b:
                        pool.wait_ge(v_done, u + 2)
                        at_least(pool, o_full, u + 1)
                        alone(pool, passed_pool)
                        spread_batches(nc.gpsimd, vbd, v, c).then_inc(vbd_ready, 1)

                pool.wait_ge(loaded["segs"], 16 * len(GROUPS["segs"]))
                root(0)
                steps_of_tiles(pool, step)

            @block.scalar
            def _(act):
                act.wait_ge(loaded["segs"], 16 * len(GROUPS["segs"]))

                def step(t, s):
                    u = 2 * t + s
                    has_c, has_b, has_a = parts(t, s)
                    if s == 0 and has_a:
                        act.wait_ge(xT_full, t + 2)
                        at_least(act, v_full, u + 2)
                        at_least(act, qk_full, u + 2)
                        nc.scalar.copy(xT[:], x_part.rearrange("p (k t) -> p k t", k=KT)).then_inc(xT_done, 1)
                    if s == 1 and there(t):
                        act.wait_ge(y_full, u)
                        at_least(act, fused_full, t)
                        for m in range(KT):
                            ins = nc.scalar.activation(longT[:, m, :], y_part[:, P * m:P * m + P], ACT.Identity,
                                                       bias=w["lt_bo"][:, m:m + 1])
                        ins.then_inc(y_done, 1)
                    if s == 1 and has_a:
                        act.wait_ge(hot_full, t + 2)
                        nc.scalar.copy(hotT[:], hot_part).then_inc(hot_done, 1)
                    if has_a:
                        bias = w[kinds[s] + "_bqk"]
                        act.wait_ge(qk_full, u + 3)
                        at_least(act, s_full, u + 2)
                        for m in range(KT):
                            at = P * (KT + m)
                            ins = nc.scalar.activation(kT[:, m, :], qk_bank[:, at:at + P], ACT.Identity,
                                                       bias=bias[:, KT + m:KT + m + 1])
                        ins.then_inc(k_ready, 1)
                        for m in range(KT):
                            ins = nc.scalar.activation(qT[:, m, :], qk_bank[:, P * m:P * m + P], ACT.Identity,
                                                       bias=bias[:, m:m + 1])
                        ins.then_inc(qk_done, 1)
                    if has_b:
                        act.wait_ge(sub_ready, u + 2)
                        at_least(act, pT_ready, u + 1)
                        nc.scalar.activation(prob[:], score[:], ACT.Exp).then_inc(p_ready, 1)
                    if s == 0 and there(t - 1):
                        act.wait_ge(shT_full, t)
                        nc.scalar.copy(shortT[:], short_part.rearrange("p (k t) -> p k t", k=KT)).then_inc(shT_done, 1)
                    if s == 0 and has_a:
                        at_least(act, single_ready, t + 1)
                        nc.scalar.copy(x_kept[:], xn[:]).then_inc(x_kept_ready, 1)
                steps_of_tiles(act, step)

            @block.tensor
            def _(pe):
                pe.wait_ge(loaded["segs"], 16 * len(GROUPS["segs"]))

                def project_output(u, t, s):
                    pe.wait_ge(oT_ready, u + 1)
                    at_least(pe, y_done, u)
                    if s == 0:
                        at_least(pe, fused_read, t)
                        for m in range(KT):
                            for k in range(KT):
                                ins = nc.tensor.matmul(y_part[:, P * m:P * m + P],
                                                       w["lt_o"][:, k, P * m:P * m + P], oT[:, k, :],
                                                       start=(m == 0 and k == 0), stop=True, skip_group_check=True)
                        ins.then_inc(y_full, 1)
                    else:
                        project_tokens(nc, y_part, oT, w["st_o"]).then_inc(y_full, 1)

                def step(t, s):
                    u = 2 * t + s
                    has_c, has_b, has_a = parts(t, s)
                    if has_b:
                        weight = w[kinds[1 - s] + "_qkv"]
                        pe.wait_ge(kbd_ready, u + 2)
                        pe.wait_ge(qk_done, u + 2)
                        at_least(pe, sub_ready, u + 1)
                        alone(pe, passed_pe)
                        per_batch(nc, s_banks, tokens(qT), heads_apart(kbd), 0, True).then_inc(s_full, 1)
                        at_least(pe, v_done, u + 1)
                        if s == 0:
                            at_least(pe, same_done, t + 1)
                        elif has_a:
                            pe.wait_ge(hot_ready, t + 2)
                        project_tokens(nc, v_part, xT, weight[:, :, 2 * D:3 * D]).then_inc(v_full, 1)
                    if s == 0 and has_a:
                        pe.wait_ge(xn_ready, t + 2)
                        at_least(pe, sums_read, u)
                        turn_tokens(nc, x_part, xn, c).then_inc(xT_full, 1)
                    if there(t - 1 + s):
                        project_output(u - 1, t - 1 + s, 1 - s)
                    if s == 1 and has_a:
                        at_least(pe, sums_read, u)
                        nc.tensor.transpose(hot_part, onehot[:], c.ident).then_inc(hot_full, 1)
                    if has_a:
                        if s == 0:
                            pe.wait_ge(xT_done, t + 2)
                        at_least(pe, qk_done, u + 2)
                        project_qk(nc, qk_bank, w[kinds[s] + "_qkv"], xT).then_inc(qk_full, 1)
                    if s == 0 and has_a:
                        at_least(pe, v_done, u + 2)
                        for k in range(KT):
                            ins = nc.tensor.matmul(logits, xT[:, k, :], w["protos"][:, k, :],
                                                   start=(k == 0), stop=(k == KT - 1))
                        ins.then_inc(logits_full, 1)
                    if s == 0 and there(t - 1):
                        pe.wait_ge(short_ready, t)
                        turn_tokens(nc, short_part, short, c).then_inc(shT_full, 1)
                    if s == 1 and has_a:
                        pe.wait_ge(hot_done, t + 2)
                        pe.wait_ge(v_done, u + 2)
                        alone(pe, passed_pe)
                        for b in range(BT):
                            ins = nc.tensor.matmul(same_part[SQ * b:SQ * b + SQ, :], hotT[:, SQ * b:SQ * b + SQ],
                                                   hotT[:, SQ * b:SQ * b + SQ], start=True, stop=True,
                                                   skip_group_check=True)
                        ins.then_inc(same_full, 1)
                    if has_c:
                        pe.wait_ge(pT_ready, u + 1)
                        pe.wait_ge(vbd_ready, u + 1)
                        at_least(pe, o_done, u)
                        weigh_values(nc, o_banks, sums, pT, vbd, c).then_inc(o_full, 1)
                    if s == 0 and there(t - 1):
                        pe.wait_ge(shT_done, t)
                        for k in range(2 * KT):
                            lhs = (longT if k < KT else shortT)[:, k % KT, :]
                            ins = nc.tensor.matmul(fused_part, lhs, w["fus"][:, k, :],
                                                   start=(k == 0), stop=(k == 2 * KT - 1))
                        ins.then_inc(fused_full, 1)

                steps_of_tiles(pe, step)

            @block.vector
            def _(dve):
                def norm_stats(t):
                    st.link(dve, nc.vector.bn_stats(stat[:], x[:, t, :]))
                    alone(dve, passed_dve)
                    st.link(dve, nc.vector.bn_aggr(mv[:], stat[:]))
                    nc.vector.tensor_scalar(veps[:], mv[:, 1:2], LN_EPS, None, ALU.add).then_inc(var_ready, 1)

                def norm_apply(t):
                    dve.wait_ge(rstd_ready, t + 1)
                    at_least(dve, xT_full, t)
                    at_least(dve, x_kept_ready, t)
                    nc.vector.tensor_scalar(xn[:], x[:, t, :], mv[:, 0:1], rstd[:], ALU.subtract, ALU.mult) \
                        .then_inc(xn_ready, 1)

                flat = [P, NH, SQ]

                def maximum_off(n):
                    st.link(dve, nc.vector.tensor_reduce(mx[:], score[:], AX.X, ALU.max))
                    nc.vector.tensor_tensor(score[:], score[:], mx[:].unsqueeze(2).broadcast_to(flat), ALU.subtract) \
                        .then_inc(sub_ready, 1)

                def step(t, s):
                    u = 2 * t + s
                    has_c, has_b, has_a = parts(t, s)
                    if has_c:
                        dve.wait_ge(p_ready, u + 1)
                        at_least(dve, o_full, u)
                        alone(dve, passed_dve)
                        turn_blocks(nc, pT, prob).then_inc(pT_ready, 1)
                    if has_b:
                        dve.wait_ge(v_full, u + 2)
                        at_least(dve, vbd_ready, u + 1)
                        nc.vector.tensor_tensor(v[:], v_part, w[kinds[1 - s] + "_bv"][:], ALU.add).then_inc(v_done, 1)
                        if s == 1 and has_a and there(t + 2):
                            norm_stats(t + 2)
                        dve.wait_ge(s_full, u + 2)
                        at_least(dve, p_ready, u + 1)
                        in_heads = "p f (n k) -> p f n k"
                        banks = s_banks[:, :, 0:D].rearrange(in_heads, k=SQ)
                        each = [P, 2, NH // 2, SQ]
                        if s == 0:
                            for f in range(2):
                                ins = nc.vector.tensor_tensor(
                                    score[:, 8 * f:8 * f + 8, :], banks[:, f, :, :],
                                    same[:].unsqueeze(1).broadcast_to([P, NH // 2, SQ]), ALU.mult)
                                if f == 0:
                                    st.done(ins)
                            st.link(dve, ins)
                            st.link(dve, nc.vector.tensor_tensor(score[:], score[:],
                                                                 shut[:].unsqueeze(1).broadcast_to(flat), ALU.add))
                        else:
                            st.link(dve, nc.vector.tensor_reduce(mx[:].rearrange("p (f n) -> p f n", f=2), banks,
                                                                 AX.X, ALU.max))
                            nc.vector.tensor_tensor(
                                score[:].rearrange("p (f n) k -> p f n k", f=2), banks,
                                mx[:].rearrange("p (f n) -> p f n", f=2).unsqueeze(3).broadcast_to(each),
                                ALU.subtract).then_inc(sub_ready, 1)
                    if s == 0 and there(t - 1):
                        dve.wait_ge(y_full, u)
                        at_least(dve, shT_full, t - 1)
                        nc.vector.tensor_tensor(short[:], y_part, w["st_bo"][:], ALU.add).then_inc(y_done, 1)
                        dve.wait_ge(y_done, u)
                        nc.vector.scalar_tensor_tensor(short[:], short[:], several[:], x_single[:], ALU.mult, ALU.add) \
                            .then_inc(short_ready, 1)
                        dve.wait_ge(short_ready, t)
                    if has_b and s == 0:
                        maximum_off(u + 1)
                    if s == 0 and there(t):
                        st.link(dve, nc.vector.tensor_scalar(several[:], single[:], -1.0, 1.0, ALU.mult, ALU.add))
                        dve.wait_ge(x_kept_ready, t + 1)
                        nc.vector.tensor_scalar(x_single[:], x_kept[:], single[:], None, ALU.mult) \
                            .then_inc(single_ready, 1)
                    if s == 0 and has_a:
                        dve.wait_ge(logits_full, t + 2)
                        st.link(dve, nc.vector.tensor_reduce(lmax[:], logits, AX.X, ALU.max))
                        st.link(dve, nc.vector.tensor_scalar(first[:], logits, lmax[:], None, ALU.is_ge))
                        st.link(dve, nc.vector.tensor_tensor(first[:], first[:], c.exp8, ALU.mult))
                        st.link(dve, nc.vector.tensor_reduce(chosen[:], first[:], AX.X, ALU.min))
                        nc.vector.tensor_scalar(onehot[:], c.exp8, chosen[:], None, ALU.is_equal).then_inc(hot_ready, 1)
                    if s == 1 and has_a:
                        dve.wait_ge(same_full, t + 2)
                        nc.vector.tensor_copy(same[:], same_part).then_inc(same_done, 1)
                        dve.wait_ge(same_done, t + 2)
                        st.link(dve, nc.vector.tensor_scalar(shut[:], same[:], 1.0, 1e9, ALU.subtract, ALU.mult))
                        st.link(dve, nc.vector.tensor_reduce(count[:], same[:], AX.X, ALU.add))
                        st.link(dve, nc.vector.tensor_scalar(single[:], count[:], 1.0, None, ALU.is_equal))
                        if there(t + 2):
                            norm_apply(t + 2)
                    if has_c:
                        dve.wait_ge(o_full, u + 1)
                        nc.vector.reciprocal(rden[:], sums).then_inc(sums_read, 1)
                        dve.wait_ge(sums_read, u + 1)
                        own_heads(nc, o, o_banks, rden).then_inc(o_done, 1)
                        dve.wait_ge(o_done, u + 1)
                        at_least(dve, y_full, u)
                        alone(dve, passed_dve)
                        to_features(nc, oT, o).then_inc(oT_ready, 1)
                    if s == 0 and there(t - 1):
                        dve.wait_ge(fused_full, t)
                        dve.wait_ge(bias_added, t)
                        nc.vector.tensor_tensor(x[:, t - 1, :], fused_part, x[:, t - 1, :], ALU.add) \
                            .then_inc(fused_read, 1)

                dve.wait_ge(loaded["segs"], 16 * len(GROUPS["segs"]))
                norm_stats(0)
                norm_apply(0)
                steps_of_tiles(dve, step, steps=st, per=(3 + 1 + 1 + 4) + (1 + 3 + 2))




def experts(nc, a, sb_, sem, bank, c, x, w, loaded):
    with ExitStack() as own:
        def sb(name, shape, dt=F32):
            return sb_("ex_" + name, shape, dt, own)

        def esem(name):
            return sem("ex_" + name)

        T = NT * P
        NC = len(FCH)
        w1 = [sb(f"w1_{i}", [P, KT, 2 * FE]) for i in range(2)]
        w2 = [sb(f"w2_{i}", [P, NC, D]) for i in range(2)]
        stats, mv = sb("stats", [P, NT, 6]), sb("mv", [P, NT, 2])
        veps, rstd = sb("veps", [P, NT]), sb("rstd", [P, NT])
        xn, xT = sb("xn", [P, NT, D]), sb("xT", [P, KT, T])
        logit, raw, prob = sb("logit", [P, NT, NE]), sb("raw", [P, NT, NE]), sb("prob", [P, NT, NE])
        rest, tie, hot = sb("rest", [P, NT, NE]), sb("tie", [P, NT, NE]), [sb(f"hot{i}", [P, NT, NE]) for i in range(2)]
        most, which = sb("most", [P, NT]), sb("which", [P, NT])
        route = sb("route", [P, NE * NT])
        silu = [sb(f"silu{i}", [P, 512]) for i in range(2)]
        g = [sb(f"g{i}", [P, NC, T]) for i in range(2)]
        y_bank, o_bank = bank[0:4], bank[4:8]

        st = Steps(esem("dve_steps"))
        w1_loaded, w2_loaded = [esem("w1_loaded0"), esem("w1_loaded1")], [esem("w2_loaded0"), esem("w2_loaded1")]
        veps_ready, rstd_ready, xn_ready = esem("veps_ready"), esem("rstd_ready"), esem("xn_ready")
        xT_full, xT_done, l_full, l_done = esem("xT_full"), esem("xT_done"), esem("l_full"), esem("l_done")
        sub_ready, e_ready, passed_sp = esem("sub_ready"), esem("e_ready"), esem("passed_sp")
        up_full, silu_ready, g_ready = esem("up_full"), esem("silu_ready"), esem("g_ready")
        o_full, o_done = esem("o_full"), esem("o_done")
        PIECES = 2 * NC

        def schedule(up, down, eng, steps=None, per=None):
            up(0, 0, 1)
            up(1, 1, 1)
            down(0, 0, 1)
            up(2, 0, 2)
            down(1, 1, 1)
            with eng.Fori(1, NE // 2 - 1) as j:
                if steps:
                    steps.enter(j, 1, per)
                up(2 * j + 1, 1, j + 1)
                down(2 * j, 0, j + 1)
                up(2 * j + 2, 0, j + 2)
                down(2 * j + 1, 1, j + 1)
                if steps:
                    steps.leave(NE // 2 - 2)
            up(NE - 1, 1, NE // 2)
            down(NE - 2, 0, NE // 2)
            down(NE - 1, 1, NE // 2)

        with nc.Block() as block:
            @block.sync
            def _(sp):
                def up_weights(e, i):
                    sp.dma_start(w1[i][:], a["w1"][e]).then_inc(w1_loaded[i], 16)

                def down_weights(e, i):
                    sp.dma_start(w2[i][:, 0:2, :], a["w2"][e, 0:2 * P, :].rearrange("(c p) d -> p c d", p=P)) \
                        .then_inc(w2_loaded[i], 16)
                    sp.dma_start(w2[i][0:FE - 2 * P, 2, :], a["w2"][e, 2 * P:FE, :]).then_inc(w2_loaded[i], 16)

                for i in range(2):
                    up_weights(i, i)
                    down_weights(i, i)
                with sp.Fori(1, NE // 2) as j:
                    for i in range(2):
                        sp.wait_ge(up_full, PIECES * (2 * j - 1 + i))
                        alone(sp, passed_sp)
                        up_weights(2 * j + i, i)
                        sp.wait_ge(o_full, NT * (2 * j - 1 + i))
                        alone(sp, passed_sp)
                        down_weights(2 * j + i, i)

            @block.gpsimd
            def _(pool):
                pool.wait_ge(veps_ready, 1)
                nc.gpsimd.tensor_tensor(rstd[:], veps[:], c.half[:, 0:NT], ALU.pow).then_inc(rstd_ready, 1)

            @block.scalar
            def _(act):
                for i in range(NT // 2):
                    act.wait_ge(xT_full, i + 1)
                    src = bank[i % 2][:].rearrange("p (j k t) -> p j k t", j=2, k=KT)
                    for j in range(2):
                        at = P * (2 * i + j)
                        ins = nc.scalar.copy(xT[:, :, at:at + P], src[:, j, :, :])
                    ins.then_inc(xT_done, 1)
                act.wait_ge(sub_ready, 1)
                nc.scalar.activation(raw[:], logit[:], ACT.Exp).then_inc(e_ready, 1)

                def up(e, i, r):
                    for n in range(PIECES):
                        rows = FCH[n % NC][1]
                        act.wait_ge(up_full, PIECES * e + n + 1)
                        at_least(act, g_ready, PIECES * e + n - 1)
                        nc.scalar.activation(silu[n % 2][0:rows, :], y_bank[2 * (n % 2)][0:rows, :], ACT.Silu) \
                            .then_inc(silu_ready, 1)

                schedule(up, lambda e, i, r: None, act)

            @block.tensor
            def _(pe):
                pe.wait_ge(loaded["router"], 16)
                for i in range(NT // 2):
                    pe.wait_ge(xn_ready, i + 1)
                    at_least(pe, xT_done, i - 1)
                    for j in range(2):
                        ins = turn_tokens(nc, bank[i % 2][:, D * j:D * j + D], xn[:, 2 * i + j, :], c)
                    ins.then_inc(xT_full, 1)
                pe.wait_ge(xT_done, NT // 2)
                for t in range(NT):
                    for k in range(KT):
                        ins = nc.tensor.matmul(o_bank[3][:, NE * t:NE * t + NE], xT[:, k, P * t:P * t + P],
                                               w["router"][:, k, :], start=(t == 0 and k == 0), stop=True,
                                               skip_group_check=True)
                ins.then_inc(l_full, 1)

                def up(e, i, r):
                    pe.wait_ge(w1_loaded[i], 16 * r)
                    for n in range(PIECES):
                        h, ch = n // NC, n % NC
                        lo, rows = FCH[ch]
                        at_least(pe, g_ready, PIECES * e + n - 1)
                        for part in range(2):
                            for k in range(KT):
                                at = FE * part + lo
                                ins = nc.tensor.matmul(y_bank[2 * (n % 2) + part][0:rows, :], w1[i][:, k, at:at + rows],
                                                       xT[:, k, 512 * h:512 * h + 512], start=(k == 0),
                                                       stop=(k == KT - 1))
                        ins.then_inc(up_full, 1)

                def down(e, i, r):
                    pe.wait_ge(w2_loaded[i], 32 * r)
                    for t in range(NT):
                        if t % (NT // 2) == 0:
                            pe.wait_ge(g_ready, PIECES * e + NC * (2 * t // NT + 1))
                        at_least(pe, o_done, NT * e + t - 3)
                        for ch, (lo, rows) in enumerate(FCH):
                            ins = nc.tensor.matmul(o_bank[t % 4][:, 0:D], g[i][0:rows, ch, P * t:P * t + P],
                                                   w2[i][0:rows, ch, :], start=(ch == 0), stop=(ch == NC - 1))
                        ins.then_inc(o_full, 1)

                def first_down(e, i, r):
                    if isinstance(e, int) and e == 0:
                        pe.wait_ge(l_done, 1)
                    down(e, i, r)

                schedule(up, first_down, pe)

            @block.vector
            def _(dve):
                for t in range(NT):
                    ins = nc.vector.bn_stats(stats[:, t, :], x[:, t, :])
                st.link(dve, ins)
                for t in range(NT):
                    ins = nc.vector.bn_aggr(mv[:, t, :], stats[:, t, :])
                st.link(dve, ins)
                nc.vector.tensor_scalar(veps[:], mv[:, :, 1], LN_EPS, None, ALU.add).then_inc(veps_ready, 1)
                dve.wait_ge(rstd_ready, 1)
                for t in range(NT):
                    ins = nc.vector.tensor_scalar(xn[:, t, :], x[:, t, :], mv[:, t, 0:1], rstd[:, t:t + 1],
                                                  ALU.subtract, ALU.mult)
                    if t % 2:
                        ins.then_inc(xn_ready, 1)

                each = [P, NT, NE]
                dve.wait_ge(l_full, 1)
                nc.vector.tensor_copy(logit[:], o_bank[3][:, 0:NT * NE].rearrange("p (t e) -> p t e", t=NT)) \
                    .then_inc(l_done, 1)
                dve.wait_ge(l_done, 1)

                def over(v):
                    return v[:].unsqueeze(2).broadcast_to(each)

                st.link(dve, nc.vector.tensor_reduce(most[:], logit[:], AX.X, ALU.max))
                nc.vector.tensor_tensor(logit[:], logit[:], over(most), ALU.subtract).then_inc(sub_ready, 1)
                dve.wait_ge(e_ready, 1)
                st.link(dve, nc.vector.tensor_reduce(most[:], raw[:], AX.X, ALU.add))
                st.link(dve, nc.vector.reciprocal(which[:], most[:]))
                st.link(dve, nc.vector.tensor_tensor(prob[:], raw[:], over(which), ALU.mult))
                number = c.exp8.unsqueeze(1).broadcast_to(each)
                for k in range(2):
                    of = (prob, rest)[k]
                    st.link(dve, nc.vector.tensor_reduce(most[:], of[:], AX.X, ALU.max))
                    st.link(dve, nc.vector.tensor_tensor(tie[:], of[:], over(most), ALU.is_ge))
                    st.link(dve, nc.vector.tensor_tensor(tie[:], tie[:], number, ALU.mult))
                    st.link(dve, nc.vector.tensor_reduce(which[:], tie[:], AX.X, ALU.min))
                    st.link(dve, nc.vector.tensor_tensor(hot[k][:], number, over(which), ALU.is_equal))
                    if k == 0:
                        st.link(dve, nc.vector.scalar_tensor_tensor(rest[:], hot[0][:], -2.0, prob[:], ALU.mult, ALU.add))
                st.link(dve, nc.vector.tensor_tensor(hot[0][:], hot[0][:], hot[1][:], ALU.add))
                st.link(dve, nc.vector.tensor_tensor(route[:].rearrange("p (e t) -> p t e", e=NE), prob[:], hot[0][:],
                                                     ALU.mult))

                def up(e, i, r):
                    for n in range(PIECES):
                        h, ch = n // NC, n % NC
                        rows = FCH[ch][1]
                        dve.wait_ge(silu_ready, PIECES * e + n + 1)
                        nc.vector.tensor_tensor(g[i][0:rows, ch, 512 * h:512 * h + 512],
                                                y_bank[2 * (n % 2) + 1][0:rows, :], silu[n % 2][0:rows, :], ALU.mult) \
                            .then_inc(g_ready, 1)

                def down(e, i, r):
                    for t in range(NT):
                        dve.wait_ge(o_full, NT * e + t + 1)
                        at_least(dve, o_done, NT * (e - 1) + t + 1)
                        if isinstance(e, int):
                            p_route = route[:, NT * e + t:NT * e + t + 1]
                        else:
                            p_route = route[:, bass.ds(e * NT + t, 1)]
                        nc.vector.scalar_tensor_tensor(x[:, t, :], o_bank[t % 4][:, 0:D], p_route, x[:, t, :],
                                                       ALU.mult, ALU.add).then_inc(o_done, 1)

                schedule(up, down, dve)


def _blocks(weight):
    wt = np.asarray(weight).T
    return np.ascontiguousarray(wt.reshape(wt.shape[0] // P, P, wt.shape[1]).transpose(1, 0, 2))


def _plain(weight):
    wt = np.asarray(weight)
    return np.ascontiguousarray(wt.reshape(wt.shape[0] // P, P, wt.shape[1]).transpose(1, 0, 2))


def _by_head(weight):
    wt = np.asarray(weight).reshape(KT, 2, 4, DH, -1)
    return np.ascontiguousarray(wt.transpose(2, 0, 3, 1, 4).reshape(P, 2, -1))


def _column(vector):
    return np.ascontiguousarray(np.asarray(vector).reshape(-1, P).T)


def _constants():
    cst = np.zeros((P, C_END), np.float32)
    p = np.arange(P)[:, None]
    cst[:, C_ID:C_ID + P] = np.eye(P)
    cst[:, C_HEADQ:C_HEADQ + P] = (p % 64) // DH == np.arange(P)[None] // SQ
    cst[:, C_HEAD:C_HEAD + 4] = (p % 64) // DH == np.arange(4)[None]
    cst[:, C_QUARTER:C_QUARTER + 4] = cst[:, C_HEAD:C_HEAD + 4] * DH ** -0.5
    cst[:, C_HEAD8:C_HEAD8 + 8] = p // DH == np.arange(8)[None]
    cst[:, C_ROW:C_ROW + 4] = p // SQ == np.arange(4)[None]
    cst[:, C_EQ:C_EQ + SQ] = p % SQ == np.arange(SQ)[None]
    cst[:, C_CAUSAL:C_CAUSAL + SQ] = np.where(np.arange(SQ)[None] > p % SQ, -1e9, 0.0)
    ratio = 2.0 ** (-8.0 / NH)
    cst[:, C_SLOPE:C_SLOPE + NG] = [[ratio ** (4 * g + q // SQ + 1) for g in range(NG)] for q in range(P)]
    cst[:, C_EXP8:C_EXP8 + 8] = np.arange(8)[None] - 8.0
    cst[0:16, C_LAST:C_LAST + 16] = np.eye(16)
    cst[:, C_HALF:C_HALF + 16] = -0.5
    cst[:, C_ONES:C_ONES + SQ] = 1.0
    return cst


def kernel(**inputs):
    import concourse.bacc as bacc
    from concourse.bass_utils import run_bass_kernel_spmd as run

    i = {k: np.asarray(v) for k, v in inputs.items()}
    ctx = i["ctx_1024"]
    host = {
        "cst": _constants(),
        "x": i["x"].reshape(NT, P, D).transpose(1, 0, 2),
        "ctx_T": ctx.transpose(0, 2, 1).reshape(NB, KT, P, SK).transpose(0, 2, 1, 3),
        "ctx": ctx,
        "ctx_rows": ctx[:, SK - 1, :].reshape(NT, BT, D),
        "ctx_last_T": ctx[:, SK - 1, :].T.reshape(KT, P, NB).transpose(1, 0, 2),
        "qpos_T": i["itok_BxS_8_8191"].T,
        "kpos": i["itok_BxS2_1_8191"],
        "mask": i["mask_BxSxS2_if1"],
        "xa_q": _blocks(i["L0_xattn_W_q"]), "xa_k": _blocks(i["L0_xattn_W_k"]),
        "xa_v": _blocks(i["L0_xattn_W_v"]), "xa_o": _blocks(i["L0_xattn_W_o"]),
        "ra_qkv": _plain(i["L0_attn_w_qkv"]), "ra_o": _by_head(i["L0_attn_w_out"]),
        "ra_bqk": _column(i["L0_attn_b_qkv"][:2 * D]), "ra_bv": i["L0_attn_b_qkv"][2 * D:],
        "ra_bo": i["L0_attn_b_out"],
        "w_gate": i["L0_ffn_w_gate"].reshape(FT, P, D).transpose(1, 0, 2).reshape(P, -1, QB),
        "w_up": i["L0_ffn_w_up"].reshape(FT, P, D).transpose(1, 0, 2).reshape(P, -1, QB),
        "w_down": i["L0_ffn_w_down"].reshape(KT, P, FF).transpose(1, 0, 2).reshape(P, -1, QB),
        "cx_q": _blocks(i["L1_xattn_Wq"]), "cx_k": _plain(i["L1_xattn_Wk"]), "cx_v": _blocks(i["L1_xattn_Wv"]),
        "cx_bq": _column(i["L1_xattn_bq"]), "cx_bk": _column(i["L1_xattn_bk"]), "cx_bv": i["L1_xattn_bv"],
        "lt_qkv": _blocks(i["L1_attn_lt_w_in"]), "lt_o": _by_head(i["L1_attn_lt_w_out"].T),
        "lt_bqk": _column(i["L1_attn_lt_b_in"][:2 * D]), "lt_bv": i["L1_attn_lt_b_in"][2 * D:],
        "lt_bo": _column(i["L1_attn_lt_b_out"]),
        "st_qkv": _blocks(i["L1_attn_st_w_in"]), "st_o": _by_head(i["L1_attn_st_w_out"].T),
        "st_bqk": _column(i["L1_attn_st_b_in"][:2 * D]), "st_bv": i["L1_attn_st_b_in"][2 * D:],
        "st_bo": i["L1_attn_st_b_out"],
        "protos": _blocks(i["L1_attn_protos"]), "fus": _blocks(i["L1_attn_fus_w"]), "fus_b": i["L1_attn_fus_b"],
        "router": _plain(i["L1_ffn_router_weight"]),
        "w1": i["L1_ffn_w1"].reshape(NE, KT, P, 2 * FE).transpose(0, 2, 1, 3),
        "w2": i["L1_ffn_w2"],
    }
    nc = bacc.Bacc("TRN2", target_bir_lowering=False, num_devices=1)
    given, views = {}, {}
    for name, array in host.items():
        array = np.ascontiguousarray(array)
        given["in_" + name] = array
        view = nc.dram_tensor("in_" + name, array.shape, mybir.dt.from_np(array.dtype), kind="ExternalInput").ap()
        if array.ndim == 1:
            view = view.unsqueeze(0).broadcast_to([P, array.shape[0]])
        views[name] = view
    out = nc.dram_tensor("out", (P, NT, D), F32, kind="ExternalOutput").ap()
    build(nc, views, out)
    got = run(nc, [given], core_ids=[0]).results[0]["out"]
    return np.ascontiguousarray(np.asarray(got).transpose(1, 0, 2)).reshape(NB, SQ, D)
```
